# Optimizing a Trainium2 kernel written in Bass

```python
import numpy as np
import jax
import jax.numpy as jnp

def _softmax(x, axis=-1):
    return jax.nn.softmax(x, axis=axis)

def _gelu(x):
    return jax.nn.gelu(x, approximate=True)

def _silu(x):
    return jax.nn.silu(x)

def _sigmoid(x):
    return jax.nn.sigmoid(x)

def _layernorm(x, axis=-1, eps=1e-05):
    m = jnp.mean(x, axis=axis, keepdims=True)
    v = jnp.var(x, axis=axis, keepdims=True)
    return (x - m) / jnp.sqrt(v + eps)

def _scatter_add(tgt, idx, src, axis=0):
    return tgt.at[idx].add(src)

def _segment_sum(src, seg, n):
    return jax.ops.segment_sum(src, seg, n)
kernel_name = 'mk_gnn_ffn_d2_gnn_r32_798d24'

def setup_inputs(seed: int=0):
    np.random.seed(seed)
    _w = jnp.asarray

    def _rec_inputs():
        import jax
        import jax.numpy as jnp
        _gk = jax.random.key(seed)
        x = -0.0002117 + 1 * jax.random.normal(jax.random.fold_in(_gk, 1), (3125, 256), jnp.float32)
        _s = jax.random.randint(jax.random.fold_in(_gk, 2), (25000,), 0, 3125, jnp.int32)
        _d = jax.random.randint(jax.random.fold_in(_gk, 3), (25000,), 0, 3125, jnp.int32)
        _loop = jnp.arange(3125, dtype=jnp.int32)
        src = jnp.concatenate([_s, _d, _loop])
        dst = jnp.concatenate([_d, _s, _loop])
        _o = jnp.argsort(dst, stable=True)
        src = src[_o]
        dst = dst[_o]
        edge_type_20 = jax.random.randint(jax.random.fold_in(_gk, 12), (53125,), 0, 20, jnp.int32)
        edge_weight1 = jax.random.uniform(jax.random.fold_in(_gk, 13), (53125, 1), jnp.float32, 0.0, 0.999998)
        return (x, src, dst, edge_type_20, edge_weight1)
    x, src, dst, edge_type_20, edge_weight1 = _rec_inputs()

    def _L0_gnn_setup():
        import jax, jax.numpy as jnp
        import numpy as np
        N_NODES = 3125
        N_EDGES = 100000
        D_IN = 256
        D_OUT = 256
        key = jax.random.key(seed)
        k1, k2, k3, k4 = jax.random.split(key, 4)
        x = jax.random.normal(k1, (N_NODES, D_IN), dtype=jnp.float32)
        edge_row = jax.random.randint(k2, (N_EDGES,), 0, N_NODES, dtype=jnp.int32)
        edge_col = jax.random.randint(k3, (N_EDGES,), 0, N_NODES, dtype=jnp.int32)
        bound = float(np.sqrt(6.0 / D_IN))
        weight = jax.random.uniform(k4, (D_IN, D_OUT), dtype=jnp.float32, minval=-bound, maxval=bound)
        bias = jnp.zeros((D_OUT,), dtype=jnp.float32)
        return {'x': x, 'edge_row': edge_row, 'edge_col': edge_col, 'weight': weight, 'bias': bias}
    _L0_gnn_all = _L0_gnn_setup()
    _L0_gnn_in = {k: v for k, v in _L0_gnn_all.items() if k in ('weight', 'bias')}
    del _L0_gnn_all

    def _L0_ffn_setup():
        import math
        import jax, jax.numpy as jnp
        import numpy as np
        CAPACITY_FACTOR = 1.25
        TOP_K = 2
        LN_EPS = 1e-05

        def _layer_norm(x, gamma, beta):
            mu = jnp.mean(x, axis=-1, keepdims=True)
            var = jnp.var(x, axis=-1, keepdims=True)
            return (x - mu) * jax.lax.rsqrt(var + LN_EPS) * gamma + beta
        key = jax.random.key(seed)
        ks = jax.random.split(key, 4)
        B, S, D, F, E = (8, 128, 256, 512, 8)
        x = jax.random.normal(ks[0], (B, S, D), dtype=jnp.float32)
        Wr = jax.random.normal(ks[1], (D, E), dtype=jnp.float32) / np.sqrt(D)
        br = jnp.zeros((E,), jnp.float32)
        W1 = jax.random.normal(ks[2], (E, D, F), dtype=jnp.float32) / np.sqrt(D)
        b1 = jnp.zeros((E, F), jnp.float32)
        W2 = jax.random.normal(ks[3], (E, F, D), dtype=jnp.float32) / np.sqrt(F)
        b2 = jnp.zeros((E, D), jnp.float32)
        gamma = jnp.ones((D,), jnp.float32)
        beta = jnp.zeros((D,), jnp.float32)
        return {'x': x, 'Wr': Wr, 'br': br, 'W1': W1, 'b1': b1, 'W2': W2, 'b2': b2, 'gamma': gamma, 'beta': beta}
    _L0_ffn_all = _L0_ffn_setup()
    _L0_ffn_in = {k: v for k, v in _L0_ffn_all.items() if k in ('Wr', 'br', 'W1', 'b1', 'W2', 'b2', 'gamma', 'beta')}
    del _L0_ffn_all

    def _L1_gnn_setup():
        import jax, jax.numpy as jnp
        import numpy as np
        N_NODES = 10000
        N_EDGES = 10000
        NUM_RELS = 20
        IN_FEAT = 256
        OUT_FEAT = 256
        key = jax.random.key(seed)
        k1, k2, k3, k4, k5, k6 = jax.random.split(key, 6)
        h = jax.random.normal(k1, (N_NODES, IN_FEAT), dtype=jnp.float32)
        gain = float(np.sqrt(2.0))
        limit = gain * float(np.sqrt(6.0 / (IN_FEAT + OUT_FEAT)))
        weight = jax.random.uniform(k2, (NUM_RELS, IN_FEAT, OUT_FEAT), dtype=jnp.float32, minval=-limit, maxval=limit)
        norm = jax.random.uniform(k3, (N_EDGES, 1), dtype=jnp.float32)
        edge_src = jax.random.randint(k4, (N_EDGES,), 0, N_NODES, dtype=jnp.int32)
        edge_dst = jax.random.randint(k5, (N_EDGES,), 0, N_NODES, dtype=jnp.int32)
        rel_type = jax.random.randint(k6, (N_EDGES,), 0, NUM_RELS, dtype=jnp.int32)
        return {'h': h, 'weight': weight, 'norm': norm, 'edge_src': edge_src, 'edge_dst': edge_dst, 'rel_type': rel_type}
    _L1_gnn_all = _L1_gnn_setup()
    _L1_gnn_in = {k: v for k, v in _L1_gnn_all.items() if k in ('weight',)}
    del _L1_gnn_all

    def _L1_ffn_setup():
        import jax, jax.numpy as jnp
        import numpy as np
        C = 256
        HID = 1024
        E = 8
        TEMP = 1.0
        key = jax.random.key(seed)
        ks = jax.random.split(key, 7)
        x = jax.random.normal(ks[0], (8, 512, C), dtype=jnp.float32)
        W1 = jax.random.normal(ks[1], (C, HID), dtype=jnp.float32) * 0.02
        b1 = jnp.zeros((HID,), dtype=jnp.float32)
        Wg = jax.random.normal(ks[2], (HID, E), dtype=jnp.float32) * 0.02
        bg = jnp.zeros((E,), dtype=jnp.float32)
        Wd = jax.random.normal(ks[3], (E, HID, C), dtype=jnp.float32) * 0.02
        bd = jnp.zeros((E, C), dtype=jnp.float32)
        return {'x': x, 'W1': W1, 'b1': b1, 'Wg': Wg, 'bg': bg, 'Wd': Wd, 'bd': bd}
    _L1_ffn_all = _L1_ffn_setup()
    _L1_ffn_in = {k: v for k, v in _L1_ffn_all.items() if k in ('W1', 'b1', 'Wg', 'bg', 'Wd', 'bd')}
    del _L1_ffn_all
    return {'x': x, 'src': src, 'dst': dst, 'edge_type_20': edge_type_20, 'edge_weight1': edge_weight1, 'L0_gnn_weight': _L0_gnn_in['weight'], 'L0_gnn_bias': _L0_gnn_in['bias'], 'L0_ffn_Wr': _L0_ffn_in['Wr'], 'L0_ffn_br': _L0_ffn_in['br'], 'L0_ffn_W1': _L0_ffn_in['W1'], 'L0_ffn_b1': _L0_ffn_in['b1'], 'L0_ffn_W2': _L0_ffn_in['W2'], 'L0_ffn_b2': _L0_ffn_in['b2'], 'L0_ffn_gamma': _L0_ffn_in['gamma'], 'L0_ffn_beta': _L0_ffn_in['beta'], 'L1_gnn_weight': _L1_gnn_in['weight'], 'L1_ffn_W1': _L1_ffn_in['W1'], 'L1_ffn_b1': _L1_ffn_in['b1'], 'L1_ffn_Wg': _L1_ffn_in['Wg'], 'L1_ffn_bg': _L1_ffn_in['bg'], 'L1_ffn_Wd': _L1_ffn_in['Wd'], 'L1_ffn_bd': _L1_ffn_in['bd']}

def reference(x, src, dst, edge_type_20, edge_weight1, L0_gnn_weight, L0_gnn_bias, L0_ffn_Wr, L0_ffn_br, L0_ffn_W1, L0_ffn_b1, L0_ffn_W2, L0_ffn_b2, L0_ffn_gamma, L0_ffn_beta, L1_gnn_weight, L1_ffn_W1, L1_ffn_b1, L1_ffn_Wg, L1_ffn_bg, L1_ffn_Wd, L1_ffn_bd):
    import jax
    import jax.numpy as jnp

    def _L0_gnn_ref(x, edge_row, edge_col, weight, bias):
        import jax, jax.numpy as jnp
        import numpy as np
        N_NODES = 3125
        N_EDGES = 100000
        D_IN = 256
        D_OUT = 256
        support = x @ weight
        gathered = jnp.take(support, edge_col, axis=0)
        out = jax.ops.segment_sum(gathered, edge_row, num_segments=N_NODES)
        return out + bias

    def _L0_ffn_ref(x, Wr, br, W1, b1, W2, b2, gamma, beta):
        import math
        import jax, jax.numpy as jnp
        import numpy as np
        CAPACITY_FACTOR = 1.25
        TOP_K = 2
        LN_EPS = 1e-05

        def _layer_norm(x, gamma, beta):
            mu = jnp.mean(x, axis=-1, keepdims=True)
            var = jnp.var(x, axis=-1, keepdims=True)
            return (x - mu) * jax.lax.rsqrt(var + LN_EPS) * gamma + beta
        B, S, D = x.shape
        E = Wr.shape[1]
        N = B * S
        K = TOP_K
        logits = jnp.mean(x, axis=1) @ Wr + br
        routing_weights = jax.nn.softmax(logits, axis=-1)
        capacity = float(math.ceil(N * CAPACITY_FACTOR / E))
        expected_loads = routing_weights.sum(axis=0) * (N / B)
        scale = jnp.where(expected_loads > capacity, capacity / expected_loads, 1.0)
        routing_weights = jax.nn.softmax(routing_weights * scale, axis=-1)
        rw_tok = jnp.broadcast_to(routing_weights[:, None, :], (B, S, E)).reshape(N, E)
        top_w, top_i = jax.lax.top_k(rw_tok, K)
        top_w = jax.nn.softmax(top_w, axis=-1)
        xf = x.reshape(N, D)
        h = jax.nn.gelu(jnp.einsum('nd,edf->enf', xf, W1) + b1[:, None, :], approximate=False)
        y = jnp.einsum('enf,efd->end', h, W2) + b2[:, None, :]
        w_dense = jnp.zeros((N, E), x.dtype).at[jnp.arange(N)[:, None], top_i].add(top_w)
        out = jnp.einsum('ne,end->nd', w_dense, y).reshape(B, S, D)
        out = _layer_norm(out + x, gamma, beta)
        return out

    def _L1_gnn_ref(h, weight, norm, edge_src, edge_dst, rel_type):
        import jax, jax.numpy as jnp
        import numpy as np
        N_NODES = 10000
        N_EDGES = 10000
        NUM_RELS = 20
        IN_FEAT = 256
        OUT_FEAT = 256
        h_all = jnp.einsum('ni,rio->nro', h, weight)
        msg = h_all[edge_src, rel_type] * norm
        agg = jax.ops.segment_sum(msg, edge_dst, num_segments=h.shape[0])
        return jax.nn.relu(agg)

    def _L1_ffn_ref(x, W1, b1, Wg, bg, Wd, bd):
        import jax, jax.numpy as jnp
        import numpy as np
        C = 256
        HID = 1024
        E = 8
        TEMP = 1.0
        orig_shape = x.shape
        xf = x.reshape(-1, orig_shape[-1])
        H = jax.nn.gelu(xf @ W1 + b1, approximate=False)
        probs = jax.nn.softmax((H @ Wg + bg) / TEMP, axis=-1)
        assign = jnp.argmax(probs, axis=-1)
        out = jnp.zeros_like(xf)
        for e in range(Wd.shape[0]):
            y = H @ Wd[e] + bd[e]
            sel = (assign == e)[:, None]
            out = out + jnp.where(sel, probs[:, e:e + 1] * y, 0.0)
        return out.reshape(orig_shape)
    x = x + _L0_gnn_ref(_layernorm(x, axis=-1), src, dst, L0_gnn_weight, L0_gnn_bias)
    x = x + _L0_ffn_ref(_layernorm(x, axis=-1)[None], L0_ffn_Wr, L0_ffn_br, L0_ffn_W1, L0_ffn_b1, L0_ffn_W2, L0_ffn_b2, L0_ffn_gamma, L0_ffn_beta)[0]
    x = x + _L1_gnn_ref(_layernorm(x, axis=-1), L1_gnn_weight, edge_weight1, src, dst, edge_type_20)
    x = x + _L1_ffn_ref(_layernorm(x, axis=-1)[None], L1_ffn_W1, L1_ffn_b1, L1_ffn_Wg, L1_ffn_bg, L1_ffn_Wd, L1_ffn_bd)[0]
    return x

_drawn_inputs = setup_inputs


def setup_inputs(seed=0):
    import zlib

    import numpy as np

    out = dict(_drawn_inputs(seed))
    spreads = {'L0_gnn_bias': (0.0, 0.46),
     'L0_ffn_br': (0.0, 0.1),
     'L0_ffn_b1': (0.0, 0.8),
     'L0_ffn_b2': (0.0, 0.8),
     'L0_ffn_gamma': (1.0, 0.2),
     'L0_ffn_beta': (0.0, 0.53),
     'L1_ffn_b1': (0.0, 0.8),
     'L1_ffn_bg': (0.0, 0.8),
     'L1_ffn_bd': (0.0, 0.8)}
    factors = {'L0_ffn_Wr': 8.0, 'L1_ffn_W1': 8.0, 'L1_ffn_Wg': 8.0, 'L1_ffn_Wd': 8.0}
    for name, (base, spread) in spreads.items():
        noise = np.random.default_rng([zlib.crc32(name.encode()), seed]).standard_normal(out[name].shape)
        drawn = base * np.exp(spread * noise) if base else spread * noise
        out[name] = jnp.asarray(drawn.astype(out[name].dtype))
    for name, factor in factors.items():
        out[name] = (out[name] * factor).astype(out[name].dtype)
    return out
```

```python
from contextlib import ExitStack

import concourse.bass as bass
from concourse import mybir

F32 = mybir.dt.float32
I32 = mybir.dt.int32
ALU = mybir.AluOpType
ACT = mybir.ActivationFunctionType
AX = mybir.AxisListType

P = 128
N = 3125
D = 256
KD = D // P
NT = -(-N // P)
LAST = N - (NT - 1) * P
U = 5
IT = NT // U
NP = NT * P
E = 53125
CH = 4
GE = CH * P
NG = -(-E // GE)
ELAST = E - (NG - 1) * GE
RING = 4
R = 20
RS = 2
SW = R * D // RS
NE = 8
F0, F1 = 512, 1024
K0, K1 = F0 // P, F1 // P
ST = (N - NE) // P + NE
SC = 4
EPS = 1e-5
CAP = float(-(-N * 5 // (4 * NE)))
assert NT == U * IT and NG % RING == 0 and ST % (2 * SC) == 0


def build(nc, x, src, dst, rel, ew, wg, bias, wr, br, w1, b1, w2, b2, gamma, beta,
          wrel, v1, c1, vg, cg, wd, bd, out):
    ctx = ExitStack()

    def sb(name, shape, dt=F32):
        return ctx.enter_context(nc.sbuf_tensor(name, shape, dt))

    def sem(name):
        return ctx.enter_context(nc.semaphore(name))

    def ds(i, n):
        return bass.ds(i, n)

    def scratch(part):
        def run():
            with ExitStack() as own:
                part(lambda name, shape, dt=F32: own.enter_context(nc.sbuf_tensor(name, shape, dt)))
        return run

    support_d = nc.dram_tensor("support_d", (N, D), F32).ap()
    rel_d = nc.dram_tensor("rel_d", (N, R * D), F32).ap()
    rel_rows = rel_d.rearrange("n (r d) -> (n r) d", r=R)
    sorted_d = nc.dram_tensor("sorted_d", (ST * P, D), F32).ap()
    y_d = nc.dram_tensor("y_d", (ST * P, D), F32).ap()

    x_all = sb("x_all", [P, NT, D])
    agg_or_xT = sb("agg_or_xT", [P, NT * D])
    agg = agg_or_xT[:, :].rearrange("p (t d) -> p t d", t=NT)
    xT_all = agg_or_xT[:, :].rearrange("p (k n) -> p k n", k=KD)
    arena = sb("arena", [P, NE * K1 * D])
    wrel_s = arena[:, 0:KD * R * D].rearrange("p (k r d) -> p k r d", k=KD, r=R)
    stage = arena[:, KD * R * D:KD * R * D + 2 * SW].rearrange("p (s n) -> p s n", s=2)
    wd_s = arena
    hT = sb("hT", [P, K1, U * P])
    ring = hT[:, :, :].rearrange("p a b -> p (a b)")[:, 0:RING * CH * D]\
        .rearrange("p (s j d) -> p s j d", s=RING, j=CH)
    xn = sb("xn", [P, U, D])
    xT = sb("xT", [P, U, KD, P])
    onehot = sb("onehot", [P, CH, P])
    ident = sb("ident", [P, P])
    ones = sb("ones", [P, P])
    before = sb("before", [P, P])
    iota_row = sb("iota_row", [P, P])
    tile_base = sb("tile_base", [P, NT])
    iota_i = sb("iota_i", [P, P], I32)
    base_i = sb("base_i", [P, NT], I32)
    stat = sb("stat", [P, NT, 6])
    mean = sb("mean", [P, NT])
    vsum = sb("vsum", [P, NT])
    dev = sb("dev", [P, NT])
    rstd = sb("rstd", [P, NT])
    wg_s = sb("wg_s", [P, KD, D])
    v1_s = sb("v1_s", [P, KD, F1])
    w1_s = sb("w1_s", [P, 2, KD, F0])
    w2_s = sb("w2_s", [P, 2, K0, D])
    b1_s = sb("b1_s", [P, 2, K0])
    c1_s = sb("c1_s", [P, K1])
    vg_s = sb("vg_s", [P, K1, NE])
    cg_s = sb("cg_s", [P, NE])
    bd_s = sb("bd_s", [P, NE, D])
    wr_s = sb("wr_s", [P, KD, NE])
    br_s = sb("br_s", [1, NE])
    b2_s = sb("b2_s", [NE, D])
    bias_s = sb("bias_s", [P, D])
    gamma_s = sb("gamma_s", [P, D])
    beta_s = sb("beta_s", [P, D])
    b2c = sb("b2c", [P, D])
    src_i = sb("src_i", [P, CH, NG], I32)
    srcrel_i = sb("srcrel_i", [P, CH, NG], I32)
    dst_f = sb("dst_f", [P, CH, NG])
    ew_f = sb("ew_f", [P, CH, NG])
    idx_slot = sb("idx_slot", [P, RING, CH], I32)
    ew_slot = sb("ew_slot", [P, CH])
    dst_rel = sb("dst_rel", [P, CH])
    spans = sb("spans", [1, 3, NG], I32)
    bank = [ctx.enter_context(nc.psum_tensor(f"bank{i}", [P, 512], F32)) for i in range(8)]

    def tslot(u):
        return bank[u % 3][:, 0:D]

    s_wrel, s_wd, s_v1, s_bd = sem("wrel_loaded"), sem("wd_loaded"), sem("v1_loaded"), sem("bd_loaded")
    s_zero = sem("sorted_d_zeroed")

    class Chain:

        def __init__(self, eng, s, start=0):
            self.eng, self.s, self.start, self.steps = eng, s, start, 0

        def __call__(self, ins):
            ins.then_inc(self.s, 1)
            self.steps += 1
            self.eng.wait_ge(self.s, self.start + self.steps)

    def rsqrt(link, y, v, t):
        link(nc.vector.tensor_scalar(t.bitcast(I32), v.bitcast(I32), 1, None, ALU.logical_shift_right))
        link(nc.vector.tensor_scalar(y.bitcast(I32), t.bitcast(I32), -1.0, float(0x5F3759DF), ALU.mult, ALU.add))
        for _ in range(3):
            link(nc.vector.tensor_tensor(t, y, y, ALU.mult))
            link(nc.vector.tensor_tensor(t, t, v, ALU.mult))
            link(nc.vector.tensor_scalar(t, t, -0.5, 1.5, ALU.mult, ALU.add))
            link(nc.vector.tensor_tensor(y, y, t, ALU.mult))

    def load_and_constants():
        s_x, s_small, s_const = sem("x_loaded"), sem("small_loaded"), sem("const_step")
        s_ci, s_pad = sem("iota_written"), sem("x_padding_zeroed")
        with nc.Block() as block:
            @block.sync
            def _(sp):
                sp.dma_start(x_all[:, 0:NT - 1, :], x[0:(NT - 1) * P, :].rearrange("(t p) d -> p t d", p=P))\
                    .then_inc(s_x, 16)
                sp.wait_ge(s_pad, 1)
                sp.dma_start(x_all[0:LAST, NT - 1, :], x[(NT - 1) * P:N, :]).then_inc(s_x, 16)
                sp.dma_start(wg_s[:, :, :], wg.rearrange("(k p) n -> p k n", p=P)).then_inc(s_small, 16)
                sp.dma_start(vg_s[:, :, :], vg.rearrange("(k p) n -> p k n", p=P)).then_inc(s_small, 16)
                sp.dma_start(wr_s[:, :, :], wr.rearrange("(k p) n -> p k n", p=P)).then_inc(s_small, 16)
                sp.dma_start(br_s[:, :], br.rearrange("(a n) -> a n", a=1)).then_inc(s_small, 16)
                sp.dma_start(b2_s[:, :], b2).then_inc(s_small, 16)
                sp.dma_start(c1_s[:, :], c1.rearrange("(k p) -> p k", p=P),
                             allow_slow_non_contiguous=True).then_inc(s_small, 16)
                for tile, vec in ((bias_s, bias), (gamma_s, gamma), (beta_s, beta), (cg_s, cg)):
                    sp.dma_start(tile[:, :], vec.partition_broadcast(P)).then_inc(s_small, 16)
                sp.wait_ge(s_x, 32)
                sp.wait_ge(s_small, 160)

            @block.gpsimd
            def _(pool):
                nc.gpsimd.iota(iota_i[:, :], pattern=[[1, P]], base=0, channel_multiplier=0).then_inc(s_ci, 1)
                nc.gpsimd.iota(base_i[:, :], pattern=[[P, NT]], base=0, channel_multiplier=0).then_inc(s_ci, 1)
                nc.gpsimd.memset(ident[:, :], 0.0).then_inc(s_const, 1)
                nc.gpsimd.memset(before[:, :], 1.0).then_inc(s_const, 1)
                nc.gpsimd.memset(ones[:, :], 1.0).then_inc(s_const, 1)
                pool.wait_ge(s_const, 3)
                nc.gpsimd.affine_select(out=ident[:, :], in_=ident[:, :], compare_op=ALU.not_equal, fill=1.0,
                                        base=0, pattern=[[-1, P]], channel_multiplier=1).then_inc(s_const, 1)
                nc.gpsimd.affine_select(out=before[:, :], in_=before[:, :], compare_op=ALU.is_gt, fill=0.0,
                                        base=0, pattern=[[1, P]], channel_multiplier=-1).then_inc(s_const, 1)

            @block.vector
            def _(dve):
                nc.vector.memset(x_all[:, NT - 1, :], 0.0).then_inc(s_pad, 1)
                dve.wait_ge(s_ci, 2)
                nc.vector.tensor_copy(iota_row[:, :], iota_i[:, :])
                nc.vector.tensor_copy(tile_base[:, :], base_i[:, :])

    @scratch
    def edges(own):
        raw = arena[:, 0:3 * GE].bitcast(I32).rearrange("p (a n) -> p a n", a=3)
        ef = arena[:, 3 * GE:7 * GE].rearrange("p (a n) -> p a n", a=4)
        SRC, SRCREL, DST, EW = range(4)
        lim = own("lim", [P, 2])
        cmpr = own("cmpr", [P, 2, NT - 1])
        tiles = own("tiles", [P, 3])
        s_pad, s_in, s_step = sem("edge_padding"), sem("edges_loaded"), sem("edge_step")
        s_f, s_t, s_tab, s_ev = sem("edge_rows_ready"), sem("edges_transposed"), sem("spans_summed"), sem("edge_copies")
        with nc.Block() as block:
            @block.sync
            def _(sp):
                sp.wait_ge(s_pad, 3)
                for a, v in ((0, src), (1, rel), (2, dst)):
                    sp.dma_start(raw[0:NG - 1, a, :], v[0:(NG - 1) * GE].rearrange("(g e) -> g e", e=GE))\
                        .then_inc(s_in, 16)
                    sp.dma_start(raw[NG - 1:NG, a, 0:ELAST], v[(NG - 1) * GE:E].rearrange("(g e) -> g e", g=1))\
                        .then_inc(s_in, 16)
                sp.dma_start(ef[0:NG - 1, EW, :], ew[0:(NG - 1) * GE, :].rearrange("(g e) a -> g (e a)", e=GE))\
                    .then_inc(s_in, 16)
                sp.dma_start(ef[NG - 1:NG, EW, 0:ELAST], ew[(NG - 1) * GE:E, :].rearrange("(g e) a -> g (e a)", g=1))\
                    .then_inc(s_in, 16)

            @block.vector
            def _(dve):
                nc.vector.memset(raw[:, 0:2, :], 0).then_inc(s_pad, 1)
                nc.vector.memset(raw[:, 2, :], NP - 1).then_inc(s_pad, 1)
                nc.vector.memset(ef[:, EW, :], 0.0).then_inc(s_pad, 1)
                link = Chain(dve, s_step)
                dve.wait_ge(s_in, 128)
                link(nc.vector.tensor_copy(ef[:, SRC, :], raw[:, 0, :]))
                link(nc.vector.tensor_copy(ef[:, SRCREL, :], raw[:, 1, :]))
                link(nc.vector.tensor_copy(ef[:, DST, :], raw[:, 2, :]))
                nc.vector.scalar_tensor_tensor(out=ef[:, SRCREL, :], in0=ef[:, SRC, :], scalar=float(R),
                                               in1=ef[:, SRCREL, :], op0=ALU.mult, op1=ALU.add).then_inc(s_f, 1)
                link(nc.vector.tensor_reduce(lim[0:NG, 0:1], ef[0:NG, DST, :], AX.X, ALU.min))
                link(nc.vector.tensor_reduce(lim[0:NG, 1:2], ef[0:NG, DST, :], AX.X, ALU.max))
                for m in range(2):
                    link(nc.vector.tensor_scalar(cmpr[0:NG, m, :], tile_base[0:NG, 1:NT], lim[0:NG, m:m + 1], None,
                                                 ALU.is_le))
                link(nc.vector.tensor_reduce(tiles[0:NG, 0:2], cmpr[0:NG, :, :], AX.X, ALU.add))
                link(nc.vector.tensor_tensor(tiles[0:NG, 2:3], tiles[0:NG, 1:2], tiles[0:NG, 0:1], ALU.subtract))
                nc.vector.tensor_scalar(tiles[0:NG, 2:3], tiles[0:NG, 2:3], 1.0, None, ALU.add).then_inc(s_f, 1)
                dve.wait_ge(s_t, 4)
                nc.vector.tensor_copy(src_i[:, :, :].rearrange("p j g -> p (j g)"), bank[SRC][:, 0:CH * NG])
                nc.vector.tensor_copy(srcrel_i[:, :, :].rearrange("p j g -> p (j g)"), bank[SRCREL][:, 0:CH * NG])
                nc.vector.tensor_copy(dst_f[:, :, :].rearrange("p j g -> p (j g)"), bank[DST][:, 0:CH * NG])
                nc.vector.tensor_copy(ew_f[:, :, :].rearrange("p j g -> p (j g)"), bank[EW][:, 0:CH * NG])
                dve.wait_ge(s_tab, 1)
                nc.vector.tensor_copy(spans[:, :, :].rearrange("a k g -> a (k g)"), bank[4][0:1, 0:3 * NG])

            @block.tensor
            def _(pe):
                pe.wait_ge(s_f, 1)
                for a in range(4):
                    for j in range(CH):
                        last = nc.tensor.transpose(bank[a][:, j * NG:(j + 1) * NG], ef[0:NG, a, j * P:(j + 1) * P],
                                                   ident[0:NG, 0:NG])
                    last.then_inc(s_t, 1)
                pe.wait_ge(s_f, 2)
                nc.tensor.matmul(bank[4][0:1, 0:NG], tiles[0:NG, 2:3], before[0:NG, 0:NG], start=True, stop=True)
                nc.tensor.matmul(bank[4][0:1, NG:2 * NG], tiles[0:NG, 0:1], ident[0:NG, 0:NG], start=True, stop=True)
                nc.tensor.matmul(bank[4][0:1, 2 * NG:3 * NG], tiles[0:NG, 2:3], ident[0:NG, 0:NG],
                                 start=True, stop=True).then_inc(s_tab, 1)

    def join_stats(link, st, m, v, t):
        link(nc.vector.tensor_tensor(m, st[:, :, 1], st[:, :, 4], ALU.add))
        link(nc.vector.tensor_tensor(t, st[:, :, 1], st[:, :, 4], ALU.subtract))
        link(nc.vector.tensor_scalar(m, m, 0.5, None, ALU.mult))
        link(nc.vector.tensor_tensor(t, t, t, ALU.mult))
        link(nc.vector.tensor_tensor(v, st[:, :, 2], st[:, :, 5], ALU.add))
        link(nc.vector.scalar_tensor_tensor(out=v, in0=t, scalar=D / 4.0, in1=v, op0=ALU.mult, op1=ALU.add))
        link(nc.vector.tensor_scalar(v, v, 1.0 / D, EPS, ALU.mult, ALU.add))

    def row_stats(dve, tag):
        s_bn, s_st = sem(f"{tag}_bn_stats"), sem(f"{tag}_stat_step")
        with dve.Fori(0, IT) as it:
            for u in range(U):
                w = it * U + u
                nc.vector.bn_stats(stat[:, ds(w, 1), :].rearrange("p a s -> p (a s)"),
                                   x_all[:, ds(w, 1), :].rearrange("p a d -> p (a d)")).then_inc(s_bn, 1)
        dve.wait_ge(s_bn, NT)
        link = Chain(dve, s_st)
        join_stats(link, stat, mean[:, :], vsum[:, :], dev[:, :])
        rsqrt(link, rstd[:, :], vsum[:, :], dev[:, :])

    def normalise(to, of, w):
        return nc.vector.tensor_scalar(to, of[:, ds(w, 1), :].rearrange("p a d -> p (a d)"), mean[:, ds(w, 1)], rstd[:, ds(w, 1)],
                                       ALU.subtract, ALU.mult)

    def transposes(u):
        for k in range(KD):
            last = nc.tensor.transpose(tslot(u)[:, k * P:(k + 1) * P], xn[:, u, k * P:(k + 1) * P], ident[:, :])
        return last

    def support():
        s_xn, s_T, s_xT, s_mm = sem("p1_xn_ready"), sem("p1_transposed"), sem("p1_xT_ready"), sem("p1_product")
        s_row, s_out = sem("p1_rows_ready"), [sem(f"p1_rows_stored{u}") for u in range(U)]
        rows = hT[:, 0:2, :].rearrange("p a b -> p (a b)").rearrange("p (u d) -> p u d", u=U)
        with nc.Block() as block:
            @block.vector
            def _(dve):
                row_stats(dve, "p1")

                def tile(it, u, first):
                    w = it * U + u
                    if not first:
                        dve.wait_ge(s_T, w - U + 1)
                    normalise(xn[:, u, :], x_all, w).then_inc(s_xn, 1)

                def rows_of(it, u, first):
                    w = it * U + u
                    dve.wait_ge(s_mm, w + 1)
                    if not first:
                        dve.wait_ge(s_out[u], 16 * it)
                    nc.vector.tensor_copy(rows[:, u, :], bank[3 + u][:, 0:D]).then_inc(s_row, 1)
                    nc.vector.tensor_tensor(x_all[:, ds(w, 1), :], x_all[:, ds(w, 1), :],
                                            bias_s[:, None, :], ALU.add)

                def one_pass(it, first):
                    for u in range(U):
                        tile(it, u, first)
                    for u in range(U):
                        rows_of(it, u, first)

                one_pass(0, True)
                with dve.Fori(1, IT) as it:
                    one_pass(it, False)

            @block.tensor
            def _(pe):
                def one_pass(it, first):
                    for v in range(U + 1):
                        if v < U:
                            w = it * U + v
                            pe.wait_ge(s_xn, w + 1)
                            if not first or v >= 2:
                                pe.wait_ge(s_xT, w - 1)
                            transposes(v).then_inc(s_T, 1)
                        if v > 0:
                            u = v - 1
                            w = it * U + u
                            pe.wait_ge(s_xT, w + 1)
                            if not first:
                                pe.wait_ge(s_row, w - U + 1)
                            for k in range(KD):
                                last = nc.tensor.matmul(bank[3 + u][:, 0:D], xT[:, u, k, :], wg_s[:, k, :],
                                                        start=(k == 0), stop=(k == KD - 1))
                            last.then_inc(s_mm, 1)

                one_pass(0, True)
                with pe.Fori(1, IT) as it:
                    one_pass(it, False)

            @block.scalar
            def _(act):
                def one_pass(it, first):
                    for u in range(U):
                        w = it * U + u
                        act.wait_ge(s_T, w + 1)
                        if not first:
                            act.wait_ge(s_mm, w - U + 1)
                        nc.scalar.copy(xT[:, u, :, :].rearrange("p k n -> p (k n)"), tslot(u)).then_inc(s_xT, 1)

                one_pass(0, True)
                with act.Fori(1, IT) as it:
                    one_pass(it, False)

            @block.sync
            def _(sp):
                with sp.Fori(0, IT - 1) as it:
                    for u in range(U):
                        w = it * U + u
                        sp.wait_ge(s_row, w + 1)
                        sp.dma_start(support_d[ds(w * P, P), :], rows[:, u, :]).then_inc(s_out[u], 16)
                for u in range(U):
                    w = (IT - 1) * U + u
                    n = min(P, N - w * P)
                    sp.wait_ge(s_row, w + 1)
                    sp.dma_start(support_d[w * P:w * P + n, :], rows[0:n, u, :]).then_inc(s_out[u], 16)
                for u in range(U):
                    sp.wait_ge(s_out[u], 16 * IT)

    def segment_sum(tag, table, index, weighted, acc):
        s_idx, s_got = sem(f"{tag}_indices_ready"), [sem(f"{tag}_rows_gathered{s}") for s in range(RING)]
        s_used, s_hot, s_sum = sem(f"{tag}_group_used"), sem(f"{tag}_onehot_ready"), sem(f"{tag}_step_summed")
        s_go = sem(f"{tag}_gathers_started")
        s_acc, s_rel, s_ew = sem(f"{tag}_step_added"), sem(f"{tag}_dst_rel_ready"), sem(f"{tag}_weights_ready")
        passes = NG // RING
        with nc.Block() as block:
            @block.scalar
            def _(act):
                def group(it, s, first):
                    g = it * RING + s
                    if not first:
                        act.wait_ge(s_used, g - RING + 1)
                    nc.scalar.copy(idx_slot[:, s, :], index[:, :, ds(g, 1)].rearrange("p j a -> p (j a)"))\
                        .then_inc(s_idx, 1)

                for s in range(RING):
                    group(0, s, True)
                with act.Fori(1, passes) as it:
                    for s in range(RING):
                        group(it, s, False)

            @block.gpsimd
            def _(pool):
                with pool.Fori(0, passes) as it:
                    for s in range(RING):
                        pool.wait_ge(s_idx, it * RING + s + 1)
                        pool.sem_inc(s_go, 1)
                        for j in range(CH):
                            nc.gpsimd.indirect_dma_start(
                                out=ring[:, s, j, :], out_offset=None, in_=table,
                                in_offset=bass.IndirectOffsetOnAxis(ap=idx_slot[:, s, j:j + 1], axis=0),
                            ).then_inc(s_got[s], 16)

            @block.vector
            def _(dve):
                dve.sem_inc(s_acc, 1)
                with dve.Fori(0, passes) as it:
                    for s in range(RING):
                        g = it * RING + s
                        step0 = dve.value_load(spans[0:1, 0, ds(g, 1)], min_val=0, max_val=NG * NT)
                        tile0 = dve.value_load(spans[0:1, 1, ds(g, 1)], min_val=0, max_val=NT - 1)
                        count = dve.value_load(spans[0:1, 2, ds(g, 1)], min_val=1, max_val=NT)
                        if weighted:
                            nc.vector.tensor_copy(ew_slot[:, :], ew_f[:, :, ds(g, 1)].rearrange("p j a -> p (j a)"))\
                                .then_inc(s_ew, 1)
                        with dve.Fori(0, count) as i:
                            w = nc.s_assert_within(tile0 + i, 0, NT - 1, skip_runtime_bounds_check_because=
                                                   "a group's tiles end at that of its greatest destination")
                            step = step0 + i
                            nc.vector.tensor_scalar(dst_rel[:, :], dst_f[:, :, ds(g, 1)].rearrange("p j a -> p (j a)"),
                                                    tile_base[:, ds(w, 1)], None, ALU.subtract).then_inc(s_rel, 1)
                            dve.wait_ge(s_rel, step + 1)
                            if weighted:
                                dve.wait_ge(s_ew, g + 1)
                            for j in range(CH):
                                last = nc.vector.tensor_scalar(
                                    onehot[:, j, :], iota_row[:, :], dst_rel[:, j:j + 1],
                                    ew_slot[:, j:j + 1] if weighted else 1.0, ALU.is_equal, ALU.mult)
                            last.then_inc(s_hot, 1)
                            dve.wait_ge(s_sum, step + 1)
                            dve.wait_ge(s_acc, step + 1)
                            nc.vector.tensor_tensor(acc[:, ds(w, 1), :], acc[:, ds(w, 1), :],
                                                    bank[0][:, None, 0:D], ALU.add).then_inc(s_acc, 1)
                        nc.vector.nop().then_inc(s_used, 1)

            @block.tensor
            def _(pe):
                with pe.Fori(0, passes) as it:
                    for s in range(RING):
                        g = it * RING + s
                        step0 = pe.value_load(spans[0:1, 0, ds(g, 1)], min_val=0, max_val=NG * NT)
                        count = pe.value_load(spans[0:1, 2, ds(g, 1)], min_val=1, max_val=NT)
                        with pe.Fori(0, count) as i:
                            step = step0 + i
                            pe.wait_ge(s_got[s], 16 * CH * (it + 1))
                            pe.wait_ge(s_hot, step + 1)
                            pe.wait_ge(s_acc, step + 1)
                            for j in range(CH):
                                last = nc.tensor.matmul(bank[0][:, 0:D], onehot[:, j, :], ring[:, s, j, :],
                                                        start=(j == 0), stop=(j == CH - 1))
                            last.then_inc(s_sum, 1)

    def transposed_norm(tag):
        s_xn, s_T, s_xT = sem(f"{tag}_xn_ready"), sem(f"{tag}_transposed"), sem(f"{tag}_xT_ready")
        with nc.Block() as block:
            @block.vector
            def _(dve):
                row_stats(dve, tag)
                for u in range(U):
                    normalise(xn[:, u, :], x_all, u).then_inc(s_xn, 1)
                with dve.Fori(1, IT) as it:
                    for u in range(U):
                        w = it * U + u
                        dve.wait_ge(s_T, w - U + 1)
                        normalise(xn[:, u, :], x_all, w).then_inc(s_xn, 1)

            @block.tensor
            def _(pe):
                def tile(w, u, first):
                    pe.wait_ge(s_xn, w + 1)
                    if not first or u >= 2:
                        pe.wait_ge(s_xT, w - 1)
                    transposes(u).then_inc(s_T, 1)

                for u in range(U):
                    tile(u, u, True)
                with pe.Fori(1, IT) as it:
                    for u in range(U):
                        tile(it * U + u, u, False)

            @block.scalar
            def _(act):
                with act.Fori(0, IT) as it:
                    for u in range(U):
                        w = it * U + u
                        act.wait_ge(s_T, w + 1)
                        nc.scalar.copy(xT_all[:, :, ds(w * P, P)], tslot(u).rearrange("p (k n) -> p k n", k=KD))\
                            .then_inc(s_xT, 1)

    idx2 = sb("idx2", [1, 2], I32)
    w_pair = sb("w_pair", [P, 2])

    @scratch
    def routing(own):
        col = own("rt_col", [P, KD])
        rt = own("rt_rows", [1, 10, NE])
        sc = own("rt_scalars", [1, 12])
        wd8 = own("rt_wd8", [NE, P])
        s_mean, s_lg, s_step, s_idx = sem("rt_mean"), sem("rt_logits"), sem("rt_step"), sem("rt_experts_known")
        s_exp, s_w, s_e, s_b = sem("rt_exp_asked"), sem("rt_weights"), sem("rt_exp_done"), sem("rt_broadcast")
        s_ld, s_wT, s_b2 = sem("rt_matrices_loaded"), sem("rt_weights_on_partitions"), sem("rt_b2_done")
        with nc.Block() as block:
            @block.vector
            def _(dve):
                link = Chain(dve, s_step)

                def row(i):
                    return rt[0:1, i, :]

                def s(i):
                    return sc[0:1, i:i + 1]

                nc.vector.tensor_reduce(col[:, :], xT_all[:, :, 0:N], AX.X, ALU.add).then_inc(s_mean, 1)
                dve.wait_ge(s_lg, 1)
                link(nc.vector.tensor_scalar(row(0), bank[0][0:1, 0:NE], 1.0 / N, None, ALU.mult))
                link(nc.vector.tensor_tensor(row(0), row(0), br_s[:, :], ALU.add))

                def softmax(n):
                    link(nc.vector.tensor_reduce(s(0), row(0), AX.X, ALU.max))
                    nc.vector.tensor_scalar(row(0), row(0), s(0), None, ALU.subtract).then_inc(s_exp, 1)
                    dve.wait_ge(s_e, n)
                    link(nc.vector.tensor_reduce(s(1), row(1), AX.X, ALU.add))
                    link(nc.vector.reciprocal(s(2), s(1)))
                    link(nc.vector.tensor_scalar(row(1), row(1), s(2), None, ALU.mult))

                softmax(1)
                link(nc.vector.tensor_scalar(row(2), row(1), float(N), CAP, ALU.mult, ALU.max))
                link(nc.vector.memset(row(3), CAP))
                link(nc.vector.reciprocal(row(2), row(2)))
                link(nc.vector.tensor_scalar(row(3), row(2), CAP, 1.0, ALU.mult, ALU.min))
                link(nc.vector.tensor_tensor(row(0), row(1), row(3), ALU.mult))
                softmax(2)

                def first_greatest(value, index, hot):
                    link(nc.vector.tensor_reduce(value, row(1), AX.X, ALU.max))
                    link(nc.vector.tensor_scalar(row(4), row(1), value, -float(NE), ALU.is_equal, ALU.mult))
                    link(nc.vector.tensor_tensor(row(4), row(4), iota_row[0:1, 0:NE], ALU.add))
                    link(nc.vector.tensor_reduce(index, row(4), AX.X, ALU.min))
                    link(nc.vector.tensor_scalar(hot, row(4), index, None, ALU.is_equal))
                    link(nc.vector.tensor_scalar(index, index, float(NE), None, ALU.add))

                first_greatest(s(4), s(6), row(5))
                link(nc.vector.scalar_tensor_tensor(out=row(1), in0=row(5), scalar=-2.0, in1=row(1),
                                                    op0=ALU.mult, op1=ALU.add))
                first_greatest(s(5), s(7), row(6))
                nc.vector.tensor_copy(idx2[:, :], sc[0:1, 6:8]).then_inc(s_idx, 1)
                nc.vector.tensor_scalar(sc[0:1, 8:10], sc[0:1, 4:6], s(4), None, ALU.subtract).then_inc(s_exp, 1)
                dve.wait_ge(s_e, 3)
                link(nc.vector.tensor_reduce(s(0), sc[0:1, 10:12], AX.X, ALU.add))
                link(nc.vector.reciprocal(s(1), s(0)))
                link(nc.vector.tensor_scalar(sc[0:1, 10:12], sc[0:1, 10:12], s(1), None, ALU.mult))
                link(nc.vector.tensor_scalar(row(5), row(5), s(10), None, ALU.mult))
                nc.vector.scalar_tensor_tensor(out=row(7), in0=row(6), scalar=s(11), in1=row(5),
                                               op0=ALU.mult, op1=ALU.add).then_inc(s_w, 1)
                dve.wait_ge(s_b, 1)
                link(nc.vector.tensor_copy(w_pair[:, :], bank[1][:, 0:2]))
                nc.vector.tensor_scalar(wd8[:, :], ones[0:NE, :], bank[2][0:NE, 0:1], None, ALU.mult).then_inc(s_wT, 1)
                dve.wait_ge(s_b2, 1)
                nc.vector.tensor_copy(b2c[:, :], bank[3][:, 0:D])
                dve.wait_ge(s_ld, 96)
                for i in range(2):
                    nc.vector.tensor_scalar(w2_s[:, i, :, :], w2_s[:, i, :, :], w_pair[:, i:i + 1], None, ALU.mult)

            @block.scalar
            def _(act):
                for n in range(2):
                    act.wait_ge(s_exp, n + 1)
                    nc.scalar.activation(rt[0:1, 1, :], rt[0:1, 0, :], ACT.Exp).then_inc(s_e, 1)
                act.wait_ge(s_exp, 3)
                nc.scalar.activation(sc[0:1, 10:12], sc[0:1, 8:10], ACT.Exp).then_inc(s_e, 1)

            @block.tensor
            def _(pe):
                pe.wait_ge(s_mean, 1)
                for k in range(KD):
                    last = nc.tensor.matmul(bank[0][0:1, 0:NE], col[:, k:k + 1], wr_s[:, k, :],
                                            start=(k == 0), stop=(k == KD - 1))
                last.then_inc(s_lg, 1)
                pe.wait_ge(s_w, 1)
                nc.tensor.matmul(bank[1][:, 0:2], ones[0:1, :], sc[0:1, 10:12], start=True, stop=True)
                nc.tensor.matmul(bank[2][0:NE, 0:1], rt[0:1, 7, :], ones[0:1, 0:1], start=True, stop=True)\
                    .then_inc(s_b, 1)
                pe.wait_ge(s_wT, 1)
                nc.tensor.matmul(bank[3][:, 0:D], wd8[:, :], b2_s[:, :], start=True, stop=True).then_inc(s_b2, 1)

            @block.sync
            def _(sp):
                sp.wait_ge(s_idx, 1)
                for i in range(2):
                    e = sp.value_load(idx2[0:1, i:i + 1], min_val=0, max_val=NE - 1)
                    sp.dma_start(w1_s[:, i, :, :], w1[ds(e, 1), :, :].rearrange("a (k p) n -> p (a k) n", p=P))\
                        .then_inc(s_ld, 16)
                    sp.dma_start(w2_s[:, i, :, :], w2[ds(e, 1), :, :].rearrange("a (k p) n -> p (a k) n", p=P))\
                        .then_inc(s_ld, 16)
                    sp.dma_start(b1_s[:, i, :], b1[ds(e, 1), :].rearrange("a (k p) -> p (a k)", p=P),
                                 allow_slow_non_contiguous=True)\
                        .then_inc(s_ld, 16)
                sp.wait_ge(s_ld, 96)

    @scratch
    def top2_ffn(own):
        HW = U * P // 2
        mv = own("f0_mean", [P, U])
        st = own("f0_stats", [P, U, 6])
        rs, va, tmp = own("f0_rstd", [P, U]), own("f0_var", [P, U]), own("f0_tmp", [P, U])
        o = own("f0_out", [P, U, D])
        s_h, s_g, s_y = sem("f0_hidden_product"), sem("f0_gelu_done"), sem("f0_output_product")
        s_o, s_r = sem("f0_chunk_step"), sem("f0_row_step")
        NH = 2 * 2 * K0
        with nc.Block() as block:
            @block.tensor
            def _(pe):
                def chunk(c, first):
                    for i in range(NH):
                        f, h = divmod(i, 2)
                        e, b = divmod(f, K0)
                        if not first or i >= 4:
                            pe.wait_ge(s_g, c * NH + i - 3)
                        for k in range(KD):
                            last = nc.tensor.matmul(bank[i % 4][:, 0:HW], w1_s[:, e, k, b * P:(b + 1) * P],
                                                    xT_all[:, k, ds(c * (U * P) + h * HW, HW)],
                                                    start=(k == 0), stop=(k == KD - 1))
                        last.then_inc(s_h, 1)
                    pe.wait_ge(s_g, (c + 1) * NH)
                    for u in range(U):
                        if not first or u == U - 1:
                            pe.wait_ge(s_r, c * U + (1 if u == U - 1 else 0))
                        y = bank[4 + u % 4][:, 0:D]
                        for f in range(2 * K0):
                            last = nc.tensor.matmul(y, hT[:, f, u * P:(u + 1) * P], w2_s[:, f // K0, f % K0, :],
                                                    start=(f == 0), stop=(f == 2 * K0 - 1))
                        last.then_inc(s_y, 1)

                chunk(0, True)
                with pe.Fori(1, IT) as c:
                    chunk(c, False)

            @block.scalar
            def _(act):
                def chunk(c, first):
                    for i in range(NH):
                        f, h = divmod(i, 2)
                        e, b = divmod(f, K0)
                        act.wait_ge(s_h, c * NH + i + 1)
                        if not first:
                            act.wait_ge(s_y, c * U)
                        nc.scalar.activation(hT[:, f, h * HW:(h + 1) * HW], bank[i % 4][:, 0:HW], ACT.Gelu,
                                             bias=b1_s[:, e, b:b + 1]).then_inc(s_g, 1)

                chunk(0, True)
                with act.Fori(1, IT) as c:
                    chunk(c, False)

            @block.vector
            def _(dve):
                STEPS = 28
                with dve.Fori(0, IT) as c:
                    link = Chain(dve, s_o, c * STEPS)
                    for u in range(U):
                        last = normalise(xn[:, u, :], x_all, c * U + u)
                    link(last)
                    link(nc.vector.tensor_tensor(xn[:, :, :], xn[:, :, :], b2c[:, None, :].to_broadcast([P, U, D]),
                                                 ALU.add))
                    for u in range(U):
                        y = bank[4 + u % 4][:, 0:D]
                        dve.wait_ge(s_y, c * U + u + 1)
                        nc.vector.tensor_tensor(o[:, u, :], xn[:, u, :], y, ALU.add).then_inc(s_r, 1)
                    for u in range(U):
                        dve.wait_ge(s_r, c * U + u + 1)
                        last = nc.vector.bn_stats(st[:, u, :], o[:, u, :])
                    link(last)
                    join_stats(link, st, mv[:, :], va[:, :], tmp[:, :])
                    rsqrt(link, rs[:, :], va[:, :], tmp[:, :])
                    for u in range(U):
                        last = nc.vector.tensor_scalar(o[:, u, :], o[:, u, :], mv[:, u:u + 1], rs[:, u:u + 1],
                                                       ALU.subtract, ALU.mult)
                    link(last)
                    link(nc.vector.tensor_tensor(o[:, :, :], o[:, :, :], gamma_s[:, None, :].to_broadcast([P, U, D]),
                                                 ALU.mult))
                    link(nc.vector.tensor_tensor(o[:, :, :], o[:, :, :], beta_s[:, None, :].to_broadcast([P, U, D]),
                                                 ALU.add))
                    link(nc.vector.tensor_tensor(x_all[:, ds(c * U, U), :], x_all[:, ds(c * U, U), :], o[:, :, :],
                                                 ALU.add))
                    assert link.steps == STEPS

    def relational_table():
        s_xn, s_T, s_xT, s_mm = sem("p3_xn_ready"), sem("p3_transposed"), sem("p3_xT_ready"), sem("p3_product")
        s_ca, s_cv = sem("p3_copied_scalar"), sem("p3_copied_vector")
        s_out = [sem(f"p3_stored{s}") for s in range(RS)]
        PAIRS = R // 2
        PS = PAIRS // RS
        NB = PS
        with nc.Block() as block:
            @block.gpsimd
            def _(pool):
                nc.gpsimd.memset(agg[:, :, :], 0.0)

            NA, NV = (PS + 1) // 2, PS // 2

            def copies(eng, copy, it, u, done, count, parity):
                w = it * U + u
                for s in range(RS):
                    q = w * RS + s
                    if not (isinstance(it, int) and it == 0 and u == 0):
                        eng.wait_ge(s_out[s], 16 * w)
                    for i in range(parity, PS, 2):
                        eng.wait_ge(s_mm, q * PS + i + 1)
                        copy(stage[:, s, i * 512:(i + 1) * 512], bank[3 + i][:, :]).then_inc(done, 1)

            @block.vector
            def _(dve):
                row_stats(dve, "p3")

                def one_pass(it, first):
                    for u in range(U):
                        if not first:
                            dve.wait_ge(s_T, it * U + u - U + 1)
                        normalise(xn[:, u, :], x_all, it * U + u).then_inc(s_xn, 1)
                    for u in range(U):
                        copies(dve, nc.vector.tensor_copy, it, u, s_cv, NV, 1)

                one_pass(0, True)
                with dve.Fori(1, IT) as it:
                    one_pass(it, False)

            @block.scalar
            def _(act):
                def one_pass(it, first):
                    for u in range(U):
                        w = it * U + u
                        act.wait_ge(s_T, w + 1)
                        if not first:
                            act.wait_ge(s_mm, (w - U + 1) * PAIRS)
                        nc.scalar.copy(xT[:, u, :, :].rearrange("p k n -> p (k n)"), tslot(u)).then_inc(s_xT, 1)
                        copies(act, nc.scalar.copy, it, u, s_ca, NA, 0)

                one_pass(0, True)
                with act.Fori(1, IT) as it:
                    one_pass(it, False)

            @block.tensor
            def _(pe):
                pe.wait_ge(s_wrel, 16 * KD)

                def one_pass(it, first):
                    for u in range(U):
                        w = it * U + u
                        pe.wait_ge(s_xn, w + 1)
                        if not first or u >= 2:
                            pe.wait_ge(s_xT, w - 1)
                        transposes(u).then_inc(s_T, 1)
                        pe.wait_ge(s_xT, w + 1)
                        for s in range(RS):
                            q = w * RS + s
                            for i in range(PS):
                                if not (first and u == 0 and s == 0):
                                    if i % 2 == 0:
                                        pe.wait_ge(s_ca, (q - 1) * NA + i // 2 + 1)
                                    else:
                                        pe.wait_ge(s_cv, (q - 1) * NV + i // 2 + 1)
                                r = 2 * (s * PS + i)
                                for k in range(KD):
                                    last = nc.tensor.matmul(
                                        bank[3 + i][:, :], xT[:, u, k, :],
                                        wrel_s[:, k, r:r + 2, :].rearrange("p r d -> p (r d)"),
                                        start=(k == 0), stop=(k == KD - 1))
                                last.then_inc(s_mm, 1)

                one_pass(0, True)
                with pe.Fori(1, IT) as it:
                    one_pass(it, False)

            @block.sync
            def _(sp):
                def store(w, s, n):
                    by_scalar, by_vector = (w * RS + s + 1) * NA, (w * RS + s + 1) * NV
                    if not isinstance(w, int):
                        by_scalar, by_vector = sp.to_reg(by_scalar), sp.to_reg(by_vector)
                    sp.wait_ge(s_ca, by_scalar)
                    sp.wait_ge(s_cv, by_vector)
                    rows = rel_d[ds(w * P, n), s * SW:(s + 1) * SW]
                    sp.dma_start(rows, stage[0:n, s, :]).then_inc(s_out[s], 16)

                with sp.Fori(0, NT - 1) as w:
                    for s in range(RS):
                        store(w, s, P)
                for s in range(RS):
                    store(NT - 1, s, LAST)
                for s in range(RS):
                    sp.wait_ge(s_out[s], 16 * NT)

    def add_relu():
        with nc.Block() as block:
            @block.vector
            def _(dve):
                nc.vector.scalar_tensor_tensor(
                    out=x_all[:, :, :].rearrange("p t d -> p (t d)"), in0=agg_or_xT[:, :], scalar=0.0,
                    in1=x_all[:, :, :].rearrange("p t d -> p (t d)"), op0=ALU.max, op1=ALU.add)

            @block.scalar
            def _(act):
                for e in range(NE):
                    act.dma_start(wd_s[:, e * K1 * D:(e + 1) * K1 * D].rearrange("p (k d) -> p k d", k=K1),
                                  wd[e, :, :].rearrange("(k p) d -> p k d", p=P)).then_inc(s_wd, 16)

    logit = sb("logit", [P, NT, NE])
    prob = sb("prob", [P, NT])
    pos_i = sb("pos_i", [P, NT], I32)
    expert_i = sb("expert_i", [1, ST], I32)

    HW1 = U * P // 2

    def hidden_products(pe, c, first, s_h, s_g, rhs, width, parts):
        n = K1 * parts
        for i in range(n):
            f, h = divmod(i, parts)
            if not first or i >= 4:
                pe.wait_ge(s_g, c * n + i - 3)
            for k in range(KD):
                last = nc.tensor.matmul(bank[i % 4][:, 0:width], v1_s[:, k, f * P:(f + 1) * P], rhs(k, h),
                                        start=(k == 0), stop=(k == KD - 1))
            last.then_inc(s_h, 1)
        pe.wait_ge(s_g, (c + 1) * n)

    def choose_logits():
        s_h, s_g, s_l, s_c = sem("p4_hidden_product"), sem("p4_gelu_done"), sem("p4_logits"), sem("p4_logits_copied")
        NH = K1 * 2
        with nc.Block() as block:
            @block.tensor
            def _(pe):
                pe.wait_ge(s_v1, 16)

                def chunk(c, first):
                    hidden_products(pe, c, first, s_h, s_g,
                                    lambda k, h: xT_all[:, k, ds(c * (U * P) + h * HW1, HW1)], HW1, 2)
                    if not first:
                        pe.wait_ge(s_c, c)
                    for u in range(U):
                        for f in range(K1):
                            last = nc.tensor.matmul(bank[4][:, u * NE:(u + 1) * NE], hT[:, f, u * P:(u + 1) * P],
                                                    vg_s[:, f, :], start=(f == 0), stop=(f == K1 - 1))
                    last.then_inc(s_l, 1)

                chunk(0, True)
                with pe.Fori(1, IT) as c:
                    chunk(c, False)

            @block.scalar
            def _(act):
                def chunk(c, first):
                    for i in range(NH):
                        f, h = divmod(i, 2)
                        act.wait_ge(s_h, c * NH + i + 1)
                        if not first:
                            act.wait_ge(s_l, c)
                        nc.scalar.activation(hT[:, f, h * HW1:(h + 1) * HW1], bank[i % 4][:, 0:HW1], ACT.Gelu,
                                             bias=c1_s[:, f:f + 1]).then_inc(s_g, 1)

                chunk(0, True)
                with act.Fori(1, IT) as c:
                    chunk(c, False)

            @block.vector
            def _(dve):
                with dve.Fori(0, IT) as c:
                    dve.wait_ge(s_l, c + 1)
                    nc.vector.tensor_tensor(logit[:, ds(c * U, U), :],
                                            bank[4][:, 0:U * NE].rearrange("p (u e) -> p u e", u=U),
                                            cg_s[:, None, :].to_broadcast([P, U, NE]), ALU.add).then_inc(s_c, 1)

    @scratch
    def dispatch(own):
        sel = own("ds_sel", [P, NT, NE])
        work = own("ds_work", [P, NT, NE])
        run = [own(f"ds_run{i}", [P, NT, NE]) for i in range(2)]
        tot = own("ds_tot", [P, NT, NE])
        vec = own("ds_vec", [P, NT])
        cnt = own("ds_cnt", [P, NE, NT])
        nt = [own(f"ds_nt{i}", [P, NE]) for i in range(2)]
        base = own("ds_base", [P, NE])
        past = own("ds_past", [1, ST, NE])
        ex = own("ds_ex", [1, ST])
        s_step, s_max, s_exp = sem("ds_step"), sem("ds_exp_asked"), sem("ds_exp_done")
        s_sel, s_cum, s_pos = sem("ds_choice_ready"), sem("ds_counts"), sem("ds_rows_known")
        s_xn, s_put = sem("ds_xn_ready"), [sem(f"ds_scattered{u}") for u in range(U)]
        ALLE = [P, NT, NE]
        with nc.Block() as block:
            @block.vector
            def _(dve):
                link = Chain(dve, s_step)
                link(nc.vector.tensor_reduce(vec[:, :], logit[:, :, :], AX.X, ALU.max))
                nc.vector.tensor_tensor(work[:, :, :], logit[:, :, :], vec[:, :, None].to_broadcast(ALLE),
                                        ALU.subtract).then_inc(s_max, 1)
                dve.wait_ge(s_exp, 1)
                link(nc.vector.tensor_reduce(vec[:, :], sel[:, :, :], AX.X, ALU.add))
                link(nc.vector.reciprocal(vec[:, :], vec[:, :]))
                link(nc.vector.tensor_tensor(work[:, :, :], sel[:, :, :], vec[:, :, None].to_broadcast(ALLE), ALU.mult))
                link(nc.vector.tensor_reduce(prob[:, :], work[:, :, :], AX.X, ALU.max))
                link(nc.vector.tensor_tensor(work[:, :, :], work[:, :, :], prob[:, :, None].to_broadcast(ALLE),
                                             ALU.is_equal))
                link(nc.vector.scalar_tensor_tensor(
                    out=work[:, :, :], in0=work[:, :, :], scalar=-float(NE),
                    in1=iota_row[:, None, 0:NE].to_broadcast(ALLE), op0=ALU.mult, op1=ALU.add))
                link(nc.vector.tensor_reduce(vec[:, :], work[:, :, :], AX.X, ALU.min))
                link(nc.vector.tensor_tensor(sel[:, :, :], work[:, :, :], vec[:, :, None].to_broadcast(ALLE),
                                             ALU.is_equal))
                nc.vector.tensor_scalar(sel[:, NT - 1, :], sel[:, NT - 1, :], valid[:, 0:1], None, ALU.mult)\
                    .then_inc(s_sel, 1)
                dve.wait_ge(s_cum, 1)
                flat = [P, NT * NE]
                link(nc.vector.tensor_copy(tot[:, :, :].rearrange("p t e -> p (t e)"), bank[1][:, 0:NT * NE]))
                link(nc.vector.tensor_copy(run[0][:, :, :], tot[:, :, :]))
                a, step = 0, 1
                while step < NT:
                    link(nc.vector.tensor_copy(run[1 - a][:, 0:step, :], run[a][:, 0:step, :]))
                    link(nc.vector.tensor_tensor(run[1 - a][:, step:NT, :], run[a][:, step:NT, :],
                                                 run[a][:, 0:NT - step, :], ALU.add))
                    a, step = 1 - a, step * 2
                inc = run[a]
                link(nc.vector.tensor_tensor(cnt[:, :, :], inc[:, NT - 1, :, None].to_broadcast([P, NE, NT]),
                                             tile_base[:, None, :].to_broadcast([P, NE, NT]), ALU.is_gt))
                link(nc.vector.tensor_reduce(base[:, :], cnt[:, :, :], AX.X, ALU.add))
                link(nc.vector.tensor_copy(nt[0][:, :], base[:, :]))
                b, step = 0, 1
                while step < NE:
                    link(nc.vector.tensor_copy(nt[1 - b][:, 0:step], nt[b][:, 0:step]))
                    link(nc.vector.tensor_tensor(nt[1 - b][:, step:NE], nt[b][:, step:NE], nt[b][:, 0:NE - step],
                                                 ALU.add))
                    b, step = 1 - b, step * 2
                upto = nt[b]
                link(nc.vector.tensor_tensor(base[:, :], upto[:, :], base[:, :], ALU.subtract))
                link(nc.vector.tensor_scalar(base[:, :], base[:, :], float(P), None, ALU.mult))
                link(nc.vector.tensor_tensor(work[:, :, :], inc[:, :, :], tot[:, :, :], ALU.subtract))
                link(nc.vector.tensor_tensor(work[:, :, :], work[:, :, :],
                                             bank[0][:, 0:NT * NE].rearrange("p (t e) -> p t e", t=NT), ALU.add))
                link(nc.vector.tensor_tensor(work[:, :, :], work[:, :, :], base[:, None, :].to_broadcast(ALLE), ALU.add))
                link(nc.vector.tensor_tensor(work[:, :, :], work[:, :, :], sel[:, :, :], ALU.mult))
                link(nc.vector.tensor_reduce(vec[:, :], work[:, :, :], AX.X, ALU.add))
                nc.vector.tensor_copy(pos_i[:, :], vec[:, :]).then_inc(s_pos, 1)
                link(nc.vector.tensor_tensor(past[:, :, :], iota_row[0:1, 0:ST, None].to_broadcast([1, ST, NE]),
                                             upto[0:1, None, :].to_broadcast([1, ST, NE]), ALU.is_ge))
                link(nc.vector.tensor_reduce(ex[:, :], past[:, :, :], AX.X, ALU.add))
                nc.vector.tensor_scalar(expert_i[:, :], ex[:, :], NE - 1.0, None, ALU.min)
                for w in range(NT):
                    u = w % U
                    if w >= U:
                        dve.wait_ge(s_put[u], 16 * (w // U))
                    nc.vector.tensor_scalar(xn[:, u, :], x_all[:, w, :], mean[:, w:w + 1], rstd[:, w:w + 1],
                                            ALU.subtract, ALU.mult).then_inc(s_xn, 1)

            @block.scalar
            def _(act):
                act.wait_ge(s_max, 1)
                nc.scalar.activation(sel[:, :, :], work[:, :, :], ACT.Exp).then_inc(s_exp, 1)

            @block.tensor
            def _(pe):
                pe.wait_ge(s_sel, 1)
                rows = sel[:, :, :].rearrange("p t e -> p (t e)")
                nc.tensor.matmul(bank[0][:, 0:NT * NE], before[:, :], rows, start=True, stop=True)
                nc.tensor.matmul(bank[1][:, 0:NT * NE], ones[:, :], rows, start=True, stop=True).then_inc(s_cum, 1)

            @block.gpsimd
            def _(pool):
                pool.wait_ge(s_pos, 1)
                pool.wait_ge(s_zero, 16 * ZERO_DMAS)
                for w in range(NT):
                    n = P if w < NT - 1 else LAST
                    pool.wait_ge(s_xn, w + 1)
                    nc.gpsimd.indirect_dma_start(
                        out=sorted_d, out_offset=bass.IndirectOffsetOnAxis(ap=pos_i[0:n, w:w + 1], axis=0),
                        in_=xn[0:n, w % U, :], in_offset=None).then_inc(s_put[w % U], 16)
                for u in range(U):
                    pool.wait_ge(s_put[u], 16 * IT)

    def sorted_experts():
        CD = SC * D
        xs = agg_or_xT[:, 0:2 * CD].rearrange("p (i u d) -> p i u d", i=2, u=SC)
        xsT = agg_or_xT[:, 2 * CD:3 * CD].rearrange("p (k n) -> p k n", k=KD)
        yo = agg_or_xT[:, 3 * CD:4 * CD].rearrange("p (u d) -> p u d", u=SC)
        W = SC * P
        CN = ST // SC
        s_in, s_T, s_xT = [sem(f"se_rows_loaded{i}") for i in range(2)], sem("se_transposed"), sem("se_xT_ready")
        s_h, s_g, s_y = sem("se_hidden_product"), sem("se_gelu_done"), sem("se_output_product")
        s_r, s_st = sem("se_rows_ready"), sem("se_stored")
        rows_in = sorted_d.rearrange("(c u p) d -> c p u d", p=P, u=SC)
        rows_out = y_d.rearrange("(c u p) d -> c p u d", p=P, u=SC)
        with nc.Block() as block:
            @block.sync
            def _(sp):
                for i in range(2):
                    sp.dma_start(xs[:, i, :, :], rows_in[i]).then_inc(s_in[i], 16)
                with sp.Fori(1, CN // 2) as it:
                    for i in range(2):
                        c = it * 2 + i
                        sp.wait_ge(s_T, (c - 1) * SC)
                        sp.dma_start(xs[:, i, :, :], rows_in[ds(c, 1)].rearrange("a p u d -> p (a u) d"))\
                            .then_inc(s_in[i], 16)

            @block.tensor
            def _(pe):
                pe.wait_ge(s_v1, 16)
                pe.wait_ge(s_wd, 16 * NE)

                def chunk(c, i, first):
                    pe.wait_ge(s_in[i], 16 * (c // 2 + 1) if isinstance(c, int) else 16 * (c - i) // 2 + 16)
                    for u in range(SC):
                        if not first or u >= 2:
                            pe.wait_ge(s_xT, c * SC + u - 1)
                        for k in range(KD):
                            last = nc.tensor.transpose(bank[6 + u % 2][:, k * P:(k + 1) * P],
                                                       xs[:, i, u, k * P:(k + 1) * P], ident[:, :])
                        last.then_inc(s_T, 1)
                    pe.wait_ge(s_xT, (c + 1) * SC)
                    hidden_products(pe, c, first, s_h, s_g, lambda k, h: xsT[:, k, :], W, 1)
                    for u in range(SC):
                        e = pe.value_load(expert_i[0:1, ds(c * SC + u, 1)], min_val=0, max_val=NE - 1)
                        if not first or u >= 2:
                            pe.wait_ge(s_r, c * SC + u - 1)
                        y = bank[4 + u % 2][:, 0:D]
                        for f in range(K1):
                            last = nc.tensor.matmul(y, hT[:, f, u * P:(u + 1) * P],
                                                    wd_s[:, ds(e * (K1 * D) + f * D, D)],
                                                    start=(f == 0), stop=(f == K1 - 1))
                        last.then_inc(s_y, 1)

                chunk(0, 0, True)
                chunk(1, 1, False)
                with pe.Fori(1, CN // 2) as it:
                    for i in range(2):
                        chunk(it * 2 + i, i, False)

            @block.scalar
            def _(act):
                def chunk(c, first):
                    for f in range(K1):
                        act.wait_ge(s_h, c * K1 + f + 1)
                        if not first:
                            act.wait_ge(s_y, c * SC)
                        nc.scalar.activation(hT[:, f, 0:W], bank[f % 4][:, 0:W], ACT.Gelu,
                                             bias=c1_s[:, f:f + 1]).then_inc(s_g, 1)

                chunk(0, True)
                with act.Fori(1, CN) as c:
                    chunk(c, False)

            @block.vector
            def _(dve):
                dve.wait_ge(s_bd, 16)

                def chunk(c, first):
                    for u in range(SC):
                        dve.wait_ge(s_T, c * SC + u + 1)
                        if not first:
                            dve.wait_ge(s_h, c * K1)
                        nc.vector.tensor_copy(
                            xsT[:, :, u * P:(u + 1) * P],
                            bank[6 + u % 2][:, 0:D].rearrange("p (k n) -> p k n", k=KD))\
                            .then_inc(s_xT, 1)
                    for u in range(SC):
                        e = dve.value_load(expert_i[0:1, ds(c * SC + u, 1)], min_val=0, max_val=NE - 1)
                        dve.wait_ge(s_y, c * SC + u + 1)
                        if not first:
                            dve.wait_ge(s_st, 16 * c)
                        y = bank[4 + u % 2][:, 0:D]
                        nc.vector.tensor_tensor(yo[:, u, :], bd_s[:, ds(e, 1), :].rearrange("p a d -> p (a d)"), y,
                                                ALU.add).then_inc(s_r, 1)

                chunk(0, True)
                with dve.Fori(1, CN) as c:
                    chunk(c, False)

            @block.gpsimd
            def _(pool):
                with pool.Fori(0, CN) as c:
                    pool.wait_ge(s_r, (c + 1) * SC)
                    pool.dma_start(rows_out[ds(c, 1)].rearrange("a p u d -> p (a u) d"), yo[:, :, :])\
                        .then_inc(s_st, 16)
                pool.wait_ge(s_st, 16 * CN)

    def combine():
        s_got, s_add, s_out = [sem(f"cb_gathered{u}") for u in range(U)], sem("cb_added"), sem("cb_stored")
        with nc.Block() as block:
            @block.gpsimd
            def _(pool):
                for w in range(NT):
                    n = P if w < NT - 1 else LAST
                    if w >= U:
                        pool.wait_ge(s_add, w - U + 1)
                    nc.gpsimd.indirect_dma_start(
                        out=xn[0:n, w % U, :], out_offset=None, in_=y_d,
                        in_offset=bass.IndirectOffsetOnAxis(ap=pos_i[0:n, w:w + 1], axis=0)).then_inc(s_got[w % U], 16)

            @block.vector
            def _(dve):
                for w in range(NT):
                    n = P if w < NT - 1 else LAST
                    dve.wait_ge(s_got[w % U], 16 * (w // U + 1))
                    nc.vector.scalar_tensor_tensor(
                        out=x_all[0:n, w, :], in0=xn[0:n, w % U, :], scalar=prob[0:n, w:w + 1],
                        in1=x_all[0:n, w, :], op0=ALU.mult, op1=ALU.add).then_inc(s_add, 1)

            @block.sync
            def _(sp):
                for c in range(IT):
                    sp.wait_ge(s_add, (c + 1) * U)
                    if c < IT - 1:
                        sp.dma_start(out[c * U * P:(c + 1) * U * P, :].rearrange("(t p) d -> p t d", p=P),
                                     x_all[:, c * U:(c + 1) * U, :]).then_inc(s_out, 16)
                sp.dma_start(out[c * U * P:(NT - 1) * P, :].rearrange("(t p) d -> p t d", p=P),
                             x_all[:, c * U:NT - 1, :]).then_inc(s_out, 16)
                sp.dma_start(out[(NT - 1) * P:N, :], x_all[0:LAST, NT - 1, :]).then_inc(s_out, 16)
                sp.wait_ge(s_out, 16 * (IT + 1))

    valid = sb("valid", [P, 1])
    ZERO_DMAS = 4

    def prefetch():
        zeros = hT[:, 0:4, :].rearrange("p a b -> p (a b)")[:, 0:ST * D // ZERO_DMAS]
        s_z = sem("zeros_ready")
        with nc.Block() as block:
            @block.vector
            def _(dve):
                nc.vector.memset(zeros, 0.0).then_inc(s_z, 1)
                nc.vector.tensor_scalar(valid[:, :], before[:, LAST:LAST + 1], 1.0, None, ALU.mult)

            @block.scalar
            def _(act):
                act.wait_ge(s_z, 1)
                rows = sorted_d.rearrange("(p r) d -> p (r d)", p=P)
                n = ST * D // ZERO_DMAS
                for i in range(ZERO_DMAS):
                    act.dma_start(rows[:, i * n:(i + 1) * n], zeros).then_inc(s_zero, 16)
                for k in range(KD):
                    act.dma_start(wrel_s[:, k, :, :], wrel[:, k * P:(k + 1) * P, :].rearrange("r p d -> p r d"))\
                        .then_inc(s_wrel, 16)
                act.dma_start(v1_s[:, :, :], v1.rearrange("(k p) n -> p k n", p=P)).then_inc(s_v1, 16)
                act.dma_start(bd_s[:, :, :], bd.partition_broadcast(P)).then_inc(s_bd, 16)
                act.wait_ge(s_zero, 16 * ZERO_DMAS)

    parts = [
        load_and_constants, edges, prefetch, support,
        lambda: segment_sum("sum1", support_d, src_i, False, x_all),
        lambda: transposed_norm("ln2"), routing, top2_ffn,
        relational_table,
        lambda: segment_sum("sum3", rel_rows, srcrel_i, True, agg),
        add_relu,
        lambda: transposed_norm("ln4"), choose_logits, dispatch, sorted_experts, combine,
    ]
    with ctx:
        for part in parts:
            part()


INS = ["x", "src", "dst", "edge_type_20", "edge_weight1", "L0_gnn_weight", "L0_gnn_bias", "L0_ffn_Wr", "L0_ffn_br",
       "L0_ffn_W1", "L0_ffn_b1", "L0_ffn_W2", "L0_ffn_b2", "L0_ffn_gamma", "L0_ffn_beta", "L1_gnn_weight",
       "L1_ffn_W1", "L1_ffn_b1", "L1_ffn_Wg", "L1_ffn_bg", "L1_ffn_Wd", "L1_ffn_bd"]


def kernel(**inputs):
    import numpy as np
    import concourse.bacc as bacc
    from concourse.bass_utils import run_bass_kernel_spmd

    nc = bacc.Bacc("TRN2", target_bir_lowering=False, num_devices=1)
    arrays, args = {}, []
    for name in INS:
        a = np.ascontiguousarray(inputs[name])
        arrays[f"in_{name}"] = a
        args.append(nc.dram_tensor(f"in_{name}", a.shape, mybir.dt.from_np(a.dtype), kind="ExternalInput").ap())
    out = nc.dram_tensor("out", (N, D), F32, kind="ExternalOutput").ap()
    build(nc, *args, out)
    r = run_bass_kernel_spmd(nc, [arrays], core_ids=[0])
    return r.results[0]["out"]
```

```python
from contextlib import ExitStack

import concourse.bass as bass
from concourse import mybir

F32 = mybir.dt.float32
F32R = mybir.dt.float32r
I32 = mybir.dt.int32
ALU = mybir.AluOpType
ACT = mybir.ActivationFunctionType
AX = mybir.AxisListType

P = 128
N = 3125
D = 256
KD = D // P
NT = -(-N // P)
LAST = N - (NT - 1) * P
U = 5
IT = NT // U
NP = NT * P
E = 53125
CH = 4
GE = CH * P
NG = -(-E // GE)
ELAST = E - (NG - 1) * GE
RING = 4
R = 20
RS = 2
SW = R * D // RS
NE = 8
F0, F1 = 512, 1024
K0, K1 = F0 // P, F1 // P
ST = (N - NE) // P + NE
SC = 4
EPS = 1e-5
CAP = float(-(-N * 5 // (4 * NE)))
assert NT == U * IT and NG % RING == 0 and ST % (2 * SC) == 0


def build(nc, x, src, dst, rel, ew, wg, bias, wr, br, w1, b1, w2, b2, gamma, beta,
          wrel, v1, c1, vg, cg, wd, bd, out):
    ctx = ExitStack()

    def sb(name, shape, dt=F32):
        return ctx.enter_context(nc.sbuf_tensor(name, shape, dt))

    def sem(name):
        return ctx.enter_context(nc.semaphore(name))

    def ds(i, n):
        return bass.ds(i, n)

    def scratch(part):
        def run():
            with ExitStack() as own:
                part(lambda name, shape, dt=F32: own.enter_context(nc.sbuf_tensor(name, shape, dt)))
        return run

    support_d = nc.dram_tensor("support_d", (N, D), F32).ap()
    rel_d = nc.dram_tensor("rel_d", (N, R * D), F32).ap()
    rel_rows = rel_d.rearrange("n (r d) -> (n r) d", r=R)
    sorted_d = nc.dram_tensor("sorted_d", (ST * P, D), F32).ap()
    y_d = nc.dram_tensor("y_d", (ST * P, D), F32).ap()

    x_all = sb("x_all", [P, NT, D])
    agg_or_xT = sb("agg_or_xT", [P, NT * D])
    agg = agg_or_xT[:, :].rearrange("p (t d) -> p t d", t=NT)
    xT_all = agg_or_xT[:, :].rearrange("p (k n) -> p k n", k=KD)
    hT = sb("hT", [P, K1, U * P])
    ring = hT[:, :, :].rearrange("p a b -> p (a b)")[:, 0:RING * CH * D]\
        .rearrange("p (s j d) -> p s j d", s=RING, j=CH)
    xn = sb("xn", [P, U, D])
    ident = sb("ident", [P, P])
    ones = sb("ones", [P, P])
    before = sb("before", [P, P])
    iota_row = sb("iota_row", [P, P])
    tile_base = sb("tile_base", [P, NT])
    iota_i = sb("iota_i", [P, P], I32)
    base_i = sb("base_i", [P, NT], I32)
    stat = sb("stat", [P, NT, 6])
    mean = sb("mean", [P, NT])
    vsum = sb("vsum", [P, NT])
    dev = sb("dev", [P, NT])
    rstd = sb("rstd", [P, NT])
    wg_s = sb("wg_s", [P, KD, D])
    c1_s = sb("c1_s", [P, K1])
    vg_s = sb("vg_s", [P, K1, NE])
    cg_s = sb("cg_s", [P, NE])
    wr_s = sb("wr_s", [P, KD, NE])
    br_s = sb("br_s", [1, NE])
    b2_s = sb("b2_s", [NE, D])
    bias_s = sb("bias_s", [P, D])
    gamma_s = sb("gamma_s", [P, D])
    beta_s = sb("beta_s", [P, D])
    src_i = sb("src_i", [P, CH, NG], I32)
    srcrel_i = sb("srcrel_i", [P, CH, NG], I32)
    dst_f = sb("dst_f", [P, CH, NG])
    dst_rel = sb("dst_rel", [P, CH, NG + 1])
    ew_f = sb("ew_f", [P, CH, NG])
    idx_slot = sb("idx_slot", [P, RING, CH], I32)
    spans = sb("spans", [1, 3, NG + 1], I32)
    bank = [ctx.enter_context(nc.psum_tensor(f"bank{i}", [P, 512], F32)) for i in range(8)]

    def tslot(u):
        return bank[u % 3][:, 0:D]

    s_wrel, s_wd, s_v1, s_bd = sem("wrel_loaded"), sem("wd_loaded"), sem("v1_loaded"), sem("bd_loaded")
    s_zero = sem("sorted_d_zeroed")

    class Chain:

        def __init__(self, eng, s, start=0):
            self.eng, self.s, self.start, self.steps = eng, s, start, 0

        def __call__(self, ins):
            ins.then_inc(self.s, 1)
            self.steps += 1
            self.eng.wait_ge(self.s, self.start + self.steps)

    def rsqrt(link, y, v, t):
        link(nc.vector.tensor_scalar(t.bitcast(I32), v.bitcast(I32), 1, None, ALU.logical_shift_right))
        link(nc.vector.tensor_scalar(y.bitcast(I32), t.bitcast(I32), -1.0, float(0x5F3759DF), ALU.mult, ALU.add))
        for _ in range(3):
            link(nc.vector.tensor_tensor(t, y, y, ALU.mult))
            link(nc.vector.tensor_tensor(t, t, v, ALU.mult))
            link(nc.vector.tensor_scalar(t, t, -0.5, 1.5, ALU.mult, ALU.add))
            link(nc.vector.tensor_tensor(y, y, t, ALU.mult))

    def load_and_constants():
        s_x, s_small, s_const = sem("x_loaded"), sem("small_loaded"), sem("const_step")
        s_ci, s_pad = sem("iota_written"), sem("x_padding_zeroed")
        with nc.Block() as block:
            @block.sync
            def _(sp):
                sp.dma_start(x_all[:, 0:NT - 1, :], x[0:(NT - 1) * P, :].rearrange("(t p) d -> p t d", p=P))\
                    .then_inc(s_x, 16)
                sp.wait_ge(s_pad, 1)
                sp.dma_start(x_all[0:LAST, NT - 1, :], x[(NT - 1) * P:N, :]).then_inc(s_x, 16)
                sp.dma_start(wg_s[:, :, :], wg.rearrange("(k p) n -> p k n", p=P)).then_inc(s_small, 16)
                sp.dma_start(vg_s[:, :, :], vg.rearrange("(k p) n -> p k n", p=P)).then_inc(s_small, 16)
                sp.dma_start(wr_s[:, :, :], wr.rearrange("(k p) n -> p k n", p=P)).then_inc(s_small, 16)
                sp.dma_start(br_s[:, :], br.rearrange("(a n) -> a n", a=1)).then_inc(s_small, 16)
                sp.dma_start(b2_s[:, :], b2).then_inc(s_small, 16)
                sp.dma_start(c1_s[:, :], c1.rearrange("(k p) -> p k", p=P),
                             allow_slow_non_contiguous=True).then_inc(s_small, 16)
                for tile, vec in ((bias_s, bias), (gamma_s, gamma), (beta_s, beta), (cg_s, cg)):
                    sp.dma_start(tile[:, :], vec.partition_broadcast(P)).then_inc(s_small, 16)
                sp.wait_ge(s_x, 32)
                sp.wait_ge(s_small, 160)

            @block.gpsimd
            def _(pool):
                nc.gpsimd.iota(iota_i[:, :], pattern=[[1, P]], base=0, channel_multiplier=0).then_inc(s_ci, 1)
                nc.gpsimd.iota(base_i[:, :], pattern=[[P, NT]], base=0, channel_multiplier=0).then_inc(s_ci, 1)
                nc.gpsimd.memset(ident[:, :], 0.0).then_inc(s_const, 1)
                nc.gpsimd.memset(before[:, :], 1.0).then_inc(s_const, 1)
                nc.gpsimd.memset(ones[:, :], 1.0).then_inc(s_const, 1)
                pool.wait_ge(s_const, 3)
                nc.gpsimd.affine_select(out=ident[:, :], in_=ident[:, :], compare_op=ALU.not_equal, fill=1.0,
                                        base=0, pattern=[[-1, P]], channel_multiplier=1).then_inc(s_const, 1)
                nc.gpsimd.affine_select(out=before[:, :], in_=before[:, :], compare_op=ALU.is_gt, fill=0.0,
                                        base=0, pattern=[[1, P]], channel_multiplier=-1).then_inc(s_const, 1)

            @block.vector
            def _(dve):
                nc.vector.memset(x_all[:, NT - 1, :], 0.0).then_inc(s_pad, 1)
                dve.wait_ge(s_ci, 2)
                nc.vector.tensor_copy(iota_row[:, :], iota_i[:, :])
                nc.vector.tensor_copy(tile_base[:, :], base_i[:, :])

    @scratch
    def edges(own):
        raw = own("raw", [P, 3, GE], I32)
        ef = own("ef", [P, 4, GE])
        SRC, SRCREL, DST, EW = range(4)
        lim = own("lim", [P, 2])
        cmpr = own("cmpr", [P, 2, NT - 1])
        tiles = own("tiles", [P, 3])
        first_row = own("first_row", [1, NG])
        s_pad, s_in, s_step = sem("edge_padding"), sem("edges_loaded"), sem("edge_step")
        s_f, s_t, s_tab, s_ev = sem("edge_rows_ready"), sem("edges_transposed"), sem("spans_summed"), sem("edge_copies")
        with nc.Block() as block:
            @block.sync
            def _(sp):
                sp.wait_ge(s_pad, 3)
                for a, v in ((0, src), (1, rel), (2, dst)):
                    sp.dma_start(raw[0:NG - 1, a, :], v[0:(NG - 1) * GE].rearrange("(g e) -> g e", e=GE))\
                        .then_inc(s_in, 16)
                    sp.dma_start(raw[NG - 1:NG, a, 0:ELAST], v[(NG - 1) * GE:E].rearrange("(g e) -> g e", g=1))\
                        .then_inc(s_in, 16)
                sp.dma_start(ef[0:NG - 1, EW, :], ew[0:(NG - 1) * GE, :].rearrange("(g e) a -> g (e a)", e=GE))\
                    .then_inc(s_in, 16)
                sp.dma_start(ef[NG - 1:NG, EW, 0:ELAST], ew[(NG - 1) * GE:E, :].rearrange("(g e) a -> g (e a)", g=1))\
                    .then_inc(s_in, 16)

            @block.vector
            def _(dve):
                nc.vector.memset(raw[:, 0:2, :], 0).then_inc(s_pad, 1)
                nc.vector.memset(raw[:, 2, :], NP - 1).then_inc(s_pad, 1)
                nc.vector.memset(ef[:, EW, :], 0.0).then_inc(s_pad, 1)
                link = Chain(dve, s_step)
                dve.wait_ge(s_in, 128)
                link(nc.vector.tensor_copy(ef[:, SRC, :], raw[:, 0, :]))
                link(nc.vector.tensor_copy(ef[:, SRCREL, :], raw[:, 1, :]))
                link(nc.vector.tensor_copy(ef[:, DST, :], raw[:, 2, :]))
                nc.vector.scalar_tensor_tensor(out=ef[:, SRCREL, :], in0=ef[:, SRC, :], scalar=float(R),
                                               in1=ef[:, SRCREL, :], op0=ALU.mult, op1=ALU.add).then_inc(s_f, 1)
                link(nc.vector.tensor_reduce(lim[0:NG, 0:1], ef[0:NG, DST, :], AX.X, ALU.min))
                link(nc.vector.tensor_reduce(lim[0:NG, 1:2], ef[0:NG, DST, :], AX.X, ALU.max))
                for m in range(2):
                    link(nc.vector.tensor_scalar(cmpr[0:NG, m, :], tile_base[0:NG, 1:NT], lim[0:NG, m:m + 1], None,
                                                 ALU.is_le))
                link(nc.vector.tensor_reduce(tiles[0:NG, 0:2], cmpr[0:NG, :, :], AX.X, ALU.add))
                nc.vector.tensor_tensor(tiles[0:NG, 2:3], tiles[0:NG, 1:2], tiles[0:NG, 0:1], ALU.subtract)\
                    .then_inc(s_f, 1)
                dve.wait_ge(s_t, 4)
                nc.vector.tensor_copy(src_i[:, :, :].rearrange("p j g -> p (j g)"), bank[SRC][:, 0:CH * NG])
                nc.vector.tensor_copy(srcrel_i[:, :, :].rearrange("p j g -> p (j g)"), bank[SRCREL][:, 0:CH * NG])
                nc.vector.tensor_copy(dst_f[:, :, :].rearrange("p j g -> p (j g)"), bank[DST][:, 0:CH * NG])\
                    .then_inc(s_ev, 1)
                nc.vector.memset(dst_rel[:, :, NG:NG + 1], 0.0)
                nc.vector.tensor_copy(ew_f[:, :, :].rearrange("p j g -> p (j g)"), bank[EW][:, 0:CH * NG])
                dve.wait_ge(s_tab, 1)
                nc.vector.tensor_copy(spans[:, :, 0:NG], bank[4][0:1, 0:3 * NG].rearrange("a (k g) -> a k g", k=3))
                nc.vector.memset(spans[:, :, NG:NG + 1], 0)
                nc.vector.tensor_scalar(first_row[:, :], bank[4][0:1, NG:2 * NG], -float(P), None, ALU.mult)\
                    .then_inc(s_ev, 1)
                dve.wait_ge(s_tab, 2)
                dve.wait_ge(s_ev, 2)
                nc.vector.tensor_tensor(dst_rel[:, :, 0:NG], dst_f[:, :, :],
                                        bank[5][:, None, 0:NG].to_broadcast([P, CH, NG]), ALU.add)

            @block.tensor
            def _(pe):
                pe.wait_ge(s_f, 1)
                for a in range(4):
                    for j in range(CH):
                        last = nc.tensor.transpose(bank[a][:, j * NG:(j + 1) * NG], ef[0:NG, a, j * P:(j + 1) * P],
                                                   ident[0:NG, 0:NG])
                    last.then_inc(s_t, 1)
                pe.wait_ge(s_f, 2)
                nc.tensor.matmul(bank[4][0:1, 0:NG], tiles[0:NG, 2:3], before[0:NG, 0:NG], start=True, stop=True)
                nc.tensor.matmul(bank[4][0:1, NG:2 * NG], tiles[0:NG, 0:1], ident[0:NG, 0:NG], start=True, stop=True)
                nc.tensor.matmul(bank[4][0:1, 2 * NG:3 * NG], tiles[0:NG, 2:3], ident[0:NG, 0:NG],
                                 start=True, stop=True).then_inc(s_tab, 1)
                pe.wait_ge(s_ev, 2)
                nc.tensor.matmul(bank[5][:, 0:NG], ones[0:1, :], first_row[:, :], start=True, stop=True)\
                    .then_inc(s_tab, 1)

    def join_stats(link, st, m, v, t):
        link(nc.vector.tensor_tensor(m, st[:, :, 1], st[:, :, 4], ALU.add))
        link(nc.vector.tensor_tensor(t, st[:, :, 1], st[:, :, 4], ALU.subtract))
        link(nc.vector.tensor_scalar(m, m, 0.5, None, ALU.mult))
        link(nc.vector.tensor_tensor(t, t, t, ALU.mult))
        link(nc.vector.tensor_tensor(v, st[:, :, 2], st[:, :, 5], ALU.add))
        link(nc.vector.scalar_tensor_tensor(out=v, in0=t, scalar=D / 4.0, in1=v, op0=ALU.mult, op1=ALU.add))
        link(nc.vector.tensor_scalar(v, v, 1.0 / D, EPS, ALU.mult, ALU.add))

    def row_stats(dve, tag):
        s_bn, s_st = sem(f"{tag}_bn_stats"), sem(f"{tag}_stat_step")
        with dve.Fori(0, IT) as it:
            for u in range(U):
                w = it * U + u
                nc.vector.bn_stats(stat[:, ds(w, 1), :].rearrange("p a s -> p (a s)"),
                                   x_all[:, ds(w, 1), :].rearrange("p a d -> p (a d)")).then_inc(s_bn, 1)
        dve.wait_ge(s_bn, NT)
        link = Chain(dve, s_st)
        join_stats(link, stat, mean[:, :], vsum[:, :], dev[:, :])
        rsqrt(link, rstd[:, :], vsum[:, :], dev[:, :])

    def normalise(to, of, w):
        return nc.vector.tensor_scalar(to, of[:, ds(w, 1), :].rearrange("p a d -> p (a d)"), mean[:, ds(w, 1)], rstd[:, ds(w, 1)],
                                       ALU.subtract, ALU.mult)

    def transposes(u):
        for k in range(KD):
            last = nc.tensor.transpose(tslot(u)[:, k * P:(k + 1) * P], xn[:, u, k * P:(k + 1) * P], ident[:, :])
        return last

    @scratch
    def support(own):
        s_xn, s_T, s_xT, s_mm = sem("p1_xn_ready"), sem("p1_transposed"), sem("p1_xT_ready"), sem("p1_product")
        s_row, s_out = sem("p1_rows_ready"), [sem(f"p1_rows_stored{u}") for u in range(U)]
        rows = hT[:, 0:2, :].rearrange("p a b -> p (a b)").rearrange("p (u d) -> p u d", u=U)
        xT = own("p1_xT", [P, U, KD, P])
        with nc.Block() as block:
            @block.vector
            def _(dve):
                row_stats(dve, "p1")

                def tile(it, u, first):
                    w = it * U + u
                    if not first:
                        dve.wait_ge(s_T, w - U + 1)
                    normalise(xn[:, u, :], x_all, w).then_inc(s_xn, 1)

                def rows_of(it, u, first):
                    w = it * U + u
                    dve.wait_ge(s_mm, w + 1)
                    if not first:
                        dve.wait_ge(s_out[u], 16 * it)
                    nc.vector.tensor_copy(rows[:, u, :], bank[3 + u][:, 0:D]).then_inc(s_row, 1)
                    nc.vector.tensor_tensor(x_all[:, ds(w, 1), :], x_all[:, ds(w, 1), :],
                                            bias_s[:, None, :], ALU.add)

                def one_pass(it, first):
                    for u in range(U):
                        tile(it, u, first)
                    for u in range(U):
                        rows_of(it, u, first)

                one_pass(0, True)
                with dve.Fori(1, IT) as it:
                    one_pass(it, False)

            @block.tensor
            def _(pe):
                def one_pass(it, first):
                    for v in range(U + 1):
                        if v < U:
                            w = it * U + v
                            pe.wait_ge(s_xn, w + 1)
                            if not first or v >= 2:
                                pe.wait_ge(s_xT, w - 1)
                            transposes(v).then_inc(s_T, 1)
                        if v > 0:
                            u = v - 1
                            w = it * U + u
                            pe.wait_ge(s_xT, w + 1)
                            if not first:
                                pe.wait_ge(s_row, w - U + 1)
                            for k in range(KD):
                                last = nc.tensor.matmul(bank[3 + u][:, 0:D], xT[:, u, k, :], wg_s[:, k, :],
                                                        start=(k == 0), stop=(k == KD - 1))
                            last.then_inc(s_mm, 1)

                one_pass(0, True)
                with pe.Fori(1, IT) as it:
                    one_pass(it, False)

            @block.scalar
            def _(act):
                def one_pass(it, first):
                    for u in range(U):
                        w = it * U + u
                        act.wait_ge(s_T, w + 1)
                        if not first:
                            act.wait_ge(s_mm, w - U + 1)
                        nc.scalar.copy(xT[:, u, :, :].rearrange("p k n -> p (k n)"), tslot(u)).then_inc(s_xT, 1)

                one_pass(0, True)
                with act.Fori(1, IT) as it:
                    one_pass(it, False)

            @block.sync
            def _(sp):
                with sp.Fori(0, IT - 1) as it:
                    for u in range(U):
                        w = it * U + u
                        sp.wait_ge(s_row, w + 1)
                        sp.dma_start(support_d[ds(w * P, P), :], rows[:, u, :]).then_inc(s_out[u], 16)
                for u in range(U):
                    w = (IT - 1) * U + u
                    n = min(P, N - w * P)
                    sp.wait_ge(s_row, w + 1)
                    sp.dma_start(support_d[w * P:w * P + n, :], rows[0:n, u, :]).then_inc(s_out[u], 16)
                for u in range(U):
                    sp.wait_ge(s_out[u], 16 * IT)

    def segment_sum(tag, table, index, weighted, acc, meanwhile):
        with ExitStack() as mine:
            def own(name, shape, dt=F32):
                return mine.enter_context(nc.sbuf_tensor(f"{tag}_{name}", shape, dt))

            segment_sum_program(own, tag, table, index, weighted, acc, meanwhile)

    def segment_sum_program(own, tag, table, index, weighted, acc, meanwhile):
        head = own("head", [P, RING, CH, D], F32R)
        rest = own("rest", [P, 2, CH, D], F32R)
        onehot = own("onehot", [P, 3, CH, P], F32R)
        dst_rel2 = own("dst_rel2", [P, CH])
        s_idx, s_got = sem(f"{tag}_indices_ready"), [sem(f"{tag}_rows_gathered{s}") for s in range(RING)]
        s_go = sem(f"{tag}_gathers_started")
        s_head, s_rest = sem(f"{tag}_heads_ready"), sem(f"{tag}_rests_ready")
        s_hot = sem(f"{tag}_onehot_ready")
        s_sum, s_acc, s_used = sem(f"{tag}_summed"), sem(f"{tag}_added"), sem(f"{tag}_group_used")
        s_rel2, s_hot2 = sem(f"{tag}_further_dst_rel"), sem(f"{tag}_further_onehot")
        s_sum2, s_acc2 = sem(f"{tag}_further_summed"), sem(f"{tag}_further_added")
        passes, LAP = NG // (2 * RING), 2 * RING

        def column(of, g):
            return of[:, :, ds(g, 1)].rearrange("p j a -> p (j a)")

        with nc.Block() as block:
            @block.sync
            def _(sp):
                meanwhile(sp)

            @block.scalar
            def _(act):
                def indices(g, s):
                    nc.scalar.copy(idx_slot[:, s, :], column(index, g)).then_inc(s_idx, 1)

                def group(it, s, first, last):
                    g = it * LAP + s
                    act.wait_ge(s_got[s % RING], 16 * CH * (2 * it + s // RING + 1))
                    if not first or s >= RING:
                        act.wait_ge(s_used, g - RING + 1)
                    for j in range(CH):
                        ins = nc.scalar.activation(head[:, s % RING, j, :], ring[:, s % RING, j, :], ACT.Copy,
                                                   scale=ew_f[:, j, ds(g, 1)] if weighted else 1.0)
                    ins.then_inc(s_head, 1)
                    if not (last and s > LAP - RING) and not (first and s == 0):
                        act.wait_ge(s_rest, g)
                        indices(g + RING - 1, (s + RING - 1) % RING)

                for s in range(RING):
                    indices(s, s)
                for s in range(LAP):
                    group(0, s, True, False)
                with act.Fori(1, passes - 1) as it:
                    for s in range(LAP):
                        group(it, s, False, False)
                for s in range(LAP):
                    group(passes - 1, s, False, True)

            @block.gpsimd
            def _(pool):
                with pool.Fori(0, passes) as it:
                    for s in range(LAP):
                        pool.wait_ge(s_idx, it * LAP + s + 1)
                        pool.sem_inc(s_go, 1)
                        for j in range(CH):
                            nc.gpsimd.indirect_dma_start(
                                out=ring[:, s % RING, j, :], out_offset=None, in_=table,
                                in_offset=bass.IndirectOffsetOnAxis(ap=idx_slot[:, s % RING, j:j + 1], axis=0),
                            ).then_inc(s_got[s % RING], 16)

            @block.vector
            def _(dve):
                def make_onehot(slot, rel_of):
                    for j in range(CH):
                        last = nc.vector.tensor_scalar(onehot[:, slot, j, :], iota_row[:, :], rel_of(j), None,
                                                       ALU.is_equal)
                    return last

                def first_onehot(g, s):
                    make_onehot(s % 2, lambda j: dst_rel[:, j, ds(g, 1)]).then_inc(s_hot, 1)

                def add(w, b):
                    return nc.vector.tensor_tensor(acc[:, ds(w, 1), :], acc[:, ds(w, 1), :],
                                                   bank[b][:, None, 0:D], ALU.add)

                def split(it, s):
                    g = it * LAP + s
                    dve.wait_ge(s_head, g + 1)
                    if weighted:
                        for j in range(CH):
                            last = nc.vector.scalar_tensor_tensor(
                                out=rest[:, s % 2, j, :], in0=ring[:, s % RING, j, :], scalar=ew_f[:, j, ds(g, 1)],
                                in1=head[:, s % RING, j, :].bitcast(F32), op0=ALU.mult, op1=ALU.subtract)
                    else:
                        last = nc.vector.tensor_tensor(rest[:, s % 2, :, :], ring[:, s % RING, :, :],
                                                       head[:, s % RING, :, :].bitcast(F32), ALU.subtract)
                    last.then_inc(s_rest, 1)

                def finish(g, b):
                    w = dve.value_load(spans[0:1, 1, ds(g, 1)], min_val=0, max_val=NT - 1)
                    further = dve.value_load(spans[0:1, 2, ds(g, 1)], min_val=0, max_val=NT - 1)
                    dve.wait_ge(s_sum, g + 1)
                    dve.wait_ge(s_acc, g + 1)
                    add(w, b).then_inc(s_acc, 1)
                    with dve.If(further > 0):
                        before_g = dve.value_load(spans[0:1, 0, ds(g, 1)], min_val=0, max_val=NG * NT)
                        with dve.Fori(0, further) as i:
                            v = nc.s_assert_within(w + i + 1, 1, NT - 1, skip_runtime_bounds_check_because=
                                                   "a group's tiles end at that of its greatest destination")
                            n = before_g + i + 1
                            nc.vector.tensor_scalar(dst_rel2[:, :], column(dst_f, g), tile_base[:, ds(v, 1)], None,
                                                    ALU.subtract).then_inc(s_rel2, 1)
                            dve.wait_ge(s_rel2, n)
                            make_onehot(2, lambda j: dst_rel2[:, j:j + 1]).then_inc(s_hot2, 1)
                            dve.wait_ge(s_sum2, n)
                            add(v, 2).then_inc(s_acc2, 1)
                            dve.wait_ge(s_acc2, n)
                        nc.vector.nop()
                    nc.vector.nop().then_inc(s_used, 1)

                def step(it, s, first):
                    g = it * LAP + s
                    split(it, s)
                    if not first:
                        finish(g - 1, (s - 1) % 2)
                    first_onehot(g + 1, s + 1)

                dve.sem_inc(s_acc, 1)
                first_onehot(0, 0)
                for s in range(LAP):
                    step(0, s, s == 0)
                with dve.Fori(1, passes) as it:
                    for s in range(LAP):
                        step(it, s, False)
                finish(NG - 1, (NG - 1) % 2)

            @block.tensor
            def _(pe):
                def product(slot, s, b):
                    for j in range(CH):
                        for i, part in enumerate((head[:, s % RING, j, :], rest[:, s % 2, j, :])):
                            last = nc.tensor.matmul(bank[b][:, 0:D], onehot[:, slot, j, :], part,
                                                    start=(j == i == 0), stop=(j == CH - 1 and i == 1))
                    return last

                with pe.Fori(0, passes) as it:
                    for s in range(LAP):
                        g = it * LAP + s
                        further = pe.value_load(spans[0:1, 2, ds(g, 1)], min_val=0, max_val=NT - 1)
                        pe.wait_ge(s_hot, g + 1)
                        pe.wait_ge(s_rest, g + 1)
                        product(s % 2, s, s % 2).then_inc(s_sum, 1)
                        with pe.If(further > 0):
                            before_g = pe.value_load(spans[0:1, 0, ds(g, 1)], min_val=0, max_val=NG * NT)
                            with pe.Fori(0, further) as i:
                                pe.wait_ge(s_hot2, before_g + i + 1)
                                product(2, s, 2).then_inc(s_sum2, 1)
                            pe.nop()
                        pe.nop()

    def transposed_norm(tag):
        s_xn, s_T, s_xT = sem(f"{tag}_xn_ready"), sem(f"{tag}_transposed"), sem(f"{tag}_xT_ready")
        with nc.Block() as block:
            @block.vector
            def _(dve):
                row_stats(dve, tag)
                for u in range(U):
                    normalise(xn[:, u, :], x_all, u).then_inc(s_xn, 1)
                with dve.Fori(1, IT) as it:
                    for u in range(U):
                        w = it * U + u
                        dve.wait_ge(s_T, w - U + 1)
                        normalise(xn[:, u, :], x_all, w).then_inc(s_xn, 1)

            @block.tensor
            def _(pe):
                def tile(w, u, first):
                    pe.wait_ge(s_xn, w + 1)
                    if not first or u >= 2:
                        pe.wait_ge(s_xT, w - 1)
                    transposes(u).then_inc(s_T, 1)

                for u in range(U):
                    tile(u, u, True)
                with pe.Fori(1, IT) as it:
                    for u in range(U):
                        tile(it * U + u, u, False)

            @block.scalar
            def _(act):
                with act.Fori(0, IT) as it:
                    for u in range(U):
                        w = it * U + u
                        act.wait_ge(s_T, w + 1)
                        nc.scalar.copy(xT_all[:, :, ds(w * P, P)], tslot(u).rearrange("p (k n) -> p k n", k=KD))\
                            .then_inc(s_xT, 1)

    idx2 = sb("idx2", [1, 2], I32)
    w_pair = sb("w_pair", [P, 2])

    @scratch
    def routing(own):
        col = own("rt_col", [P, KD])
        rt = own("rt_rows", [1, 10, NE])
        sc = own("rt_scalars", [1, 12])
        wd8 = own("rt_wd8", [NE, P])
        s_mean, s_lg, s_step, s_idx = sem("rt_mean"), sem("rt_logits"), sem("rt_step"), sem("rt_experts_known")
        s_exp, s_w, s_e, s_b = sem("rt_exp_asked"), sem("rt_weights"), sem("rt_exp_done"), sem("rt_broadcast")
        s_ld, s_wT, s_b2 = sem("rt_matrices_loaded"), sem("rt_weights_on_partitions"), sem("rt_b2_done")
        with nc.Block() as block:
            @block.vector
            def _(dve):
                link = Chain(dve, s_step)

                def row(i):
                    return rt[0:1, i, :]

                def s(i):
                    return sc[0:1, i:i + 1]

                nc.vector.tensor_reduce(col[:, :], xT_all[:, :, 0:N], AX.X, ALU.add).then_inc(s_mean, 1)
                dve.wait_ge(s_lg, 1)
                link(nc.vector.tensor_scalar(row(0), bank[0][0:1, 0:NE], 1.0 / N, None, ALU.mult))
                link(nc.vector.tensor_tensor(row(0), row(0), br_s[:, :], ALU.add))

                def softmax(n):
                    link(nc.vector.tensor_reduce(s(0), row(0), AX.X, ALU.max))
                    nc.vector.tensor_scalar(row(0), row(0), s(0), None, ALU.subtract).then_inc(s_exp, 1)
                    dve.wait_ge(s_e, n)
                    link(nc.vector.tensor_reduce(s(1), row(1), AX.X, ALU.add))
                    link(nc.vector.reciprocal(s(2), s(1)))
                    link(nc.vector.tensor_scalar(row(1), row(1), s(2), None, ALU.mult))

                softmax(1)
                link(nc.vector.tensor_scalar(row(2), row(1), float(N), CAP, ALU.mult, ALU.max))
                link(nc.vector.memset(row(3), CAP))
                link(nc.vector.reciprocal(row(2), row(2)))
                link(nc.vector.tensor_scalar(row(3), row(2), CAP, 1.0, ALU.mult, ALU.min))
                link(nc.vector.tensor_tensor(row(0), row(1), row(3), ALU.mult))
                softmax(2)

                def first_greatest(value, index, hot):
                    link(nc.vector.tensor_reduce(value, row(1), AX.X, ALU.max))
                    link(nc.vector.tensor_scalar(row(4), row(1), value, -float(NE), ALU.is_equal, ALU.mult))
                    link(nc.vector.tensor_tensor(row(4), row(4), iota_row[0:1, 0:NE], ALU.add))
                    link(nc.vector.tensor_reduce(index, row(4), AX.X, ALU.min))
                    link(nc.vector.tensor_scalar(hot, row(4), index, None, ALU.is_equal))
                    link(nc.vector.tensor_scalar(index, index, float(NE), None, ALU.add))

                first_greatest(s(4), s(6), row(5))
                link(nc.vector.scalar_tensor_tensor(out=row(1), in0=row(5), scalar=-2.0, in1=row(1),
                                                    op0=ALU.mult, op1=ALU.add))
                first_greatest(s(5), s(7), row(6))
                nc.vector.tensor_copy(idx2[:, :], sc[0:1, 6:8]).then_inc(s_idx, 1)
                nc.vector.tensor_scalar(sc[0:1, 8:10], sc[0:1, 4:6], s(4), None, ALU.subtract).then_inc(s_exp, 1)
                dve.wait_ge(s_e, 3)
                link(nc.vector.tensor_reduce(s(0), sc[0:1, 10:12], AX.X, ALU.add))
                link(nc.vector.reciprocal(s(1), s(0)))
                link(nc.vector.tensor_scalar(sc[0:1, 10:12], sc[0:1, 10:12], s(1), None, ALU.mult))
                link(nc.vector.tensor_scalar(row(5), row(5), s(10), None, ALU.mult))
                nc.vector.scalar_tensor_tensor(out=row(7), in0=row(6), scalar=s(11), in1=row(5),
                                               op0=ALU.mult, op1=ALU.add).then_inc(s_w, 1)
                dve.wait_ge(s_b, 1)
                link(nc.vector.tensor_copy(w_pair[:, :], bank[1][:, 0:2]))
                nc.vector.tensor_scalar(wd8[:, :], ones[0:NE, :], bank[2][0:NE, 0:1], None, ALU.mult).then_inc(s_wT, 1)
                dve.wait_ge(s_b2, 1)
                nc.vector.tensor_copy(late["b2c"][:, :], bank[3][:, 0:D])
                dve.wait_ge(s_ld, 96)
                for i in range(2):
                    nc.vector.tensor_scalar(late["w2_s"][:, i, :, :], late["w2_s"][:, i, :, :], w_pair[:, i:i + 1], None, ALU.mult)

            @block.scalar
            def _(act):
                for n in range(2):
                    act.wait_ge(s_exp, n + 1)
                    nc.scalar.activation(rt[0:1, 1, :], rt[0:1, 0, :], ACT.Exp).then_inc(s_e, 1)
                act.wait_ge(s_exp, 3)
                nc.scalar.activation(sc[0:1, 10:12], sc[0:1, 8:10], ACT.Exp).then_inc(s_e, 1)

            @block.tensor
            def _(pe):
                pe.wait_ge(s_mean, 1)
                for k in range(KD):
                    last = nc.tensor.matmul(bank[0][0:1, 0:NE], col[:, k:k + 1], wr_s[:, k, :],
                                            start=(k == 0), stop=(k == KD - 1))
                last.then_inc(s_lg, 1)
                pe.wait_ge(s_w, 1)
                nc.tensor.matmul(bank[1][:, 0:2], ones[0:1, :], sc[0:1, 10:12], start=True, stop=True)
                nc.tensor.matmul(bank[2][0:NE, 0:1], rt[0:1, 7, :], ones[0:1, 0:1], start=True, stop=True)\
                    .then_inc(s_b, 1)
                pe.wait_ge(s_wT, 1)
                nc.tensor.matmul(bank[3][:, 0:D], wd8[:, :], b2_s[:, :], start=True, stop=True).then_inc(s_b2, 1)

            @block.sync
            def _(sp):
                sp.wait_ge(s_idx, 1)
                for i in range(2):
                    e = sp.value_load(idx2[0:1, i:i + 1], min_val=0, max_val=NE - 1)
                    sp.dma_start(late["w1_s"][:, i, :, :], w1[ds(e, 1), :, :].rearrange("a (k p) n -> p (a k) n", p=P))\
                        .then_inc(s_ld, 16)
                    sp.dma_start(late["w2_s"][:, i, :, :], w2[ds(e, 1), :, :].rearrange("a (k p) n -> p (a k) n", p=P))\
                        .then_inc(s_ld, 16)
                    sp.dma_start(late["b1_s"][:, i, :], b1[ds(e, 1), :].rearrange("a (k p) -> p (a k)", p=P),
                                 allow_slow_non_contiguous=True)\
                        .then_inc(s_ld, 16)
                sp.wait_ge(s_ld, 96)

    @scratch
    def top2_ffn(own):
        HW = U * P // 2
        mv = own("f0_mean", [P, U])
        st = own("f0_stats", [P, U, 6])
        rs, va, tmp = own("f0_rstd", [P, U]), own("f0_var", [P, U]), own("f0_tmp", [P, U])
        o = own("f0_out", [P, U, D])
        s_h, s_g, s_y = sem("f0_hidden_product"), sem("f0_gelu_done"), sem("f0_output_product")
        s_o, s_r = sem("f0_chunk_step"), sem("f0_row_step")
        NH = 2 * 2 * K0
        with nc.Block() as block:
            @block.tensor
            def _(pe):
                def chunk(c, first):
                    for i in range(NH):
                        f, h = divmod(i, 2)
                        e, b = divmod(f, K0)
                        if not first or i >= 4:
                            pe.wait_ge(s_g, c * NH + i - 3)
                        for k in range(KD):
                            last = nc.tensor.matmul(bank[i % 4][:, 0:HW], late["w1_s"][:, e, k, b * P:(b + 1) * P],
                                                    xT_all[:, k, ds(c * (U * P) + h * HW, HW)],
                                                    start=(k == 0), stop=(k == KD - 1))
                        last.then_inc(s_h, 1)
                    pe.wait_ge(s_g, (c + 1) * NH)
                    for u in range(U):
                        if not first or u == U - 1:
                            pe.wait_ge(s_r, c * U + (1 if u == U - 1 else 0))
                        y = bank[4 + u % 4][:, 0:D]
                        for f in range(2 * K0):
                            last = nc.tensor.matmul(y, hT[:, f, u * P:(u + 1) * P], late["w2_s"][:, f // K0, f % K0, :],
                                                    start=(f == 0), stop=(f == 2 * K0 - 1))
                        last.then_inc(s_y, 1)

                chunk(0, True)
                with pe.Fori(1, IT) as c:
                    chunk(c, False)

            @block.scalar
            def _(act):
                def chunk(c, first):
                    for i in range(NH):
                        f, h = divmod(i, 2)
                        e, b = divmod(f, K0)
                        act.wait_ge(s_h, c * NH + i + 1)
                        if not first:
                            act.wait_ge(s_y, c * U)
                        nc.scalar.activation(hT[:, f, h * HW:(h + 1) * HW], bank[i % 4][:, 0:HW], ACT.Gelu,
                                             bias=late["b1_s"][:, e, b:b + 1]).then_inc(s_g, 1)

                chunk(0, True)
                with act.Fori(1, IT) as c:
                    chunk(c, False)

            @block.vector
            def _(dve):
                STEPS = 28
                with dve.Fori(0, IT) as c:
                    link = Chain(dve, s_o, c * STEPS)
                    for u in range(U):
                        last = normalise(xn[:, u, :], x_all, c * U + u)
                    link(last)
                    link(nc.vector.tensor_tensor(xn[:, :, :], xn[:, :, :], late["b2c"][:, None, :].to_broadcast([P, U, D]),
                                                 ALU.add))
                    for u in range(U):
                        y = bank[4 + u % 4][:, 0:D]
                        dve.wait_ge(s_y, c * U + u + 1)
                        nc.vector.tensor_tensor(o[:, u, :], xn[:, u, :], y, ALU.add).then_inc(s_r, 1)
                    for u in range(U):
                        dve.wait_ge(s_r, c * U + u + 1)
                        last = nc.vector.bn_stats(st[:, u, :], o[:, u, :])
                    link(last)
                    join_stats(link, st, mv[:, :], va[:, :], tmp[:, :])
                    rsqrt(link, rs[:, :], va[:, :], tmp[:, :])
                    for u in range(U):
                        last = nc.vector.tensor_scalar(o[:, u, :], o[:, u, :], mv[:, u:u + 1], rs[:, u:u + 1],
                                                       ALU.subtract, ALU.mult)
                    link(last)
                    link(nc.vector.tensor_tensor(o[:, :, :], o[:, :, :], gamma_s[:, None, :].to_broadcast([P, U, D]),
                                                 ALU.mult))
                    link(nc.vector.tensor_tensor(o[:, :, :], o[:, :, :], beta_s[:, None, :].to_broadcast([P, U, D]),
                                                 ALU.add))
                    link(nc.vector.tensor_tensor(x_all[:, ds(c * U, U), :], x_all[:, ds(c * U, U), :], o[:, :, :],
                                                 ALU.add))
                    assert link.steps == STEPS

    @scratch
    def relational_table(own):
        s_xn, s_T, s_xT, s_mm = sem("p3_xn_ready"), sem("p3_transposed"), sem("p3_xT_ready"), sem("p3_product")
        s_ca, s_cv = sem("p3_copied_scalar"), sem("p3_copied_vector")
        s_out = [sem(f"p3_stored{s}") for s in range(RS)]
        xT = own("p3_xT", [P, U, KD, P])
        stage = own("p3_stage", [P, RS, SW])
        PAIRS = R // 2
        PS = PAIRS // RS
        NB = PS
        with nc.Block() as block:
            @block.gpsimd
            def _(pool):
                nc.gpsimd.memset(agg[:, :, :], 0.0)

            NA, NV = (PS + 1) // 2, PS // 2

            def copies(eng, copy, it, u, done, count, parity):
                w = it * U + u
                for s in range(RS):
                    q = w * RS + s
                    if not (isinstance(it, int) and it == 0 and u == 0):
                        eng.wait_ge(s_out[s], 16 * w)
                    for i in range(parity, PS, 2):
                        eng.wait_ge(s_mm, q * PS + i + 1)
                        copy(stage[:, s, i * 512:(i + 1) * 512], bank[3 + i][:, :]).then_inc(done, 1)

            @block.vector
            def _(dve):
                row_stats(dve, "p3")

                def one_pass(it, first):
                    for u in range(U):
                        if not first:
                            dve.wait_ge(s_T, it * U + u - U + 1)
                        normalise(xn[:, u, :], x_all, it * U + u).then_inc(s_xn, 1)
                    for u in range(U):
                        copies(dve, nc.vector.tensor_copy, it, u, s_cv, NV, 1)

                one_pass(0, True)
                with dve.Fori(1, IT) as it:
                    one_pass(it, False)

            @block.scalar
            def _(act):
                def one_pass(it, first):
                    for u in range(U):
                        w = it * U + u
                        act.wait_ge(s_T, w + 1)
                        if not first:
                            act.wait_ge(s_mm, (w - U + 1) * PAIRS)
                        nc.scalar.copy(xT[:, u, :, :].rearrange("p k n -> p (k n)"), tslot(u)).then_inc(s_xT, 1)
                        copies(act, nc.scalar.copy, it, u, s_ca, NA, 0)

                one_pass(0, True)
                with act.Fori(1, IT) as it:
                    one_pass(it, False)

            @block.tensor
            def _(pe):
                pe.wait_ge(s_wrel, 16 * KD)

                def one_pass(it, first):
                    for u in range(U):
                        w = it * U + u
                        pe.wait_ge(s_xn, w + 1)
                        if not first or u >= 2:
                            pe.wait_ge(s_xT, w - 1)
                        transposes(u).then_inc(s_T, 1)
                        pe.wait_ge(s_xT, w + 1)
                        for s in range(RS):
                            q = w * RS + s
                            for i in range(PS):
                                if not (first and u == 0 and s == 0):
                                    if i % 2 == 0:
                                        pe.wait_ge(s_ca, (q - 1) * NA + i // 2 + 1)
                                    else:
                                        pe.wait_ge(s_cv, (q - 1) * NV + i // 2 + 1)
                                r = 2 * (s * PS + i)
                                for k in range(KD):
                                    last = nc.tensor.matmul(
                                        bank[3 + i][:, :], xT[:, u, k, :],
                                        late["wrel_s"][:, k, r:r + 2, :].rearrange("p r d -> p (r d)"),
                                        start=(k == 0), stop=(k == KD - 1))
                                last.then_inc(s_mm, 1)

                one_pass(0, True)
                with pe.Fori(1, IT) as it:
                    one_pass(it, False)

            @block.sync
            def _(sp):
                def store(w, s, n):
                    by_scalar, by_vector = (w * RS + s + 1) * NA, (w * RS + s + 1) * NV
                    if not isinstance(w, int):
                        by_scalar, by_vector = sp.to_reg(by_scalar), sp.to_reg(by_vector)
                    sp.wait_ge(s_ca, by_scalar)
                    sp.wait_ge(s_cv, by_vector)
                    rows = rel_d[ds(w * P, n), s * SW:(s + 1) * SW]
                    sp.dma_start(rows, stage[0:n, s, :]).then_inc(s_out[s], 16)

                with sp.Fori(0, NT - 1) as w:
                    for s in range(RS):
                        store(w, s, P)
                for s in range(RS):
                    store(NT - 1, s, LAST)
                for s in range(RS):
                    sp.wait_ge(s_out[s], 16 * NT)

    def add_relu():
        with nc.Block() as block:
            @block.vector
            def _(dve):
                nc.vector.scalar_tensor_tensor(
                    out=x_all[:, :, :].rearrange("p t d -> p (t d)"), in0=agg_or_xT[:, :], scalar=0.0,
                    in1=x_all[:, :, :].rearrange("p t d -> p (t d)"), op0=ALU.max, op1=ALU.add)

    logit = sb("logit", [P, NT, NE])
    prob = sb("prob", [P, NT])
    pos_i = sb("pos_i", [P, NT], I32)
    expert_i = sb("expert_i", [1, ST], I32)

    HW1 = U * P // 2

    def hidden_products(pe, c, first, s_h, s_g, rhs, width, parts):
        n = K1 * parts
        for i in range(n):
            f, h = divmod(i, parts)
            if not first or i >= 4:
                pe.wait_ge(s_g, c * n + i - 3)
            for k in range(KD):
                last = nc.tensor.matmul(bank[i % 4][:, 0:width], late["v1_s"][:, k, f * P:(f + 1) * P], rhs(k, h),
                                        start=(k == 0), stop=(k == KD - 1))
            last.then_inc(s_h, 1)
        pe.wait_ge(s_g, (c + 1) * n)

    def choose_logits():
        s_h, s_g, s_l, s_c = sem("p4_hidden_product"), sem("p4_gelu_done"), sem("p4_logits"), sem("p4_logits_copied")
        NH = K1 * 2
        with nc.Block() as block:
            @block.tensor
            def _(pe):
                pe.wait_ge(s_v1, 16)

                def chunk(c, first):
                    hidden_products(pe, c, first, s_h, s_g,
                                    lambda k, h: xT_all[:, k, ds(c * (U * P) + h * HW1, HW1)], HW1, 2)
                    if not first:
                        pe.wait_ge(s_c, c)
                    for u in range(U):
                        for f in range(K1):
                            last = nc.tensor.matmul(bank[4][:, u * NE:(u + 1) * NE], hT[:, f, u * P:(u + 1) * P],
                                                    vg_s[:, f, :], start=(f == 0), stop=(f == K1 - 1))
                    last.then_inc(s_l, 1)

                chunk(0, True)
                with pe.Fori(1, IT) as c:
                    chunk(c, False)

            @block.scalar
            def _(act):
                def chunk(c, first):
                    for i in range(NH):
                        f, h = divmod(i, 2)
                        act.wait_ge(s_h, c * NH + i + 1)
                        if not first:
                            act.wait_ge(s_l, c)
                        nc.scalar.activation(hT[:, f, h * HW1:(h + 1) * HW1], bank[i % 4][:, 0:HW1], ACT.Gelu,
                                             bias=c1_s[:, f:f + 1]).then_inc(s_g, 1)

                chunk(0, True)
                with act.Fori(1, IT) as c:
                    chunk(c, False)

            @block.vector
            def _(dve):
                with dve.Fori(0, IT) as c:
                    dve.wait_ge(s_l, c + 1)
                    nc.vector.tensor_tensor(logit[:, ds(c * U, U), :],
                                            bank[4][:, 0:U * NE].rearrange("p (u e) -> p u e", u=U),
                                            cg_s[:, None, :].to_broadcast([P, U, NE]), ALU.add).then_inc(s_c, 1)

    @scratch
    def dispatch(own):
        sel = own("ds_sel", [P, NT, NE])
        work = own("ds_work", [P, NT, NE])
        run = [own(f"ds_run{i}", [P, NT, NE]) for i in range(2)]
        tot = own("ds_tot", [P, NT, NE])
        vec = own("ds_vec", [P, NT])
        cnt = own("ds_cnt", [P, NE, NT])
        nt = [own(f"ds_nt{i}", [P, NE]) for i in range(2)]
        base = own("ds_base", [P, NE])
        past = own("ds_past", [1, ST, NE])
        ex = own("ds_ex", [1, ST])
        s_step, s_max, s_exp = sem("ds_step"), sem("ds_exp_asked"), sem("ds_exp_done")
        s_sel, s_cum, s_pos = sem("ds_choice_ready"), sem("ds_counts"), sem("ds_rows_known")
        s_xn, s_put = sem("ds_xn_ready"), [sem(f"ds_scattered{u}") for u in range(U)]
        ALLE = [P, NT, NE]
        with nc.Block() as block:
            @block.vector
            def _(dve):
                link = Chain(dve, s_step)
                link(nc.vector.tensor_reduce(vec[:, :], logit[:, :, :], AX.X, ALU.max))
                nc.vector.tensor_tensor(work[:, :, :], logit[:, :, :], vec[:, :, None].to_broadcast(ALLE),
                                        ALU.subtract).then_inc(s_max, 1)
                dve.wait_ge(s_exp, 1)
                link(nc.vector.tensor_reduce(vec[:, :], sel[:, :, :], AX.X, ALU.add))
                link(nc.vector.reciprocal(vec[:, :], vec[:, :]))
                link(nc.vector.tensor_tensor(work[:, :, :], sel[:, :, :], vec[:, :, None].to_broadcast(ALLE), ALU.mult))
                link(nc.vector.tensor_reduce(prob[:, :], work[:, :, :], AX.X, ALU.max))
                link(nc.vector.tensor_tensor(work[:, :, :], work[:, :, :], prob[:, :, None].to_broadcast(ALLE),
                                             ALU.is_equal))
                link(nc.vector.scalar_tensor_tensor(
                    out=work[:, :, :], in0=work[:, :, :], scalar=-float(NE),
                    in1=iota_row[:, None, 0:NE].to_broadcast(ALLE), op0=ALU.mult, op1=ALU.add))
                link(nc.vector.tensor_reduce(vec[:, :], work[:, :, :], AX.X, ALU.min))
                link(nc.vector.tensor_tensor(sel[:, :, :], work[:, :, :], vec[:, :, None].to_broadcast(ALLE),
                                             ALU.is_equal))
                nc.vector.tensor_scalar(sel[:, NT - 1, :], sel[:, NT - 1, :], valid[:, 0:1], None, ALU.mult)\
                    .then_inc(s_sel, 1)
                dve.wait_ge(s_cum, 1)
                flat = [P, NT * NE]
                link(nc.vector.tensor_copy(tot[:, :, :].rearrange("p t e -> p (t e)"), bank[1][:, 0:NT * NE]))
                link(nc.vector.tensor_copy(run[0][:, :, :], tot[:, :, :]))
                a, step = 0, 1
                while step < NT:
                    link(nc.vector.tensor_copy(run[1 - a][:, 0:step, :], run[a][:, 0:step, :]))
                    link(nc.vector.tensor_tensor(run[1 - a][:, step:NT, :], run[a][:, step:NT, :],
                                                 run[a][:, 0:NT - step, :], ALU.add))
                    a, step = 1 - a, step * 2
                inc = run[a]
                link(nc.vector.tensor_tensor(cnt[:, :, :], inc[:, NT - 1, :, None].to_broadcast([P, NE, NT]),
                                             tile_base[:, None, :].to_broadcast([P, NE, NT]), ALU.is_gt))
                link(nc.vector.tensor_reduce(base[:, :], cnt[:, :, :], AX.X, ALU.add))
                link(nc.vector.tensor_copy(nt[0][:, :], base[:, :]))
                b, step = 0, 1
                while step < NE:
                    link(nc.vector.tensor_copy(nt[1 - b][:, 0:step], nt[b][:, 0:step]))
                    link(nc.vector.tensor_tensor(nt[1 - b][:, step:NE], nt[b][:, step:NE], nt[b][:, 0:NE - step],
                                                 ALU.add))
                    b, step = 1 - b, step * 2
                upto = nt[b]
                link(nc.vector.tensor_tensor(base[:, :], upto[:, :], base[:, :], ALU.subtract))
                link(nc.vector.tensor_scalar(base[:, :], base[:, :], float(P), None, ALU.mult))
                link(nc.vector.tensor_tensor(work[:, :, :], inc[:, :, :], tot[:, :, :], ALU.subtract))
                link(nc.vector.tensor_tensor(work[:, :, :], work[:, :, :],
                                             bank[0][:, 0:NT * NE].rearrange("p (t e) -> p t e", t=NT), ALU.add))
                link(nc.vector.tensor_tensor(work[:, :, :], work[:, :, :], base[:, None, :].to_broadcast(ALLE), ALU.add))
                link(nc.vector.tensor_tensor(work[:, :, :], work[:, :, :], sel[:, :, :], ALU.mult))
                link(nc.vector.tensor_reduce(vec[:, :], work[:, :, :], AX.X, ALU.add))
                nc.vector.tensor_copy(pos_i[:, :], vec[:, :]).then_inc(s_pos, 1)
                link(nc.vector.tensor_tensor(past[:, :, :], iota_row[0:1, 0:ST, None].to_broadcast([1, ST, NE]),
                                             upto[0:1, None, :].to_broadcast([1, ST, NE]), ALU.is_ge))
                link(nc.vector.tensor_reduce(ex[:, :], past[:, :, :], AX.X, ALU.add))
                nc.vector.tensor_scalar(expert_i[:, :], ex[:, :], NE - 1.0, None, ALU.min)
                for w in range(NT):
                    u = w % U
                    if w >= U:
                        dve.wait_ge(s_put[u], 16 * (w // U))
                    nc.vector.tensor_scalar(xn[:, u, :], x_all[:, w, :], mean[:, w:w + 1], rstd[:, w:w + 1],
                                            ALU.subtract, ALU.mult).then_inc(s_xn, 1)

            @block.scalar
            def _(act):
                act.wait_ge(s_max, 1)
                nc.scalar.activation(sel[:, :, :], work[:, :, :], ACT.Exp).then_inc(s_exp, 1)

            @block.tensor
            def _(pe):
                pe.wait_ge(s_sel, 1)
                rows = sel[:, :, :].rearrange("p t e -> p (t e)")
                nc.tensor.matmul(bank[0][:, 0:NT * NE], before[:, :], rows, start=True, stop=True)
                nc.tensor.matmul(bank[1][:, 0:NT * NE], ones[:, :], rows, start=True, stop=True).then_inc(s_cum, 1)

            @block.gpsimd
            def _(pool):
                pool.wait_ge(s_pos, 1)
                pool.wait_ge(s_zero, 16 * ZERO_DMAS)
                for w in range(NT):
                    n = P if w < NT - 1 else LAST
                    pool.wait_ge(s_xn, w + 1)
                    nc.gpsimd.indirect_dma_start(
                        out=sorted_d, out_offset=bass.IndirectOffsetOnAxis(ap=pos_i[0:n, w:w + 1], axis=0),
                        in_=xn[0:n, w % U, :], in_offset=None).then_inc(s_put[w % U], 16)
                for u in range(U):
                    pool.wait_ge(s_put[u], 16 * IT)

    def sorted_experts():
        CD = SC * D
        xs = agg_or_xT[:, 0:2 * CD].rearrange("p (i u d) -> p i u d", i=2, u=SC)
        xsT = agg_or_xT[:, 2 * CD:3 * CD].rearrange("p (k n) -> p k n", k=KD)
        yo = agg_or_xT[:, 3 * CD:4 * CD].rearrange("p (u d) -> p u d", u=SC)
        W = SC * P
        CN = ST // SC
        s_in, s_T, s_xT = [sem(f"se_rows_loaded{i}") for i in range(2)], sem("se_transposed"), sem("se_xT_ready")
        s_h, s_g, s_y = sem("se_hidden_product"), sem("se_gelu_done"), sem("se_output_product")
        s_r, s_st = sem("se_rows_ready"), sem("se_stored")
        rows_in = sorted_d.rearrange("(c u p) d -> c p u d", p=P, u=SC)
        rows_out = y_d.rearrange("(c u p) d -> c p u d", p=P, u=SC)
        with nc.Block() as block:
            @block.sync
            def _(sp):
                for i in range(2):
                    sp.dma_start(xs[:, i, :, :], rows_in[i]).then_inc(s_in[i], 16)
                with sp.Fori(1, CN // 2) as it:
                    for i in range(2):
                        c = it * 2 + i
                        sp.wait_ge(s_T, (c - 1) * SC)
                        sp.dma_start(xs[:, i, :, :], rows_in[ds(c, 1)].rearrange("a p u d -> p (a u) d"))\
                            .then_inc(s_in[i], 16)

            @block.tensor
            def _(pe):
                pe.wait_ge(s_v1, 16)
                pe.wait_ge(s_wd, 16 * NE)

                def chunk(c, i, first):
                    pe.wait_ge(s_in[i], 16 * (c // 2 + 1) if isinstance(c, int) else 16 * (c - i) // 2 + 16)
                    for u in range(SC):
                        if not first or u >= 2:
                            pe.wait_ge(s_xT, c * SC + u - 1)
                        for k in range(KD):
                            last = nc.tensor.transpose(bank[6 + u % 2][:, k * P:(k + 1) * P],
                                                       xs[:, i, u, k * P:(k + 1) * P], ident[:, :])
                        last.then_inc(s_T, 1)
                    pe.wait_ge(s_xT, (c + 1) * SC)
                    hidden_products(pe, c, first, s_h, s_g, lambda k, h: xsT[:, k, :], W, 1)
                    for u in range(SC):
                        e = pe.value_load(expert_i[0:1, ds(c * SC + u, 1)], min_val=0, max_val=NE - 1)
                        if not first or u >= 2:
                            pe.wait_ge(s_r, c * SC + u - 1)
                        y = bank[4 + u % 2][:, 0:D]
                        for f in range(K1):
                            last = nc.tensor.matmul(y, hT[:, f, u * P:(u + 1) * P],
                                                    late["wd_s"][:, ds(e * (K1 * D) + f * D, D)],
                                                    start=(f == 0), stop=(f == K1 - 1))
                        last.then_inc(s_y, 1)

                chunk(0, 0, True)
                chunk(1, 1, False)
                with pe.Fori(1, CN // 2) as it:
                    for i in range(2):
                        chunk(it * 2 + i, i, False)

            @block.scalar
            def _(act):
                def chunk(c, first):
                    for f in range(K1):
                        act.wait_ge(s_h, c * K1 + f + 1)
                        if not first:
                            act.wait_ge(s_y, c * SC)
                        nc.scalar.activation(hT[:, f, 0:W], bank[f % 4][:, 0:W], ACT.Gelu,
                                             bias=c1_s[:, f:f + 1]).then_inc(s_g, 1)

                chunk(0, True)
                with act.Fori(1, CN) as c:
                    chunk(c, False)

            @block.vector
            def _(dve):
                dve.wait_ge(s_bd, 16)

                def chunk(c, first):
                    for u in range(SC):
                        dve.wait_ge(s_T, c * SC + u + 1)
                        if not first:
                            dve.wait_ge(s_h, c * K1)
                        nc.vector.tensor_copy(
                            xsT[:, :, u * P:(u + 1) * P],
                            bank[6 + u % 2][:, 0:D].rearrange("p (k n) -> p k n", k=KD))\
                            .then_inc(s_xT, 1)
                    for u in range(SC):
                        e = dve.value_load(expert_i[0:1, ds(c * SC + u, 1)], min_val=0, max_val=NE - 1)
                        dve.wait_ge(s_y, c * SC + u + 1)
                        if not first:
                            dve.wait_ge(s_st, 16 * c)
                        y = bank[4 + u % 2][:, 0:D]
                        nc.vector.tensor_tensor(yo[:, u, :], late["bd_s"][:, ds(e, 1), :].rearrange("p a d -> p (a d)"), y,
                                                ALU.add).then_inc(s_r, 1)

                chunk(0, True)
                with dve.Fori(1, CN) as c:
                    chunk(c, False)

            @block.gpsimd
            def _(pool):
                with pool.Fori(0, CN) as c:
                    pool.wait_ge(s_r, (c + 1) * SC)
                    pool.dma_start(rows_out[ds(c, 1)].rearrange("a p u d -> p (a u) d"), yo[:, :, :])\
                        .then_inc(s_st, 16)
                pool.wait_ge(s_st, 16 * CN)

    def combine():
        s_got, s_add, s_out = [sem(f"cb_gathered{u}") for u in range(U)], sem("cb_added"), sem("cb_stored")
        with nc.Block() as block:
            @block.gpsimd
            def _(pool):
                for w in range(NT):
                    n = P if w < NT - 1 else LAST
                    if w >= U:
                        pool.wait_ge(s_add, w - U + 1)
                    nc.gpsimd.indirect_dma_start(
                        out=xn[0:n, w % U, :], out_offset=None, in_=y_d,
                        in_offset=bass.IndirectOffsetOnAxis(ap=pos_i[0:n, w:w + 1], axis=0)).then_inc(s_got[w % U], 16)

            @block.vector
            def _(dve):
                for w in range(NT):
                    n = P if w < NT - 1 else LAST
                    dve.wait_ge(s_got[w % U], 16 * (w // U + 1))
                    nc.vector.scalar_tensor_tensor(
                        out=x_all[0:n, w, :], in0=xn[0:n, w % U, :], scalar=prob[0:n, w:w + 1],
                        in1=x_all[0:n, w, :], op0=ALU.mult, op1=ALU.add).then_inc(s_add, 1)

            @block.sync
            def _(sp):
                for c in range(IT):
                    sp.wait_ge(s_add, (c + 1) * U)
                    if c < IT - 1:
                        sp.dma_start(out[c * U * P:(c + 1) * U * P, :].rearrange("(t p) d -> p t d", p=P),
                                     x_all[:, c * U:(c + 1) * U, :]).then_inc(s_out, 16)
                sp.dma_start(out[c * U * P:(NT - 1) * P, :].rearrange("(t p) d -> p t d", p=P),
                             x_all[:, c * U:NT - 1, :]).then_inc(s_out, 16)
                sp.dma_start(out[(NT - 1) * P:N, :], x_all[0:LAST, NT - 1, :]).then_inc(s_out, 16)
                sp.wait_ge(s_out, 16 * (IT + 1))

    valid = sb("valid", [P, 1])
    ZERO_DMAS = 4

    def prefetch():
        zeros = hT[:, 0:4, :].rearrange("p a b -> p (a b)")[:, 0:ST * D // ZERO_DMAS]
        s_z = sem("zeros_ready")
        with nc.Block() as block:
            @block.vector
            def _(dve):
                nc.vector.memset(zeros, 0.0).then_inc(s_z, 1)
                nc.vector.tensor_scalar(valid[:, :], before[:, LAST:LAST + 1], 1.0, None, ALU.mult)

            @block.scalar
            def _(act):
                act.wait_ge(s_z, 1)
                rows = sorted_d.rearrange("(p r) d -> p (r d)", p=P)
                n = ST * D // ZERO_DMAS
                for i in range(ZERO_DMAS):
                    act.dma_start(rows[:, i * n:(i + 1) * n], zeros).then_inc(s_zero, 16)
                act.wait_ge(s_zero, 16 * ZERO_DMAS)

    memory = ExitStack()
    late = {}

    def allocate(*buffers):
        def run():
            for name, shape in buffers:
                late[name] = memory.enter_context(nc.sbuf_tensor(name, shape, F32))
        return run

    def load_relation_weights(sp):
        for k in range(KD):
            sp.dma_start(late["wrel_s"][:, k, :, :], wrel[:, k * P:(k + 1) * P, :].rearrange("r p d -> p r d"))\
                .then_inc(s_wrel, 16)

    def load_expert_weights(sp):
        sp.dma_start(late["v1_s"][:, :, :], v1.rearrange("(k p) n -> p k n", p=P)).then_inc(s_v1, 16)
        sp.dma_start(late["bd_s"][:, :, :], bd.partition_broadcast(P)).then_inc(s_bd, 16)
        for e in range(NE):
            sp.dma_start(late["wd_s"][:, e * K1 * D:(e + 1) * K1 * D].rearrange("p (k d) -> p k d", k=K1),
                         wd[e, :, :].rearrange("(k p) d -> p k d", p=P)).then_inc(s_wd, 16)

    parts = [
        load_and_constants, edges, prefetch, support,
        allocate(("wrel_s", [P, KD, R, D])),
        lambda: segment_sum("sum1", support_d, src_i, False, x_all, load_relation_weights),
        allocate(("w1_s", [P, 2, KD, F0]), ("w2_s", [P, 2, K0, D]), ("b1_s", [P, 2, K0]), ("b2c", [P, D])),
        lambda: transposed_norm("ln2"), routing, top2_ffn,
        relational_table,
        memory.close,
        allocate(("wd_s", [P, NE * K1 * D]), ("v1_s", [P, KD, F1]), ("bd_s", [P, NE, D])),
        lambda: segment_sum("sum3", rel_rows, srcrel_i, True, agg, load_expert_weights),
        add_relu,
        lambda: transposed_norm("ln4"), choose_logits, dispatch, sorted_experts, combine,
    ]
    with ctx, memory:
        for part in parts:
            part()


INS = ["x", "src", "dst", "edge_type_20", "edge_weight1", "L0_gnn_weight", "L0_gnn_bias", "L0_ffn_Wr", "L0_ffn_br",
       "L0_ffn_W1", "L0_ffn_b1", "L0_ffn_W2", "L0_ffn_b2", "L0_ffn_gamma", "L0_ffn_beta", "L1_gnn_weight",
       "L1_ffn_W1", "L1_ffn_b1", "L1_ffn_Wg", "L1_ffn_bg", "L1_ffn_Wd", "L1_ffn_bd"]


def kernel(**inputs):
    import numpy as np
    import concourse.bacc as bacc
    from concourse.bass_utils import run_bass_kernel_spmd

    nc = bacc.Bacc("TRN2", target_bir_lowering=False, num_devices=1)
    arrays, args = {}, []
    for name in INS:
        a = np.ascontiguousarray(inputs[name])
        arrays[f"in_{name}"] = a
        args.append(nc.dram_tensor(f"in_{name}", a.shape, mybir.dt.from_np(a.dtype), kind="ExternalInput").ap())
    out = nc.dram_tensor("out", (N, D), F32, kind="ExternalOutput").ap()
    build(nc, *args, out)
    r = run_bass_kernel_spmd(nc, [arrays], core_ids=[0])
    return r.results[0]["out"]
```

```python
from contextlib import ExitStack

import concourse.bass as bass
from concourse import mybir

F32 = mybir.dt.float32
F32R = mybir.dt.float32r
I32 = mybir.dt.int32
ALU = mybir.AluOpType
ACT = mybir.ActivationFunctionType
AX = mybir.AxisListType

P = 128
N = 3125
D = 256
KD = D // P
NT = -(-N // P)
LAST = N - (NT - 1) * P
U = 5
IT = NT // U
NP = NT * P
E = 53125
CH = 4
GE = CH * P
NG = -(-E // GE)
ELAST = E - (NG - 1) * GE
RING = 4
R = 20
RP = R // 2
NE = 8
F0, F1 = 512, 1024
K0, K1 = F0 // P, F1 // P
ST = (N - NE) // P + NE
SC = 4
EPS = 1e-5
CAP = float(-(-N * 5 // (4 * NE)))
assert NT == U * IT and NG % RING == 0 and ST % (2 * SC) == 0


def build(nc, x, src, dst, rel, ew, wg, bias, wr, br, w1, b1, w2, b2, gamma, beta,
          wrel, v1, c1, vg, cg, wd, bd, out):
    ctx = ExitStack()

    def sb(name, shape, dt=F32):
        return ctx.enter_context(nc.sbuf_tensor(name, shape, dt))

    def sem(name):
        return ctx.enter_context(nc.semaphore(name))

    def ds(i, n):
        return bass.ds(i, n)

    def scratch(part):
        def run():
            with ExitStack() as own:
                part(lambda name, shape, dt=F32: own.enter_context(nc.sbuf_tensor(name, shape, dt)))
        return run

    support_d = nc.dram_tensor("support_d", (N, D), F32).ap()
    rel_d = nc.dram_tensor("rel_d", (N, R * D), F32).ap()
    rel_rows = rel_d.rearrange("n (r d) -> (n r) d", r=R)
    sorted_d = nc.dram_tensor("sorted_d", (ST * P, D + 1), F32).ap()
    y_d = nc.dram_tensor("y_d", (NP + ST * P, D), F32).ap()

    x_all = sb("x_all", [P, NT, D])
    hT = sb("hT", [P, K1, U * P])
    shared = hT[:, :, :].rearrange("p a b -> p (a b)")
    ring = shared[:, 0:RING * CH * D].rearrange("p (s j d) -> p s j d", s=RING, j=CH)
    xn = sb("xn", [P, U, D])
    ident = sb("ident", [P, P])
    valid = sb("valid", [P, NT])
    ones = sb("ones", [P, P])
    before = sb("before", [P, P])
    number = sb("number", [P, 1])
    iota_row = sb("iota_row", [P, P])
    tile_base = sb("tile_base", [P, NT])
    iota_i = sb("iota_i", [P, P], I32)
    base_i = sb("base_i", [P, NT], I32)
    stat = sb("stat", [P, NT, 6])
    mean = sb("mean", [P, NT])
    vsum = sb("vsum", [P, NT])
    dev = sb("dev", [P, NT])
    rstd = sb("rstd", [P, NT])
    wg_s = sb("wg_s", [P, KD, D])
    c1_s = sb("c1_s", [P, K1])
    vg_s = sb("vg_s", [P, K1, NE])
    cg_s = sb("cg_s", [P, NE])
    wr_s = sb("wr_s", [P, KD, NE])
    br_s = sb("br_s", [1, NE])
    b2_s = sb("b2_s", [NE, D])
    bias_s = sb("bias_s", [P, D])
    gamma_s = sb("gamma_s", [P, D])
    beta_s = sb("beta_s", [P, D])
    src_i = sb("src_i", [P, CH, NG], I32)
    srcrel_i = sb("srcrel_i", [P, CH, NG], I32)
    dst_f = sb("dst_f", [P, CH, NG])
    dst_rel = sb("dst_rel", [P, CH, NG + 1])
    ew_f = sb("ew_f", [P, CH, NG])
    idx_slot = sb("idx_slot", [P, RING, CH], I32)
    spans = sb("spans", [1, 3, NG + 1], I32)
    bank = [ctx.enter_context(nc.psum_tensor(f"bank{i}", [P, 512], F32)) for i in range(8)]

    def tslot(u):
        return bank[u][:, 0:D]

    s_wd, s_v1, s_bd = sem("wd_loaded"), sem("v1_loaded"), sem("bd_loaded")
    s_empty = sem("sorted_d_emptied")

    s_pool_turn, s_dve_turn = sem("gpsimd_turn"), sem("vector_turn")

    late = {}

    class Chain:

        def __init__(self, eng, s, start=0):
            self.eng, self.s, self.start, self.steps = eng, s, start, 0

        def __call__(self, ins):
            ins.then_inc(self.s, 1)
            self.steps += 1
            self.eng.wait_ge(self.s, self.start + self.steps)

    def rsqrt(link, y, v, t):
        link(nc.vector.tensor_scalar(t.bitcast(I32), v.bitcast(I32), 1, None, ALU.logical_shift_right))
        link(nc.vector.tensor_scalar(y.bitcast(I32), t.bitcast(I32), -1.0, float(0x5F3759DF), ALU.mult, ALU.add))
        link(nc.vector.tensor_scalar(v, v, -0.5, None, ALU.mult))
        for _ in range(3):
            link(nc.vector.tensor_tensor(t, y, y, ALU.mult))
            link(nc.vector.tensor_tensor(t, t, v, ALU.mult))
            link(nc.vector.scalar_tensor_tensor(out=y, in0=t, scalar=1.5, in1=y, op0=ALU.add, op1=ALU.mult))

    s_x, s_wg, s_small = sem("x_loaded"), sem("wg_and_bias_loaded"), sem("small_loaded")

    @scratch
    def load_and_edges(own):
        raw = own("raw", [P, 3, GE], I32)
        ef = own("ef", [P, 4, GE])
        SRC, SRCREL, DST, EW = range(4)
        row_i, number_i = own("row_i", [P, ST], I32), own("number_i", [P, 1], I32)
        lim = own("lim", [P, 2])
        cmpr = own("cmpr", [P, 2, NT - 1])
        tiles = own("tiles", [P, 3])
        first_row = own("first_row", [1, NG])
        s_const, s_ci = sem("const_step"), sem("iota_written")
        s_z = sem("zeros_written")
        s_cf, s_xpad = sem("iota_as_float"), sem("x_padding_zeroed")
        s_pad, s_in, s_step = sem("edge_padding"), sem("edges_loaded"), sem("edge_step")
        s_f, s_t, s_tab, s_ev = sem("edge_rows_ready"), sem("edges_transposed"), sem("spans_summed"), sem("edge_copies")
        with nc.Block() as block:
            @block.gpsimd
            def _(pool):
                nc.gpsimd.memset(ident[:, :], 0.0).then_inc(s_const, 1)
                nc.gpsimd.memset(before[:, :], 1.0).then_inc(s_const, 1)
                nc.gpsimd.memset(ones[:, :], 1.0).then_inc(s_const, 1)
                nc.gpsimd.iota(iota_i[:, :], pattern=[[1, P]], base=0, channel_multiplier=0).then_inc(s_ci, 1)
                nc.gpsimd.iota(base_i[:, :], pattern=[[P, NT]], base=0, channel_multiplier=0).then_inc(s_ci, 1)
                nc.gpsimd.iota(number_i[:, :], pattern=[[1, 1]], base=0, channel_multiplier=1).then_inc(s_ci, 1)
                pool.wait_ge(s_const, 3)
                nc.gpsimd.affine_select(out=ident[:, :], in_=ident[:, :], compare_op=ALU.not_equal, fill=1.0,
                                        base=0, pattern=[[-1, P]], channel_multiplier=1).then_inc(s_const, 1)
                nc.gpsimd.affine_select(out=before[:, :], in_=before[:, :], compare_op=ALU.is_gt, fill=0.0,
                                        base=0, pattern=[[1, P]], channel_multiplier=-1).then_inc(s_const, 1)
                pool.wait_ge(s_const, 5)
                nc.gpsimd.tensor_copy(valid[:, NT - 1:NT], before[:, LAST:LAST + 1])
                nc.gpsimd.memset(valid[:, 0:NT - 1], 1.0)
                nc.gpsimd.memset(late["zeros"][:, :], 0.0).then_inc(s_z, 1)
                nc.gpsimd.iota(row_i[:, :], pattern=[[1, ST]], base=0, channel_multiplier=ST).then_inc(s_z, 1)

            @block.sync
            def _(sp):
                sp.wait_ge(s_pad, 4)
                for a, v in ((0, src), (1, rel), (2, dst)):
                    sp.dma_start(raw[0:NG - 1, a, :], v[0:(NG - 1) * GE].rearrange("(g e) -> g e", e=GE))\
                        .then_inc(s_in, 16)
                    sp.dma_start(raw[NG - 1:NG, a, 0:ELAST], v[(NG - 1) * GE:E].rearrange("(g e) -> g e", g=1))\
                        .then_inc(s_in, 16)
                sp.dma_start(ef[0:NG - 1, EW, :], ew[0:(NG - 1) * GE, :].rearrange("(g e) a -> g (e a)", e=GE))\
                    .then_inc(s_in, 16)
                sp.dma_start(ef[NG - 1:NG, EW, 0:ELAST], ew[(NG - 1) * GE:E, :].rearrange("(g e) a -> g (e a)", g=1))\
                    .then_inc(s_in, 16)
                sp.dma_start(wg_s[:, :, :], wg.rearrange("(k p) n -> p k n", p=P)).then_inc(s_wg, 16)
                sp.dma_start(bias_s[:, :], bias.partition_broadcast(P)).then_inc(s_wg, 16)
                sp.wait_ge(s_xpad, 1)
                sp.dma_start(x_all[:, 0:NT - 1, :], x[0:(NT - 1) * P, :].rearrange("(t p) d -> p t d", p=P))\
                    .then_inc(s_x, 16)
                sp.dma_start(x_all[0:LAST, NT - 1, :], x[(NT - 1) * P:N, :]).then_inc(s_x, 16)
                sp.dma_start(vg_s[:, :, :], vg.rearrange("(k p) n -> p k n", p=P)).then_inc(s_small, 16)
                sp.dma_start(wr_s[:, :, :], wr.rearrange("(k p) n -> p k n", p=P)).then_inc(s_small, 16)
                sp.dma_start(br_s[:, :], br.rearrange("(a n) -> a n", a=1)).then_inc(s_small, 16)
                sp.dma_start(b2_s[:, :], b2).then_inc(s_small, 16)
                sp.dma_start(c1_s[:, :], c1.rearrange("(k p) -> p k", p=P),
                             allow_slow_non_contiguous=True).then_inc(s_small, 16)
                for tile, vec in ((gamma_s, gamma), (beta_s, beta), (cg_s, cg)):
                    sp.dma_start(tile[:, :], vec.partition_broadcast(P)).then_inc(s_small, 16)

            @block.vector
            def _(dve):
                tail = (slice((NG - 1) // 32 * 32, NG), slice(ELAST, GE))
                for a in range(2):
                    nc.vector.memset(raw[tail[0], a, tail[1]], 0).then_inc(s_pad, 1)
                nc.vector.memset(raw[tail[0], 2, tail[1]], NP - 1).then_inc(s_pad, 1)
                nc.vector.memset(ef[tail[0], EW, tail[1]], 0.0).then_inc(s_pad, 1)
                nc.vector.memset(x_all[:, NT - 1, :], 0.0).then_inc(s_xpad, 1)
                dve.wait_ge(s_ci, 3)
                nc.vector.tensor_copy(iota_row[:, :], iota_i[:, :])
                nc.vector.tensor_copy(tile_base[:, :], base_i[:, :]).then_inc(s_cf, 1)
                link = Chain(dve, s_step)
                dve.wait_ge(s_cf, 1)
                dve.wait_ge(s_in, 128)
                link(nc.vector.tensor_copy(ef[0:NG, SRC, :], raw[0:NG, 0, :]))
                link(nc.vector.tensor_copy(ef[0:NG, SRCREL, :], raw[0:NG, 1, :]))
                link(nc.vector.tensor_copy(ef[0:NG, DST, :], raw[0:NG, 2, :]))
                nc.vector.scalar_tensor_tensor(out=ef[0:NG, SRCREL, :], in0=ef[0:NG, SRC, :], scalar=float(R),
                                               in1=ef[0:NG, SRCREL, :], op0=ALU.mult, op1=ALU.add).then_inc(s_f, 1)
                link(nc.vector.tensor_reduce(lim[0:NG, 0:1], ef[0:NG, DST, :], AX.X, ALU.min))
                link(nc.vector.tensor_reduce(lim[0:NG, 1:2], ef[0:NG, DST, :], AX.X, ALU.max))
                for m in range(2):
                    link(nc.vector.tensor_scalar(cmpr[0:NG, m, :], tile_base[0:NG, 1:NT], lim[0:NG, m:m + 1], None,
                                                 ALU.is_le))
                link(nc.vector.tensor_reduce(tiles[0:NG, 0:2], cmpr[0:NG, :, :], AX.X, ALU.add))
                nc.vector.tensor_tensor(tiles[0:NG, 2:3], tiles[0:NG, 1:2], tiles[0:NG, 0:1], ALU.subtract)\
                    .then_inc(s_f, 1)
                dve.wait_ge(s_t, 4)
                nc.vector.tensor_copy(src_i[:, :, :].rearrange("p j g -> p (j g)"), bank[SRC][:, 0:CH * NG])
                nc.vector.tensor_copy(srcrel_i[:, :, :].rearrange("p j g -> p (j g)"), bank[SRCREL][:, 0:CH * NG])
                nc.vector.tensor_copy(dst_f[:, :, :].rearrange("p j g -> p (j g)"), bank[DST][:, 0:CH * NG])\
                    .then_inc(s_ev, 1)
                nc.vector.memset(dst_rel[:, :, NG:NG + 1], 0.0)
                nc.vector.tensor_copy(ew_f[:, :, :].rearrange("p j g -> p (j g)"), bank[EW][:, 0:CH * NG])
                dve.wait_ge(s_tab, 1)
                nc.vector.tensor_copy(spans[:, :, 0:NG], bank[4][0:1, 0:3 * NG].rearrange("a (k g) -> a k g", k=3))
                nc.vector.memset(spans[:, :, NG:NG + 1], 0)
                nc.vector.tensor_scalar(first_row[:, :], bank[4][0:1, NG:2 * NG], -float(P), None, ALU.mult)\
                    .then_inc(s_ev, 1)
                dve.wait_ge(s_tab, 2)
                dve.wait_ge(s_ev, 2)
                nc.vector.tensor_tensor(dst_rel[:, :, 0:NG], dst_f[:, :, :],
                                        bank[5][:, None, 0:NG].to_broadcast([P, CH, NG]), ALU.add)
                nc.vector.tensor_copy(number[:, :], number_i[:, :])
                dve.wait_ge(s_z, 2)
                nc.vector.tensor_scalar(late["zeros"][:, :].rearrange("p (r d) -> p r d", r=ST)[:, :, D], row_i[:, :],
                                        float(NP), None, ALU.add)

            @block.tensor
            def _(pe):
                pe.wait_ge(s_const, 5)
                pe.wait_ge(s_f, 1)
                for a in range(4):
                    for j in range(CH):
                        last = nc.tensor.transpose(bank[a][:, j * NG:(j + 1) * NG], ef[0:NG, a, j * P:(j + 1) * P],
                                                   ident[0:NG, 0:NG])
                    last.then_inc(s_t, 1)
                pe.wait_ge(s_f, 2)
                nc.tensor.matmul(bank[4][0:1, 0:NG], tiles[0:NG, 2:3], before[0:NG, 0:NG], start=True, stop=True)
                nc.tensor.matmul(bank[4][0:1, NG:2 * NG], tiles[0:NG, 0:1], ident[0:NG, 0:NG], start=True, stop=True)
                nc.tensor.matmul(bank[4][0:1, 2 * NG:3 * NG], tiles[0:NG, 2:3], ident[0:NG, 0:NG],
                                 start=True, stop=True).then_inc(s_tab, 1)
                pe.wait_ge(s_ev, 2)
                nc.tensor.matmul(bank[5][:, 0:NG], ones[0:1, :], first_row[:, :], start=True, stop=True)\
                    .then_inc(s_tab, 1)

    def join_stats(link, st, m, v, t):
        link(nc.vector.tensor_tensor(m, st[:, :, 1], st[:, :, 4], ALU.add))
        link(nc.vector.tensor_tensor(t, st[:, :, 1], st[:, :, 4], ALU.subtract))
        link(nc.vector.tensor_scalar(m, m, 0.5, None, ALU.mult))
        link(nc.vector.tensor_tensor(t, t, t, ALU.mult))
        link(nc.vector.tensor_tensor(v, st[:, :, 2], st[:, :, 5], ALU.add))
        link(nc.vector.scalar_tensor_tensor(out=v, in0=t, scalar=D / 4.0, in1=v, op0=ALU.mult, op1=ALU.add))
        link(nc.vector.tensor_scalar(v, v, 1.0 / D, EPS, ALU.mult, ALU.add))

    def chunk_stats(dve, link, c, st, mv, rs, va, tmp):
        dve.sem_inc(s_dve_turn, 1)
        for u in range(U):
            last = nc.vector.bn_stats(st[:, u, :], x_all[:, ds(c * U + u, 1), :].rearrange("p a d -> p (a d)"))
        link(last)
        join_stats(link, st, mv[:, :], va[:, :], tmp[:, :])
        rsqrt(link, rs[:, :], va[:, :], tmp[:, :])
        nc.vector.tensor_tensor(rs[:, :], rs[:, :], valid[:, ds(c * U, U)], ALU.mult)
        link(nc.vector.tensor_copy(mean[:, ds(c * U, U)], mv[:, :]))
        nc.vector.tensor_scalar(rstd[:, ds(c * U, U)], rs[:, :], 1.0, None, ALU.mult)

    def row_stats(dve, tag):
        s_bn, s_st = sem(f"{tag}_bn_stats"), sem(f"{tag}_stat_step")
        with dve.Fori(0, IT) as it:
            for u in range(U):
                w = it * U + u
                nc.vector.bn_stats(stat[:, ds(w, 1), :].rearrange("p a s -> p (a s)"),
                                   x_all[:, ds(w, 1), :].rearrange("p a d -> p (a d)")).then_inc(s_bn, 1)
        dve.wait_ge(s_bn, NT)
        link = Chain(dve, s_st)
        join_stats(link, stat, mean[:, :], vsum[:, :], dev[:, :])
        rsqrt(link, rstd[:, :], vsum[:, :], dev[:, :])
        link(nc.vector.tensor_tensor(rstd[:, NT - 1:NT], rstd[:, NT - 1:NT], valid[:, NT - 1:NT], ALU.mult))

    def normalise(to, of, w):
        return nc.vector.tensor_scalar(to, of[:, ds(w, 1), :].rearrange("p a d -> p (a d)"), mean[:, ds(w, 1)],
                                       rstd[:, ds(w, 1)], ALU.subtract, ALU.mult)

    def three_products(to, terms, before_term=None):
        for i, (ah, al, bh, bl) in enumerate(terms):
            if before_term:
                before_term(i)
            nc.tensor.matmul(to, ah, bh, start=(i == 0), stop=False)
            nc.tensor.matmul(to, ah, bl, start=False, stop=False)
            last = nc.tensor.matmul(to, al, bh, start=False, stop=(i == len(terms) - 1))
        return last

    def transposes(u, b=None):
        for k in range(KD):
            last = nc.tensor.transpose(tslot(u if b is None else b)[:, k * P:(k + 1) * P],
                                       xn[:, u, k * P:(k + 1) * P], ident[:, :])
        return last

    @scratch
    def support(own):
        s_xn, s_T, s_xT, s_mm = sem("p1_xn_ready"), sem("p1_transposed"), sem("p1_xT_ready"), sem("p1_product")
        s_row, s_out = sem("p1_rows_ready"), [sem(f"p1_rows_stored{u}") for u in range(U)]
        rows = shared[:, 0:U * D].rearrange("p (u d) -> p u d", u=U)
        xT = own("p1_xT", [P, U, KD, P])
        with nc.Block() as block:
            @block.vector
            def _(dve):
                dve.wait_ge(s_x, 32)
                row_stats(dve, "p1")

                def one_pass(it, first):
                    for u in range(U):
                        w = it * U + u
                        if not first:
                            dve.wait_ge(s_T, w - U + 1)
                        normalise(xn[:, u, :], x_all, w).then_inc(s_xn, 1)

                one_pass(0, True)
                with dve.Fori(1, IT) as it:
                    one_pass(it, False)

            @block.gpsimd
            def _(pool):
                pool.wait_ge(s_wg, 32)
                with pool.Fori(0, IT) as it:
                    for u in range(U):
                        w = it * U + u
                        pool.wait_ge(s_xn, w + 1)
                        nc.gpsimd.tensor_tensor(x_all[:, ds(w, 1), :], x_all[:, ds(w, 1), :],
                                                bias_s[:, None, :], ALU.add)

            @block.tensor
            def _(pe):
                def transpose_tile(it, u, first):
                    w = it * U + u
                    pe.wait_ge(s_xn, w + 1)
                    if not first or u >= 3:
                        pe.wait_ge(s_xT, w - (2 if u >= 2 else 1))
                    transposes(u, u % 3).then_inc(s_T, 1)

                def product(w, u, first):
                    pe.wait_ge(s_xT, w + 1)
                    if not first:
                        pe.wait_ge(s_row, w - U + 1)
                    for k in range(KD):
                        last = nc.tensor.matmul(bank[3 + u][:, 0:D], xT[:, u, k, :], wg_s[:, k, :],
                                                start=(k == 0), stop=(k == KD - 1))
                    last.then_inc(s_mm, 1)

                pe.wait_ge(s_wg, 32)
                transpose_tile(0, 0, True)
                for u in range(1, U):
                    transpose_tile(0, u, True)
                    product(u - 1, u - 1, True)
                transpose_tile(1, 0, False)
                product(U - 1, U - 1, True)
                with pe.Fori(1, IT - 1) as it:
                    for u in range(1, U):
                        transpose_tile(it, u, False)
                        product(it * U + u - 1, u - 1, False)
                    transpose_tile(it + 1, 0, False)
                    product(it * U + U - 1, U - 1, False)
                for u in range(1, U):
                    transpose_tile(IT - 1, u, False)
                    product((IT - 1) * U + u - 1, u - 1, False)
                product(NT - 1, U - 1, False)

            @block.scalar
            def _(act):
                def copy_xT(it, u, first):
                    w = it * U + u
                    act.wait_ge(s_T, w + 1)
                    if not first:
                        act.wait_ge(s_mm, w - U + 1)
                    nc.scalar.copy(xT[:, u, :, :].rearrange("p k n -> p (k n)"), tslot(u % 3)).then_inc(s_xT, 1)

                def copy_rows(it, u, first):
                    act.wait_ge(s_mm, it * U + u + 1)
                    if not first:
                        act.wait_ge(s_out[u], 16 * it)
                    nc.scalar.copy(rows[:, u, :], bank[3 + u][:, 0:D]).then_inc(s_row, 1)

                def one_pass(it, first, second):
                    for u in range(U):
                        copy_xT(it, u, first)
                        if u >= 2:
                            copy_rows(it, u - 2, first)
                        elif not first:
                            copy_rows(it - 1, U + u - 2, second)

                one_pass(0, True, False)
                one_pass(1, False, True)
                with act.Fori(2, IT) as it:
                    one_pass(it, False, False)
                for u in range(U - 2, U):
                    copy_rows(IT - 1, u, False)

            @block.sync
            def _(sp):
                with sp.Fori(0, IT - 1) as it:
                    for u in range(U):
                        w = it * U + u
                        sp.wait_ge(s_row, w + 1)
                        sp.dma_start(support_d[ds(w * P, P), :], rows[:, u, :]).then_inc(s_out[u], 16)
                for u in range(U):
                    w = (IT - 1) * U + u
                    n = min(P, N - w * P)
                    sp.wait_ge(s_row, w + 1)
                    sp.dma_start(support_d[w * P:w * P + n, :], rows[0:n, u, :]).then_inc(s_out[u], 16)
                for u in range(U):
                    sp.wait_ge(s_out[u], 16 * IT)
                sp.wait_ge(s_small, 128)

    def segment_sum(tag, table, index, weighted, acc, fresh, meanwhile):
        with ExitStack() as mine:
            def own(name, shape, dt=F32):
                return mine.enter_context(nc.sbuf_tensor(f"{tag}_{name}", shape, dt))

            segment_sum_program(own, tag, table, index, weighted, acc, fresh, meanwhile)

    def segment_sum_program(own, tag, table, index, weighted, acc, fresh, meanwhile):
        head = own("head", [P, RING, CH, D], F32R)
        rest = own("rest", [P, 2, CH, D], F32R)
        onehot = own("onehot", [P, 3, CH, P], F32R)
        s_idx, s_got = sem(f"{tag}_indices_ready"), [sem(f"{tag}_rows_gathered{s}") for s in range(RING)]
        s_head, s_rest = sem(f"{tag}_heads_ready"), sem(f"{tag}_rests_ready")
        s_hot = sem(f"{tag}_onehot_ready")
        s_sum, s_acc, s_used = sem(f"{tag}_summed"), sem(f"{tag}_added"), sem(f"{tag}_group_used")
        s_hot2 = sem(f"{tag}_further_onehot")
        s_sum2, s_acc2 = sem(f"{tag}_further_summed"), sem(f"{tag}_further_added")
        passes, LAP = NG // (2 * RING), 2 * RING

        def column(of, g):
            return of[:, :, ds(g, 1)].rearrange("p j a -> p (j a)")

        with nc.Block() as block:
            @block.sync
            def _(sp):
                meanwhile(sp, s_head)

            @block.scalar
            def _(act):
                def indices(g, s):
                    nc.scalar.copy(idx_slot[:, s, :], column(index, g)).then_inc(s_idx, 1)

                def group(it, s, first, last):
                    g = it * LAP + s
                    act.wait_ge(s_got[s % RING], 16 * CH * (2 * it + s // RING + 1))
                    if not first or s >= RING:
                        act.wait_ge(s_used, g - RING + 1)
                    for j in range(CH):
                        ins = nc.scalar.activation(head[:, s % RING, j, :], ring[:, s % RING, j, :], ACT.Copy,
                                                   scale=ew_f[:, j, ds(g, 1)] if weighted else 1.0)
                    ins.then_inc(s_head, 1)
                    if not (last and s > LAP - RING) and not (first and s == 0):
                        act.wait_ge(s_rest, g)
                        indices(g + RING - 1, (s + RING - 1) % RING)

                for s in range(RING):
                    indices(s, s)
                for s in range(LAP):
                    group(0, s, True, False)
                with act.Fori(1, passes - 1) as it:
                    for s in range(LAP):
                        group(it, s, False, False)
                for s in range(LAP):
                    group(passes - 1, s, False, True)

            @block.gpsimd
            def _(pool):
                with pool.Fori(0, passes) as it:
                    for s in range(LAP):
                        pool.wait_ge(s_idx, it * LAP + s + 1)
                        pool.sem_inc(s_pool_turn, 1)
                        for j in range(CH):
                            nc.gpsimd.indirect_dma_start(
                                out=ring[:, s % RING, j, :], out_offset=None, in_=table,
                                in_offset=bass.IndirectOffsetOnAxis(ap=idx_slot[:, s % RING, j:j + 1], axis=0),
                            ).then_inc(s_got[s % RING], 16)

            @block.vector
            def _(dve):
                nodes = iota_row[:, None, :].to_broadcast([P, CH, P])

                def first_onehot(g, s):
                    nc.vector.tensor_tensor(onehot[:, s % 2, :, :], dst_rel[:, :, ds(g, 1)].to_broadcast([P, CH, P]),
                                            nodes, ALU.is_equal).then_inc(s_hot, 1)

                def add(w, b):
                    return nc.vector.tensor_tensor(acc[:, ds(w, 1), :], acc[:, ds(w, 1), :],
                                                   bank[b][:, None, 0:D], ALU.add)

                def split(it, s):
                    g = it * LAP + s
                    dve.wait_ge(s_head, g + 1)
                    if weighted:
                        for j in range(CH):
                            last = nc.vector.scalar_tensor_tensor(
                                out=rest[:, s % 2, j, :], in0=ring[:, s % RING, j, :], scalar=ew_f[:, j, ds(g, 1)],
                                in1=head[:, s % RING, j, :].bitcast(F32), op0=ALU.mult, op1=ALU.subtract)
                    else:
                        last = nc.vector.tensor_tensor(rest[:, s % 2, :, :], ring[:, s % RING, :, :],
                                                       head[:, s % RING, :, :].bitcast(F32), ALU.subtract)
                    last.then_inc(s_rest, 1)

                def finish(g, b):
                    w = dve.value_load(spans[0:1, 1, ds(g, 1)], min_val=0, max_val=NT - 1)
                    further = dve.value_load(spans[0:1, 2, ds(g, 1)], min_val=0, max_val=NT - 1)
                    dve.wait_ge(s_sum, g + 1)
                    dve.wait_ge(s_acc, g + 1)
                    add(w, b).then_inc(s_acc, 1)
                    with dve.If(further > 0):
                        before_g = dve.value_load(spans[0:1, 0, ds(g, 1)], min_val=0, max_val=NG * NT)
                        with dve.Fori(0, further) as i:
                            v = nc.s_assert_within(w + i + 1, 1, NT - 1, skip_runtime_bounds_check_because=
                                                   "a group's tiles end at that of its greatest destination")
                            n = before_g + i + 1
                            nc.vector.scalar_tensor_tensor(
                                out=onehot[:, 2, :, :], in0=dst_f[:, :, ds(g, 1)].to_broadcast([P, CH, P]),
                                scalar=tile_base[:, ds(v, 1)], in1=nodes, op0=ALU.subtract, op1=ALU.is_equal)\
                                .then_inc(s_hot2, 1)
                            dve.wait_ge(s_sum2, n)
                            add(v, 2).then_inc(s_acc2, 1)
                            dve.wait_ge(s_acc2, n)
                        nc.vector.nop()
                    nc.vector.nop().then_inc(s_used, 1)

                def step(it, s, first):
                    g = it * LAP + s
                    split(it, s)
                    if not first:
                        finish(g - 1, (s - 1) % 2)
                    first_onehot(g + 1, s + 1)

                first_onehot(0, 0)
                if fresh:
                    nc.vector.memset(acc[:, :, :], 0.0).then_inc(s_acc, 1)
                else:
                    dve.sem_inc(s_acc, 1)
                for s in range(LAP):
                    step(0, s, s == 0)
                with dve.Fori(1, passes) as it:
                    for s in range(LAP):
                        step(it, s, False)
                finish(NG - 1, (NG - 1) % 2)

            @block.tensor
            def _(pe):
                def product(slot, s, b):
                    for j in range(CH):
                        for i, part in enumerate((head[:, s % RING, j, :], rest[:, s % 2, j, :])):
                            last = nc.tensor.matmul(bank[b][:, 0:D], onehot[:, slot, j, :], part,
                                                    start=(j == i == 0), stop=(j == CH - 1 and i == 1))
                    return last

                with pe.Fori(0, passes) as it:
                    for s in range(LAP):
                        g = it * LAP + s
                        further = pe.value_load(spans[0:1, 2, ds(g, 1)], min_val=0, max_val=NT - 1)
                        pe.wait_ge(s_hot, g + 1)
                        pe.wait_ge(s_rest, g + 1)
                        product(s % 2, s, s % 2).then_inc(s_sum, 1)
                        with pe.If(further > 0):
                            before_g = pe.value_load(spans[0:1, 0, ds(g, 1)], min_val=0, max_val=NG * NT)
                            with pe.Fori(0, further) as i:
                                pe.wait_ge(s_hot2, before_g + i + 1)
                                product(2, s, 2).then_inc(s_sum2, 1)
                            pe.nop()
                        pe.nop()

    def transposed_norm():
        xTh, xTl = late["xTh"], late["xTl"]
        full = shared[:, 0:U * D].rearrange("p (u k n) -> p u k n", u=U, k=KD)
        s_xn, s_T = sem("ln2_xn_ready"), sem("ln2_transposed")
        s_xT, s_xTl = sem("ln2_head_ready"), sem("ln2_rest_ready")
        with nc.Block() as block:
            @block.vector
            def _(dve):
                row_stats(dve, "ln2")

                def one_pass(it, first):
                    for u in range(U):
                        w = it * U + u
                        if not first:
                            dve.wait_ge(s_T, w - U + 1)
                        normalise(xn[:, u, :], x_all, w).then_inc(s_xn, 1)

                one_pass(0, True)
                with dve.Fori(1, IT) as it:
                    one_pass(it, False)

            @block.gpsimd
            def _(pool):
                with pool.Fori(0, IT) as it:
                    for u in range(U):
                        w = it * U + u
                        pool.wait_ge(s_xT, w + 1)
                        nc.gpsimd.tensor_tensor(xTl[:, :, ds(w * P, P)], full[:, u, :, :],
                                                xTh[:, :, ds(w * P, P)].bitcast(F32), ALU.subtract).then_inc(s_xTl, 1)

            @block.tensor
            def _(pe):
                def one_pass(it, first, last_pass):
                    for u in range(U):
                        w = it * U + u
                        pe.wait_ge(s_xn, w + 1)
                        if not first:
                            pe.wait_ge(s_xT, w - U + 1)
                        nc.tensor.matmul(bank[U][0:1, 0:D], ones[:, 0:1], xn[:, u, :], start=(first and u == 0),
                                         stop=(last_pass and u == U - 1), skip_group_check=True)
                        transposes(u).then_inc(s_T, 1)

                one_pass(0, True, False)
                with pe.Fori(1, IT - 1) as it:
                    one_pass(it, False, False)
                one_pass(IT - 1, False, True)

            @block.scalar
            def _(act):
                def one_pass(it, first):
                    for u in range(U):
                        w = it * U + u
                        act.wait_ge(s_T, w + 1)
                        if not first:
                            act.wait_ge(s_xTl, w - U + 1)
                        turned = tslot(u).rearrange("p (k n) -> p k n", k=KD)
                        nc.scalar.copy(full[:, u, :, :], turned)
                        nc.scalar.copy(xTh[:, :, ds(w * P, P)], turned).then_inc(s_xT, 1)

                one_pass(0, True)
                with act.Fori(1, IT) as it:
                    one_pass(it, False)

    idx2 = sb("idx2", [1, 2], I32)
    w_pair = sb("w_pair", [P, 2])
    w2_raw = shared[:, 2 * KD * F0:2 * KD * F0 + 2 * K0 * D].rearrange("p (e k n) -> p e k n", e=2, k=K0)
    s_w2_loaded = sem("w2_loaded")

    @scratch
    def routing(own):
        row_sum = own("rt_sum", [1, D])
        col = own("rt_col", [P, KD])
        w1_raw = shared[:, 0:2 * KD * F0].rearrange("p (e k n) -> p e k n", e=2, k=KD)
        w1_h, w1_l = late["w1_h"], late["w1_l"]
        s_sum, s_col = sem("rt_sum_copied"), sem("rt_sum_on_partitions")
        s_w1h = sem("rt_w1_heads")
        rt = own("rt_rows", [1, 10, NE])
        sc = own("rt_scalars", [1, 12])
        wd8 = own("rt_wd8", [NE, P])
        s_mean, s_lg, s_step, s_idx = sem("rt_mean"), sem("rt_logits"), sem("rt_step"), sem("rt_experts_known")
        s_exp, s_w, s_e, s_b = sem("rt_exp_asked"), sem("rt_weights"), sem("rt_exp_done"), sem("rt_broadcast")
        s_ld, s_wT, s_b2 = sem("rt_matrices_loaded"), sem("rt_weights_on_partitions"), sem("rt_b2_done")
        with nc.Block() as block:
            @block.vector
            def _(dve):
                link = Chain(dve, s_step)

                def row(i):
                    return rt[0:1, i, :]

                def s(i):
                    return sc[0:1, i:i + 1]

                nc.vector.tensor_copy(row_sum[:, :], bank[U][0:1, 0:D]).then_inc(s_sum, 1)
                dve.wait_ge(s_col, 1)
                nc.vector.tensor_copy(col[:, :], bank[4][:, 0:KD]).then_inc(s_mean, 1)
                dve.wait_ge(s_lg, 1)
                link(nc.vector.tensor_scalar(row(0), bank[0][0:1, 0:NE], 1.0 / N, None, ALU.mult))
                link(nc.vector.tensor_tensor(row(0), row(0), br_s[:, :], ALU.add))

                def softmax(n):
                    link(nc.vector.tensor_reduce(s(0), row(0), AX.X, ALU.max))
                    nc.vector.tensor_scalar(row(0), row(0), s(0), None, ALU.subtract).then_inc(s_exp, 1)
                    dve.wait_ge(s_e, n)
                    link(nc.vector.tensor_reduce(s(1), row(1), AX.X, ALU.add))
                    link(nc.vector.reciprocal(s(2), s(1)))
                    link(nc.vector.tensor_scalar(row(1), row(1), s(2), None, ALU.mult))

                softmax(1)
                link(nc.vector.tensor_scalar(row(2), row(1), float(N), CAP, ALU.mult, ALU.max))
                link(nc.vector.memset(row(3), CAP))
                link(nc.vector.reciprocal(row(2), row(2)))
                link(nc.vector.tensor_scalar(row(3), row(2), CAP, 1.0, ALU.mult, ALU.min))
                link(nc.vector.tensor_tensor(row(0), row(1), row(3), ALU.mult))
                softmax(2)

                def first_greatest(value, index, hot):
                    link(nc.vector.tensor_reduce(value, row(1), AX.X, ALU.max))
                    link(nc.vector.tensor_scalar(row(4), row(1), value, -float(NE), ALU.is_equal, ALU.mult))
                    link(nc.vector.tensor_tensor(row(4), row(4), iota_row[0:1, 0:NE], ALU.add))
                    link(nc.vector.tensor_reduce(index, row(4), AX.X, ALU.min))
                    link(nc.vector.tensor_scalar(hot, row(4), index, None, ALU.is_equal))
                    link(nc.vector.tensor_scalar(index, index, float(NE), None, ALU.add))

                first_greatest(s(4), s(6), row(5))
                link(nc.vector.scalar_tensor_tensor(out=row(1), in0=row(5), scalar=-2.0, in1=row(1),
                                                    op0=ALU.mult, op1=ALU.add))
                first_greatest(s(5), s(7), row(6))
                nc.vector.tensor_copy(idx2[:, :], sc[0:1, 6:8]).then_inc(s_idx, 1)
                nc.vector.tensor_scalar(sc[0:1, 8:10], sc[0:1, 4:6], s(4), None, ALU.subtract).then_inc(s_exp, 1)
                dve.wait_ge(s_e, 3)
                link(nc.vector.tensor_reduce(s(0), sc[0:1, 10:12], AX.X, ALU.add))
                link(nc.vector.reciprocal(s(1), s(0)))
                link(nc.vector.tensor_scalar(sc[0:1, 10:12], sc[0:1, 10:12], s(1), None, ALU.mult))
                link(nc.vector.tensor_scalar(row(5), row(5), s(10), None, ALU.mult))
                nc.vector.scalar_tensor_tensor(out=row(7), in0=row(6), scalar=s(11), in1=row(5),
                                               op0=ALU.mult, op1=ALU.add).then_inc(s_w, 1)
                dve.wait_ge(s_b, 1)
                link(nc.vector.tensor_copy(w_pair[:, :], bank[1][:, 0:2]))
                nc.vector.tensor_scalar(wd8[:, :], ones[0:NE, :], bank[2][0:NE, 0:1], None, ALU.mult).then_inc(s_wT, 1)
                dve.wait_ge(s_b2, 1)
                nc.vector.tensor_copy(late["b2c"][:, :], bank[3][:, 0:D])
                for i in range(2):
                    dve.wait_ge(s_w1h, i + 1)
                    nc.vector.tensor_tensor(w1_l[:, i, :, :], w1_raw[:, i, :, :], w1_h[:, i, :, :].bitcast(F32),
                                            ALU.subtract)

            @block.scalar
            def _(act):
                for n in range(2):
                    act.wait_ge(s_exp, n + 1)
                    nc.scalar.activation(rt[0:1, 1, :], rt[0:1, 0, :], ACT.Exp).then_inc(s_e, 1)
                act.wait_ge(s_exp, 3)
                nc.scalar.activation(sc[0:1, 10:12], sc[0:1, 8:10], ACT.Exp).then_inc(s_e, 1)
                act.wait_ge(s_ld, 64)
                for i in range(2):
                    nc.scalar.copy(w1_h[:, i, :, :], w1_raw[:, i, :, :]).then_inc(s_w1h, 1)

            @block.tensor
            def _(pe):
                pe.wait_ge(s_sum, 1)
                for k in range(KD):
                    last = nc.tensor.matmul(bank[4][:, k:k + 1], row_sum[0:1, k * P:(k + 1) * P], ones[0:1, 0:1],
                                            start=True, stop=True)
                last.then_inc(s_col, 1)
                pe.wait_ge(s_mean, 1)
                for k in range(KD):
                    last = nc.tensor.matmul(bank[0][0:1, 0:NE], col[:, k:k + 1], wr_s[:, k, :],
                                            start=(k == 0), stop=(k == KD - 1))
                last.then_inc(s_lg, 1)
                pe.wait_ge(s_w, 1)
                nc.tensor.matmul(bank[1][:, 0:2], ones[0:1, :], sc[0:1, 10:12], start=True, stop=True)
                nc.tensor.matmul(bank[2][0:NE, 0:1], rt[0:1, 7, :], ones[0:1, 0:1], start=True, stop=True)\
                    .then_inc(s_b, 1)
                pe.wait_ge(s_wT, 1)
                nc.tensor.matmul(bank[3][:, 0:D], wd8[:, :], b2_s[:, :], start=True, stop=True).then_inc(s_b2, 1)

            @block.sync
            def _(sp):
                sp.wait_ge(s_idx, 1)
                experts = [sp.value_load(idx2[0:1, i:i + 1], min_val=0, max_val=NE - 1) for i in range(2)]
                for i, e in enumerate(experts):
                    sp.dma_start(w1_raw[:, i, :, :], w1[ds(e, 1), :, :].rearrange("a (k p) n -> p (a k) n", p=P))\
                        .then_inc(s_ld, 16)
                    sp.dma_start(late["b1_s"][:, i, :], b1[ds(e, 1), :].rearrange("a (k p) -> p (a k)", p=P),
                                 allow_slow_non_contiguous=True)\
                        .then_inc(s_ld, 16)
                for i, e in enumerate(experts):
                    sp.dma_start(w2_raw[:, i, :, :], w2[ds(e, 1), :, :].rearrange("a (k p) n -> p (a k) n", p=P))\
                        .then_inc(s_w2_loaded, 16)
                sp.wait_ge(s_ld, 64)

    @scratch
    def top2_ffn(own):
        HW = U * P // 2
        mv = own("f0_mean", [P, U])
        st = own("f0_stats", [P, U, 6])
        rs, va, tmp = own("f0_rstd", [P, U]), own("f0_var", [P, U]), own("f0_tmp", [P, U])
        o = own("f0_out", [P, U, D])
        hh, hl = own("f0_hT_h", [P, 2 * K0, U * P], F32R), own("f0_hT_l", [P, 2 * K0, U * P], F32R)
        gelu = shared[:, 0:4 * HW].rearrange("p (s n) -> p s n", s=4)
        w1_h, w1_l, w2_h, w2_l, xTh, xTl = (late[n] for n in ("w1_h", "w1_l", "w2_h", "w2_l", "xTh", "xTl"))
        s_hl, s_w2 = sem("f0_hidden_rest_ready"), sem("f0_w2_step")
        s_h, s_g, s_y = sem("f0_hidden_product"), sem("f0_gelu_done"), sem("f0_output_product")
        s_o, s_r = sem("f0_chunk_step"), sem("f0_row_step")
        NH = 2 * 2 * K0
        with nc.Block() as block:
            @block.tensor
            def _(pe):
                def chunk(c, first):
                    for i in range(NH):
                        f, h = divmod(i, 2)
                        e, b = divmod(f, K0)
                        if not first or i >= 4:
                            pe.wait_ge(s_g, c * NH + i - 3)
                        cols = ds(c * (U * P) + h * HW, HW)
                        three_products(bank[i % 4][:, 0:HW], [
                            (w1_h[:, e, k, b * P:(b + 1) * P], w1_l[:, e, k, b * P:(b + 1) * P],
                             xTh[:, k, cols], xTl[:, k, cols]) for k in range(KD)]).then_inc(s_h, 1)
                    def block_ready(f):
                        pe.wait_ge(s_hl, c * NH + 2 * f + 1)

                    if first:
                        pe.wait_ge(s_w2, 3)
                    for u in range(U):
                        if u == 1:
                            pe.wait_ge(s_hl, (c + 1) * NH)
                        if not first or u == U - 1:
                            pe.wait_ge(s_r, c * U + (1 if u == U - 1 else 0))
                        y = bank[4 + u % 4][:, 0:D]
                        three_products(y, [
                            (hh[:, f, u * P:(u + 1) * P], hl[:, f, u * P:(u + 1) * P],
                             w2_h[:, f // K0, f % K0, :], w2_l[:, f // K0, f % K0, :]) for f in range(2 * K0)],
                            block_ready if u == 0 else None).then_inc(s_y, 1)

                chunk(0, True)
                with pe.Fori(1, IT) as c:
                    chunk(c, False)

            @block.scalar
            def _(act):
                def chunk(c, first):
                    for i in range(NH):
                        f, h = divmod(i, 2)
                        e, b = divmod(f, K0)
                        act.wait_ge(s_h, c * NH + i + 1)
                        if not first:
                            act.wait_ge(s_y, c * U)
                        if not first or i >= 4:
                            act.wait_ge(s_hl, c * NH + i - 3)
                        for to in (gelu[:, i % 4, :], hh[:, f, h * HW:(h + 1) * HW]):
                            last = nc.scalar.activation(to, bank[i % 4][:, 0:HW], ACT.Gelu,
                                                        bias=late["b1_s"][:, e, b:b + 1])
                        last.then_inc(s_g, 1)

                chunk(0, True)
                with act.Fori(1, IT) as c:
                    chunk(c, False)

            @block.gpsimd
            def _(pool):
                with pool.Fori(0, IT) as c:
                    for i in range(NH):
                        f, h = divmod(i, 2)
                        pool.wait_ge(s_g, c * NH + i + 1)
                        part = slice(h * HW, (h + 1) * HW)
                        nc.gpsimd.tensor_tensor(hl[:, f, part], gelu[:, i % 4, :], hh[:, f, part].bitcast(F32),
                                                ALU.subtract).then_inc(s_hl, 1)

            @block.vector
            def _(dve):
                dve.wait_ge(s_w2_loaded, 32)
                for i in range(2):
                    last = nc.vector.tensor_scalar(w2_raw[:, i, :, :], w2_raw[:, i, :, :], w_pair[:, i:i + 1], None,
                                                   ALU.mult)
                last.then_inc(s_w2, 1)
                dve.wait_ge(s_w2, 1)
                nc.vector.tensor_copy(w2_h[:, :, :, :], w2_raw).then_inc(s_w2, 1)
                dve.wait_ge(s_w2, 2)
                nc.vector.tensor_tensor(w2_l[:, :, :, :], w2_raw, w2_h[:, :, :, :].bitcast(F32), ALU.subtract)\
                    .then_inc(s_w2, 1)
                STEPS = 45
                with dve.Fori(0, IT) as c:
                    link = Chain(dve, s_o, c * STEPS)
                    for u in range(U):
                        last = normalise(xn[:, u, :], x_all, c * U + u)
                    link(last)
                    rows = x_all[:, ds(c * U, U), :]
                    nc.vector.tensor_tensor(rows, rows, beta_s[:, None, :].to_broadcast([P, U, D]), ALU.add)
                    link(nc.vector.tensor_tensor(xn[:, :, :], xn[:, :, :],
                                                 late["b2c"][:, None, :].to_broadcast([P, U, D]), ALU.add))
                    for u in range(U + 1):
                        if u < U:
                            dve.wait_ge(s_y, c * U + u + 1)
                            nc.vector.tensor_tensor(o[:, u, :], xn[:, u, :], bank[4 + u % 4][:, 0:D], ALU.add)\
                                .then_inc(s_r, 1)
                        if u > 0:
                            dve.wait_ge(s_r, c * U + u)
                            last = nc.vector.bn_stats(st[:, u - 1, :], o[:, u - 1, :])
                    link(last)
                    join_stats(link, st, mv[:, :], va[:, :], tmp[:, :])
                    rsqrt(link, rs[:, :], va[:, :], tmp[:, :])
                    for u in range(U):
                        last = nc.vector.scalar_tensor_tensor(out=o[:, u, :], in0=o[:, u, :], scalar=mv[:, u:u + 1],
                                                              in1=gamma_s[:, :], op0=ALU.subtract, op1=ALU.mult)
                    link(last)
                    for u in range(U):
                        row = x_all[:, ds(c * U + u, 1), :].rearrange("p a d -> p (a d)")
                        last = nc.vector.scalar_tensor_tensor(out=row, in0=o[:, u, :], scalar=rs[:, u:u + 1],
                                                              in1=row, op0=ALU.mult, op1=ALU.add)
                    link(last)
                    chunk_stats(dve, link, c, st, mv, rs, va, tmp)
                    assert link.steps == STEPS

    @scratch
    def relational_table(own):
        xTh, xTl = late["xTh"], late["xTl"]
        STAGES, BANKS = 5, 5
        stage = shared[:, 0:STAGES * 2 * D].rearrange("p (s n) -> p s n", s=STAGES)
        raw = own("p3_w_raw", [P, 2, KD, 2, D])
        wh, wl = own("p3_w_h", [P, 2, KD, 2 * D], F32R), own("p3_w_l", [P, 2, KD, 2 * D], F32R)
        s_raw, s_raw0 = [sem(f"p3_weights_loaded{i}") for i in range(2)], sem("p3_first_weights_loaded")
        s_xn, s_T, s_xTh, s_xT = sem("p3_xn_ready"), sem("p3_transposed"), sem("p3_xT_head"), sem("p3_xT_ready")
        s_wh, s_w, s_mm = sem("p3_weight_heads"), sem("p3_weights_ready"), sem("p3_product")
        s_copied = [sem("p3_copied_scalar"), sem("p3_copied_vector")]
        s_out = [sem(f"p3_stored{s}") for s in range(STAGES)]
        TURN = 2 * NT
        assert TURN % STAGES == 0 and TURN % BANKS == 0

        AHEAD = 2

        def turned(w):
            return bank[BANKS + w % 3][:, 0:D]

        def by_feature(ap):
            return ap.rearrange("p (k n) -> p k n", k=KD)

        def copied(it, m):
            return it * (TURN // 2) + m // 2 + 1

        def load(q, eng, s_loaded):
            for k in range(KD):
                eng.dma_start(raw[:, q % 2, k, :, :],
                              wrel[2 * q:2 * q + 2, k * P:(k + 1) * P, :].rearrange("r p d -> p r d"))\
                    .then_inc(s_loaded, 16)

        with nc.Block() as block:
            @block.sync
            def _(sp):
                load(0, sp, s_raw0)

                def one_pass(it):
                    for m in range(TURN):
                        h, w = divmod(m, NT)
                        n = P if w < NT - 1 else LAST
                        sp.wait_ge(s_copied[m % 2], copied(it, m))
                        sp.dma_start(rel_d[w * P:w * P + n, ds((it * 2 + h) * (2 * D), 2 * D)],
                                     stage[0:n, m % STAGES, :]).then_inc(s_out[m % STAGES], 16)

                with sp.Fori(0, RP // 2) as it:
                    one_pass(it)
                for s in range(STAGES):
                    sp.wait_ge(s_out[s], 16 * (RP // 2) * (TURN // STAGES))

            @block.gpsimd
            def _(pool):
                load(1, pool, s_raw[1])
                for q in range(RP):
                    i = q % 2
                    if q == 0:
                        pool.wait_ge(s_raw0, 16 * KD)
                    else:
                        pool.wait_ge(s_raw[i], 16 * KD * (q // 2 + i))
                    if q >= 2:
                        pool.wait_ge(s_mm, (q - 1) * NT)
                    if q > 0:
                        nc.gpsimd.tensor_copy(wh[:, i, :, :], raw[:, i, :, :, :].rearrange("p k r d -> p k (r d)"))\
                            .then_inc(s_wh, 1)
                    pool.wait_ge(s_wh, q + 1)
                    nc.gpsimd.tensor_tensor(wl[:, i, :, :], raw[:, i, :, :, :].rearrange("p k r d -> p k (r d)"),
                                            wh[:, i, :, :].bitcast(F32), ALU.subtract).then_inc(s_w, 1)
                    if q + 2 < RP:
                        pool.wait_ge(s_w, q + 1)
                        load(q + 2, pool, s_raw[i])

            @block.tensor
            def _(pe):
                def transpose_tile(w):
                    pe.wait_ge(s_xn, w + 1)
                    if w >= 3:
                        pe.wait_ge(s_xT, w - 2)
                    for k in range(KD):
                        last = nc.tensor.transpose(turned(w)[:, k * P:(k + 1) * P], xn[:, w % U, k * P:(k + 1) * P],
                                                   ident[:, :])
                    last.then_inc(s_T, 1)

                def one_pass(it, first):
                    for m in range(TURN):
                        h, w = divmod(m, NT)
                        if first and h == 0:
                            if w + AHEAD < NT:
                                transpose_tile(w + AHEAD)
                            pe.wait_ge(s_xT, w + 1)
                        if w == 0:
                            pe.wait_ge(s_w, it * 2 + h + 1)
                        if not first or m >= BANKS:
                            pe.wait_ge(s_copied[(m - BANKS) % 2], copied(it, m - BANKS))
                        part = slice(w * P, (w + 1) * P)
                        three_products(bank[m % BANKS][:, :], [
                            (xTh[:, k, part], xTl[:, k, part], wh[:, h, k, :], wl[:, h, k, :]) for k in range(KD)])\
                            .then_inc(s_mm, 1)

                for w in range(AHEAD):
                    transpose_tile(w)
                one_pass(0, True)
                with pe.Fori(1, RP // 2) as it:
                    one_pass(it, False)

            def copies(eng, copy, parity, prepare):
                def one_pass(it, first):
                    for m in range(TURN):
                        if first and m < NT:
                            prepare(m)
                        if m % 2 != parity:
                            continue
                        eng.wait_ge(s_mm, it * TURN + m + 1)
                        if not first or m >= STAGES:
                            eng.wait_ge(s_out[m % STAGES], 16 * (it * (TURN // STAGES) + m // STAGES))
                        copy(stage[:, m % STAGES, :], bank[m % BANKS][:, :]).then_inc(s_copied[parity], 1)

                one_pass(0, True)
                with eng.Fori(1, RP // 2) as it:
                    one_pass(it, False)

            @block.scalar
            def _(act):
                def head(w):
                    act.wait_ge(s_T, w + 1)
                    nc.scalar.copy(xTh[:, :, w * P:(w + 1) * P], by_feature(turned(w))).then_inc(s_xTh, 1)

                def prepare(w):
                    if w + AHEAD < NT:
                        head(w + AHEAD)

                for w in range(AHEAD):
                    head(w)
                act.wait_ge(s_raw0, 16 * KD)
                nc.scalar.copy(wh[:, 0, :, :], raw[:, 0, :, :, :].rearrange("p k r d -> p k (r d)")).then_inc(s_wh, 1)
                copies(act, nc.scalar.copy, 0, prepare)

            @block.vector
            def _(dve):
                def normalise_tile(w):
                    if w >= U:
                        dve.wait_ge(s_T, w - U + 1)
                    normalise(xn[:, w % U, :], x_all, w).then_inc(s_xn, 1)

                def rest(w):
                    dve.wait_ge(s_xTh, w + 1)
                    part = slice(w * P, (w + 1) * P)
                    nc.vector.tensor_tensor(xTl[:, :, part], by_feature(turned(w)), xTh[:, :, part].bitcast(F32),
                                            ALU.subtract).then_inc(s_xT, 1)

                def prepare(w):
                    if w + U < NT:
                        normalise_tile(w + U)
                    if w + AHEAD < NT:
                        rest(w + AHEAD)

                for w in range(U):
                    normalise_tile(w)
                for w in range(AHEAD):
                    rest(w)
                copies(dve, nc.vector.tensor_copy, 1, prepare)

    logit = sb("logit", [P, NT, NE])
    prob = sb("prob", [P, NT])
    pos_i = sb("pos_i", [P, NT], I32)
    expert_i = sb("expert_i", [1, ST], I32)

    @scratch
    def choose_logits(own):
        HALF = U * P // 2
        NH = K1 * 2
        LAG = 3
        TILE_AT = (6, 8, 10, 12, 14)
        TURN_AT = 5
        v1_h, v1_l = late["v1_h"], late["v1_l"]
        xTh, xTl = own("p4_xT_h", [P, KD, 2 * U * P], F32R), own("p4_xT_l", [P, KD, 2 * U * P], F32R)
        hh, hl = own("p4_h_h", [P, 4, HALF], F32R), own("p4_h_l", [P, 4, HALF], F32R)
        gelu = shared[:, KD * F1:KD * F1 + 4 * HALF].rearrange("p (s n) -> p s n", s=4)
        vgs = own("p4_vg_parts", [P, K1, 2 * NE], F32R)
        fold = own("p4_fold", [2 * NE, NE])
        lT = shared[0:2 * NE, KD * F1 + 4 * HALF:KD * F1 + 6 * HALF]
        st, mv, rs = own("p4_stats", [P, U, 6]), own("p4_mean", [P, U]), own("p4_rstd", [P, U])
        va, tmp = own("p4_var", [P, U]), own("p4_tmp", [P, U])
        s_step, s_xn, s_T = sem("p4_step"), sem("p4_xn_ready"), sem("p4_transposed")
        s_xTh, s_xT, s_wh, s_w = sem("p4_xT_head"), sem("p4_xT_ready"), sem("p4_weight_heads"), sem("p4_weights_ready")
        s_vg = sem("p4_vg_ready")
        s_h, s_g, s_hl = sem("p4_hidden_product"), sem("p4_gelu_done"), sem("p4_hidden_split")
        s_lg, s_lT = sem("p4_logit_product"), sem("p4_logitsT_copied")
        s_l, s_c = sem("p4_logits"), sem("p4_logits_added")

        def turned(u, first):
            return bank[u if first and u < 4 else 6][:, 0:D]

        def by_feature(ap):
            return ap.rearrange("p (k n) -> p k n", k=KD)

        def columns(c, first, n):
            return ds((c % 2) * (U * P) + first, n)

        with nc.Block() as block:
            @block.sync
            def _(sp):
                sp.dma_start(late["v1_raw"], v1.rearrange("(k p) n -> p k n", p=P)).then_inc(s_v1, 16)

            @block.gpsimd
            def _(pool):
                pool.wait_ge(s_wh, 1)
                nc.gpsimd.tensor_tensor(v1_l[:, :, :], late["v1_raw"], v1_h[:, :, :].bitcast(F32),
                                        ALU.subtract).then_inc(s_w, 1)
                with pool.Fori(0, IT) as c:
                    for i in range(NH):
                        pool.wait_ge(s_g, c * NH + i + 1)
                        nc.gpsimd.tensor_tensor(hl[:, i % 4, :], gelu[:, i % 4, :], hh[:, i % 4, :].bitcast(F32),
                                                ALU.subtract).then_inc(s_hl, 1)

            @block.tensor
            def _(pe):
                def transpose_tile(c, u, first):
                    w = c * U + u
                    pe.wait_ge(s_xn, w + 1)
                    if not first:
                        pe.wait_ge(s_xT, w)
                    for k in range(KD):
                        last = nc.tensor.transpose(turned(u, first)[:, k * P:(k + 1) * P], xn[:, u, k * P:(k + 1) * P],
                                                   ident[:, :])
                    last.then_inc(s_T, 1)

                def hidden(c, i, first):
                    f, h = divmod(i, 2)
                    if i < 2:
                        pe.wait_ge(s_xT, c * U + (3 if h == 0 else U))
                    if not first or i >= 4:
                        pe.wait_ge(s_g, c * NH + i - 3)
                    block, cols = slice(f * P, (f + 1) * P), columns(c, h * HALF, HALF)
                    three_products(bank[i % 4][:, 0:HALF], [
                        (v1_h[:, k, block], v1_l[:, k, block], xTh[:, k, cols], xTl[:, k, cols])
                        for k in range(KD)]).then_inc(s_h, 1)

                def logits(c, i, first):
                    f, h = divmod(i, 2)
                    pe.wait_ge(s_hl, c * NH + i + 1)
                    if f == 0 and not first:
                        pe.wait_ge(s_lT, (c - 1) * 2 + h + 1)
                    to = bank[4 + h][0:2 * NE, 0:HALF]
                    nc.tensor.matmul(to, vgs[:, f, :], hh[:, i % 4, :], start=(f == 0), stop=False)
                    nc.tensor.matmul(to, vgs[:, f, :], hl[:, i % 4, :], start=False, stop=(f == K1 - 1))\
                        .then_inc(s_lg, 1)

                def turn_logits(c):
                    pe.wait_ge(s_lT, (c + 1) * 2)
                    pe.wait_ge(s_c, c + 1)
                    for u in range(U):
                        last = nc.tensor.matmul(bank[7][:, u * NE:(u + 1) * NE], lT[:, u * P:(u + 1) * P], fold[:, :],
                                                start=True, stop=True)
                    last.then_inc(s_l, 1)

                def chunk(c, first, last_chunk):
                    for i in range(NH):
                        hidden(c, i, first)
                        if i >= LAG:
                            logits(c, i - LAG, first)
                        elif not first:
                            logits(c - 1, NH + i - LAG, False)
                        if i == TURN_AT and not first:
                            turn_logits(c - 1)
                        if i in TILE_AT and not last_chunk:
                            transpose_tile(c + 1, TILE_AT.index(i), False)

                for u in range(U):
                    transpose_tile(0, u, True)
                pe.wait_ge(s_w, 1)
                pe.wait_ge(s_vg, 3)
                chunk(0, True, False)
                with pe.Fori(1, IT - 1) as c:
                    chunk(c, False, False)
                chunk(IT - 1, False, True)
                for i in range(NH - LAG, NH):
                    logits(IT - 1, i, False)
                turn_logits(IT - 1)

            @block.scalar
            def _(act):
                def head_of_tile(c, u, first=False):
                    w = c * U + u
                    act.wait_ge(s_T, w + 1)
                    nc.scalar.copy(xTh[:, :, columns(c, u * P, P)], by_feature(turned(u, first))).then_inc(s_xTh, 1)

                def copy_logits(c, h, first):
                    act.wait_ge(s_lg, c * NH + NH - 1 + h)
                    if not first:
                        act.wait_ge(s_l, c)
                    nc.scalar.copy(lT[:, h * HALF:(h + 1) * HALF], bank[4 + h][0:2 * NE, 0:HALF]).then_inc(s_lT, 1)

                def chunk(c, first, second, last_chunk):
                    for i in range(NH):
                        act.wait_ge(s_h, c * NH + i + 1)
                        if not first or i >= 4:
                            act.wait_ge(s_hl, c * NH + i - 3)
                            act.wait_ge(s_lg, c * NH + i - 3)
                        for to in (gelu[:, i % 4, :], hh[:, i % 4, :]):
                            last = nc.scalar.activation(to, bank[i % 4][:, 0:HALF], ACT.Gelu,
                                                        bias=c1_s[:, i // 2:i // 2 + 1])
                        last.then_inc(s_g, 1)
                        if i in (LAG - 1, LAG) and not first:
                            copy_logits(c - 1, i - LAG + 1, second)
                        if i in TILE_AT and not last_chunk:
                            head_of_tile(c + 1, TILE_AT.index(i))

                act.wait_ge(s_v1, 16)
                nc.scalar.copy(v1_h[:, :, :], late["v1_raw"]).then_inc(s_wh, 1)
                for u in range(U):
                    head_of_tile(0, u, True)
                chunk(0, True, False, False)
                chunk(1, False, True, False)
                with act.Fori(2, IT - 1) as c:
                    chunk(c, False, False, False)
                chunk(IT - 1, False, False, True)
                for h in range(2):
                    copy_logits(IT - 1, h, False)

            @block.vector
            def _(dve):
                nc.vector.tensor_copy(vgs[:, :, 0:NE], vg_s[:, :, :]).then_inc(s_vg, 1)
                dve.wait_ge(s_vg, 1)
                nc.vector.tensor_tensor(vgs[:, :, NE:2 * NE], vg_s[:, :, :], vgs[:, :, 0:NE].bitcast(F32),
                                        ALU.subtract).then_inc(s_vg, 1)
                nc.vector.tensor_tensor(fold[:, :], ident[0:2 * NE, 0:NE], ident[0:2 * NE, NE:2 * NE], ALU.add)\
                    .then_inc(s_vg, 1)
                STEPS = 22

                def normalise_chunk(c, first):
                    link = Chain(dve, s_step, c * STEPS)
                    rows = x_all[:, ds(c * U, U), :]
                    link(nc.vector.scalar_tensor_tensor(out=rows, in0=late["agg"][:, ds(c * U, U), :], scalar=0.0,
                                                        in1=rows, op0=ALU.max, op1=ALU.add))
                    chunk_stats(dve, link, c, st, mv, rs, va, tmp)
                    assert link.steps == STEPS
                    for u in range(U):
                        if not first:
                            dve.wait_ge(s_T, (c - 1) * U + u + 1)
                        nc.vector.tensor_scalar(xn[:, u, :], x_all[:, ds(c * U + u, 1), :]
                                                .rearrange("p a d -> p (a d)"), mv[:, u:u + 1], rs[:, u:u + 1],
                                                ALU.subtract, ALU.mult).then_inc(s_xn, 1)

                def rest_of_tiles(c, first=False):
                    for u in range(U):
                        w = c * U + u
                        dve.wait_ge(s_xTh, w + 1)
                        cols = columns(c, u * P, P)
                        nc.vector.tensor_tensor(xTl[:, :, cols], by_feature(turned(u, first)),
                                                xTh[:, :, cols].bitcast(F32),
                                                ALU.subtract).then_inc(s_xT, 1)

                def add_logits(c):
                    dve.wait_ge(s_l, c + 1)
                    nc.vector.tensor_tensor(logit[:, ds(c * U, U), :],
                                            bank[7][:, 0:U * NE].rearrange("p (u e) -> p u e", u=U),
                                            cg_s[:, None, :].to_broadcast([P, U, NE]), ALU.add).then_inc(s_c, 1)

                dve.sem_inc(s_c, 1)
                normalise_chunk(0, True)
                rest_of_tiles(0, True)
                normalise_chunk(1, False)
                rest_of_tiles(1)
                with dve.Fori(2, IT) as c:
                    normalise_chunk(c, False)
                    add_logits(c - 2)
                    rest_of_tiles(c)
                add_logits(IT - 2)
                add_logits(IT - 1)

    @scratch
    def dispatch(own):
        sel = own("ds_sel", [P, NT, NE])
        work = own("ds_work", [P, NT, NE])
        run = [own(f"ds_run{i}", [P, NT, NE]) for i in range(2)]
        tot = own("ds_tot", [P, NT, NE])
        vec = own("ds_vec", [P, NT])
        cnt = own("ds_cnt", [P, NE, NT])
        nt = [own(f"ds_nt{i}", [P, NE]) for i in range(2)]
        base = own("ds_base", [P, NE])
        past = own("ds_past", [1, ST, NE])
        ex = own("ds_ex", [1, ST])
        s_step, s_max, s_exp = sem("ds_step"), sem("ds_exp_asked"), sem("ds_exp_done")
        s_sel, s_cum, s_pos = sem("ds_choice_ready"), sem("ds_counts"), sem("ds_rows_known")
        s_xn, s_put = sem("ds_xn_ready"), [sem(f"ds_scattered{u}") for u in range(U)]
        rows = own("ds_rows", [P, U, D + 1])
        token = own("ds_token", [P, NT])
        ALLE = [P, NT, NE]
        with nc.Block() as block:
            @block.vector
            def _(dve):
                link = Chain(dve, s_step)
                link(nc.vector.tensor_reduce(vec[:, :], logit[:, :, :], AX.X, ALU.max))
                nc.vector.tensor_tensor(work[:, :, :], logit[:, :, :], vec[:, :, None].to_broadcast(ALLE),
                                        ALU.subtract).then_inc(s_max, 1)
                dve.wait_ge(s_exp, 1)
                link(nc.vector.tensor_reduce(vec[:, :], sel[:, :, :], AX.X, ALU.add))
                link(nc.vector.reciprocal(vec[:, :], vec[:, :]))
                link(nc.vector.tensor_tensor(work[:, :, :], sel[:, :, :], vec[:, :, None].to_broadcast(ALLE), ALU.mult))
                link(nc.vector.tensor_reduce(prob[:, :], work[:, :, :], AX.X, ALU.max))
                link(nc.vector.tensor_tensor(work[:, :, :], work[:, :, :], prob[:, :, None].to_broadcast(ALLE),
                                             ALU.is_equal))
                link(nc.vector.scalar_tensor_tensor(
                    out=work[:, :, :], in0=work[:, :, :], scalar=-float(NE),
                    in1=iota_row[:, None, 0:NE].to_broadcast(ALLE), op0=ALU.mult, op1=ALU.add))
                link(nc.vector.tensor_reduce(vec[:, :], work[:, :, :], AX.X, ALU.min))
                link(nc.vector.tensor_tensor(sel[:, :, :], work[:, :, :], vec[:, :, None].to_broadcast(ALLE),
                                             ALU.is_equal))
                nc.vector.tensor_scalar(sel[:, NT - 1, :], sel[:, NT - 1, :], valid[:, NT - 1:NT], None, ALU.mult)\
                    .then_inc(s_sel, 1)
                dve.wait_ge(s_cum, 1)
                link(nc.vector.tensor_copy(tot[:, :, :].rearrange("p t e -> p (t e)"), bank[1][:, 0:NT * NE]))
                link(nc.vector.tensor_copy(run[0][:, :, :], tot[:, :, :]))
                a, step = 0, 1
                while step < NT:
                    link(nc.vector.tensor_copy(run[1 - a][:, 0:step, :], run[a][:, 0:step, :]))
                    link(nc.vector.tensor_tensor(run[1 - a][:, step:NT, :], run[a][:, step:NT, :],
                                                 run[a][:, 0:NT - step, :], ALU.add))
                    a, step = 1 - a, step * 2
                inc = run[a]
                link(nc.vector.tensor_tensor(cnt[:, :, :], inc[:, NT - 1, :, None].to_broadcast([P, NE, NT]),
                                             tile_base[:, None, :].to_broadcast([P, NE, NT]), ALU.is_gt))
                link(nc.vector.tensor_reduce(base[:, :], cnt[:, :, :], AX.X, ALU.add))
                link(nc.vector.tensor_copy(nt[0][:, :], base[:, :]))
                b, step = 0, 1
                while step < NE:
                    link(nc.vector.tensor_copy(nt[1 - b][:, 0:step], nt[b][:, 0:step]))
                    link(nc.vector.tensor_tensor(nt[1 - b][:, step:NE], nt[b][:, step:NE], nt[b][:, 0:NE - step],
                                                 ALU.add))
                    b, step = 1 - b, step * 2
                upto = nt[b]
                link(nc.vector.tensor_tensor(base[:, :], upto[:, :], base[:, :], ALU.subtract))
                link(nc.vector.tensor_scalar(base[:, :], base[:, :], float(P), None, ALU.mult))
                link(nc.vector.tensor_tensor(work[:, :, :], inc[:, :, :], tot[:, :, :], ALU.subtract))
                link(nc.vector.tensor_tensor(work[:, :, :], work[:, :, :],
                                             bank[0][:, 0:NT * NE].rearrange("p (t e) -> p t e", t=NT), ALU.add))
                link(nc.vector.tensor_tensor(work[:, :, :], work[:, :, :], base[:, None, :].to_broadcast(ALLE),
                                             ALU.add))
                link(nc.vector.tensor_tensor(work[:, :, :], work[:, :, :], sel[:, :, :], ALU.mult))
                link(nc.vector.tensor_reduce(vec[:, :], work[:, :, :], AX.X, ALU.add))
                nc.vector.tensor_copy(pos_i[:, :], vec[:, :]).then_inc(s_pos, 1)
                link(nc.vector.tensor_scalar(token[:, :], tile_base[:, :], number[:, :], None, ALU.add))
                link(nc.vector.tensor_tensor(past[:, :, :], iota_row[0:1, 0:ST, None].to_broadcast([1, ST, NE]),
                                             upto[0:1, None, :].to_broadcast([1, ST, NE]), ALU.is_ge))
                link(nc.vector.tensor_reduce(ex[:, :], past[:, :, :], AX.X, ALU.add))
                nc.vector.tensor_scalar(expert_i[:, :], ex[:, :], NE - 1.0, None, ALU.min)
                for w in range(NT):
                    u = w % U
                    if w >= U:
                        dve.wait_ge(s_put[u], 16 * (w // U))
                    nc.vector.tensor_copy(rows[:, u, D:D + 1], token[:, w:w + 1])
                    nc.vector.tensor_scalar(rows[:, u, 0:D], x_all[:, w, :], mean[:, w:w + 1], rstd[:, w:w + 1],
                                            ALU.subtract, ALU.mult).then_inc(s_xn, 1)

            @block.scalar
            def _(act):
                act.wait_ge(s_max, 1)
                nc.scalar.activation(sel[:, :, :], work[:, :, :], ACT.Exp).then_inc(s_exp, 1)

            @block.tensor
            def _(pe):
                pe.wait_ge(s_sel, 1)
                rows = sel[:, :, :].rearrange("p t e -> p (t e)")
                nc.tensor.matmul(bank[0][:, 0:NT * NE], before[:, :], rows, start=True, stop=True)
                nc.tensor.matmul(bank[1][:, 0:NT * NE], ones[:, :], rows, start=True, stop=True).then_inc(s_cum, 1)

            @block.gpsimd
            def _(pool):
                pool.wait_ge(s_pos, 1)
                for w in range(NT):
                    n = P if w < NT - 1 else LAST
                    pool.wait_ge(s_xn, w + 1)
                    nc.gpsimd.indirect_dma_start(
                        out=sorted_d, out_offset=bass.IndirectOffsetOnAxis(ap=pos_i[0:n, w:w + 1], axis=0),
                        in_=rows[0:n, w % U, :], in_offset=None).then_inc(s_put[w % U], 16)
                for u in range(U):
                    pool.wait_ge(s_put[u], 16 * IT)

    @scratch
    def sorted_experts(own):
        W = SC * P
        CN = ST // SC
        xs = own("se_rows", [P, 2, SC, D + 1])
        token = own("se_token", [P, 2, SC], I32)
        xTh, xTl = own("se_xT_h", [P, 2, KD, W], F32R), own("se_xT_l", [P, 2, KD, W], F32R)
        yo = own("se_out", [P, SC, D])
        bd_s = own("se_bd", [P, NE, D])
        v1_h, v1_l, wd_s = late["v1_h"], late["v1_l"], late["wd_s"]
        s_in, s_T = [sem(f"se_rows_loaded{i}") for i in range(2)], sem("se_transposed")
        s_xTh, s_xT = sem("se_xT_head_ready"), sem("se_xT_ready")
        s_h, s_g, s_y = sem("se_hidden_product"), sem("se_gelu_done"), sem("se_output_product")
        s_r, s_st = sem("se_rows_ready"), [sem(f"se_scattered{u}") for u in range(SC)]
        s_tok = sem("se_tokens_ready")
        rows_in = sorted_d.rearrange("(c u p) d -> c p u d", p=P, u=SC)
        with nc.Block() as block:
            @block.sync
            def _(sp):
                for i in range(2):
                    sp.dma_start(xs[:, i, :, :], rows_in[i]).then_inc(s_in[i], 16)
                sp.dma_start(bd_s[:, :, :], bd.partition_broadcast(P)).then_inc(s_bd, 16)
                with sp.Fori(1, CN // 2) as it:
                    for i in range(2):
                        c = it * 2 + i
                        sp.wait_ge(s_T, (c - 1) * SC)
                        sp.wait_ge(s_tok, c - 1)
                        sp.dma_start(xs[:, i, :, :], rows_in[ds(c, 1)].rearrange("a p u d -> p (a u) d"))\
                            .then_inc(s_in[i], 16)

            @block.tensor
            def _(pe):
                def transpose_tile(c, u, turn, i, first):
                    if u == 0:
                        pe.wait_ge(s_in[i], 16 * (turn + 1))
                    if not first or u >= 2:
                        pe.wait_ge(s_xT, c * SC + u - 1)
                    for k in range(KD):
                        last = nc.tensor.transpose(bank[6 + u % 2][:, k * P:(k + 1) * P],
                                                   xs[:, i, u, k * P:(k + 1) * P], ident[:, :])
                    last.then_inc(s_T, 1)

                def hidden(c, i, first, turn=None):
                    pe.wait_ge(s_xT, (c + 1) * SC)
                    for f in range(K1):
                        if not first or f >= 4:
                            pe.wait_ge(s_g, c * K1 + f - 3)
                        block = slice(f * P, (f + 1) * P)
                        three_products(bank[f % 4][:, 0:W], [
                            (v1_h[:, k, block], v1_l[:, k, block], xTh[:, i, k, :], xTl[:, i, k, :])
                            for k in range(KD)]).then_inc(s_h, 1)
                        if turn is not None and f % 2 == 0:
                            transpose_tile(c + 1, f // 2, turn, 1 - i, False)

                def outputs(c, first):
                    for u in range(SC):
                        e = pe.value_load(expert_i[0:1, ds(c * SC + u, 1)], min_val=0, max_val=NE - 1)
                        if not first or u >= 2:
                            pe.wait_ge(s_r, c * SC + u - 1)
                        y = bank[4 + u % 2][:, 0:D]
                        for f in range(K1):
                            if u == 0:
                                pe.wait_ge(s_g, c * K1 + f + 1)
                            last = nc.tensor.matmul(y, hT[:, f, u * P:(u + 1) * P],
                                                    wd_s[:, ds(e * (K1 * D) + f * D, D)],
                                                    start=(f == 0), stop=(f == K1 - 1))
                        last.then_inc(s_y, 1)

                pe.wait_ge(s_wd, 16 * NE)
                for u in range(SC):
                    transpose_tile(0, u, 0, 0, True)
                hidden(0, 0, True, 0)
                outputs(0, True)
                with pe.Fori(1, CN // 2) as it:
                    hidden(it * 2 - 1, 1, False, it)
                    outputs(it * 2 - 1, False)
                    hidden(it * 2, 0, False, it)
                    outputs(it * 2, False)
                hidden(CN - 1, 1, False)
                outputs(CN - 1, False)

            @block.scalar
            def _(act):
                def chunk(c, first):
                    for f in range(K1):
                        act.wait_ge(s_h, c * K1 + f + 1)
                        if not first:
                            act.wait_ge(s_y, c * SC)
                        nc.scalar.activation(hT[:, f, 0:W], bank[f % 4][:, 0:W], ACT.Gelu,
                                             bias=c1_s[:, f:f + 1]).then_inc(s_g, 1)

                chunk(0, True)
                with act.Fori(1, CN) as c:
                    chunk(c, False)

            @block.vector
            def _(dve):
                def split(c, i, first, second=False):
                    if not (first or second):
                        for u in range(SC):
                            dve.wait_ge(s_st[u], 16 * (c - 1))
                    for u in range(SC):
                        dve.wait_ge(s_T, c * SC + u + 1)
                        if u == 0:
                            nc.vector.tensor_copy(token[:, i, :], xs[:, i, :, D]).then_inc(s_tok, 1)
                        if not first:
                            dve.wait_ge(s_h, (c - 1) * K1)
                        rows = bank[6 + u % 2][:, 0:D].rearrange("p (k n) -> p k n", k=KD)
                        part = slice(u * P, (u + 1) * P)
                        nc.vector.tensor_copy(xTh[:, i, :, part], rows).then_inc(s_xTh, 1)
                        dve.wait_ge(s_xTh, c * SC + u + 1)
                        nc.vector.tensor_tensor(xTl[:, i, :, part], rows, xTh[:, i, :, part].bitcast(F32),
                                                ALU.subtract).then_inc(s_xT, 1)

                def finish(c, first):
                    for u in range(SC):
                        e = dve.value_load(expert_i[0:1, ds(c * SC + u, 1)], min_val=0, max_val=NE - 1)
                        dve.wait_ge(s_y, c * SC + u + 1)
                        if not first:
                            dve.wait_ge(s_st[u], 16 * c)
                        nc.vector.tensor_tensor(yo[:, u, :], bd_s[:, ds(e, 1), :].rearrange("p a d -> p (a d)"),
                                                bank[4 + u % 2][:, 0:D], ALU.add).then_inc(s_r, 1)

                split(0, 0, True)
                split(1, 1, True)
                dve.wait_ge(s_bd, 16)
                finish(0, True)
                with dve.Fori(1, CN // 2) as it:
                    split(it * 2, 0, False)
                    finish(it * 2 - 1, False)
                    split(it * 2 + 1, 1, False)
                    finish(it * 2, False)
                finish(CN - 1, False)

            @block.gpsimd
            def _(pool):
                with pool.Fori(0, CN // 2) as it:
                    for i in range(2):
                        c = it * 2 + i
                        pool.wait_ge(s_tok, c + 1)
                        for u in range(SC):
                            pool.wait_ge(s_r, c * SC + u + 1)
                            pool.sem_inc(s_pool_turn, 1)
                            nc.gpsimd.indirect_dma_start(
                                out=y_d, out_offset=bass.IndirectOffsetOnAxis(ap=token[:, i, u:u + 1], axis=0),
                                in_=yo[:, u, :], in_offset=None).then_inc(s_st[u], 16)
                for u in range(SC):
                    pool.wait_ge(s_st[u], 16 * CN)

    @scratch
    def combine(own):
        y = own("cb_rows", [P, NT, D])
        s_in, s_add, s_out = [sem(f"cb_rows_loaded{c}") for c in range(IT)], sem("cb_added"), sem("cb_stored")
        with nc.Block() as block:
            @block.scalar
            def _(act):
                for c in range(IT):
                    full = U if c < IT - 1 else U - 1
                    act.dma_start(y[:, c * U:c * U + full, :], y_d[c * U * P:(c * U + full) * P, :]
                                  .rearrange("(t p) d -> p t d", p=P)).then_inc(s_in[c], 16)
                act.dma_start(y[0:LAST, NT - 1, :], y_d[(NT - 1) * P:N, :]).then_inc(s_in[IT - 1], 16)

            @block.vector
            def _(dve):
                for w in range(NT):
                    c = w // U
                    n = P if w < NT - 1 else LAST
                    if w % U == 0:
                        dve.wait_ge(s_in[c], 16 if c < IT - 1 else 32)
                    nc.vector.scalar_tensor_tensor(
                        out=x_all[0:n, w, :], in0=y[0:n, w, :], scalar=prob[0:n, w:w + 1],
                        in1=x_all[0:n, w, :], op0=ALU.mult, op1=ALU.add).then_inc(s_add, 1)

            @block.sync
            def _(sp):
                for c in range(IT):
                    sp.wait_ge(s_add, (c + 1) * U)
                    if c < IT - 1:
                        sp.dma_start(out[c * U * P:(c + 1) * U * P, :].rearrange("(t p) d -> p t d", p=P),
                                     x_all[:, c * U:(c + 1) * U, :]).then_inc(s_out, 16)
                sp.dma_start(out[c * U * P:(NT - 1) * P, :].rearrange("(t p) d -> p t d", p=P),
                             x_all[:, c * U:NT - 1, :]).then_inc(s_out, 16)
                sp.dma_start(out[(NT - 1) * P:N, :], x_all[0:LAST, NT - 1, :]).then_inc(s_out, 16)
                sp.wait_ge(s_out, 16 * (IT + 1))

    def empty_sorted(sp, s_head):
        parts, n = 8, ST * (D + 1) // 8
        for i in range(parts):
            sp.wait_ge(s_head, 8 * (i + 1))
            sp.dma_start(sorted_d.rearrange("(p r) d -> p (r d)", p=P)[:, i * n:(i + 1) * n],
                         late["zeros"][:, i * n:(i + 1) * n]).then_inc(s_empty, 16)
        sp.wait_ge(s_empty, 16 * parts)

    live, count = [], [0]

    def allocate(*buffers):
        def run():
            live.append(ExitStack())
            for name, shape, dt in buffers:
                count[0] += 1
                late[name] = live[-1].enter_context(nc.sbuf_tensor(f"{name}_{count[0]}", shape, dt))
        return run

    def release():
        live.pop().close()

    def load_expert_weights(sp, s_head):
        for e in range(NE):
            sp.wait_ge(s_head, 8 * (e + 1))
            sp.dma_start(late["wd_s"][:, e * K1 * D:(e + 1) * K1 * D].rearrange("p (k d) -> p k d", k=K1),
                         wd[e, :, :].rearrange("(k p) d -> p k d", p=P)).then_inc(s_wd, 16)

    late["v1_raw"] = shared[:, 0:KD * F1].rearrange("p (k n) -> p k n", k=KD)
    transposed = (("xTh", [P, KD, NP], F32R), ("xTl", [P, KD, NP], F32R))
    parts = [
        allocate(("zeros", [P, ST * (D + 1)], F32)),
        load_and_edges, support,
        lambda: segment_sum("sum1", support_d, src_i, False, x_all, False, empty_sorted),
        release,
        allocate(*transposed),
        transposed_norm,
        allocate(("w1_h", [P, 2, KD, F0], F32R), ("w1_l", [P, 2, KD, F0], F32R), ("w2_h", [P, 2, K0, D], F32R),
                 ("w2_l", [P, 2, K0, D], F32R), ("b1_s", [P, 2, K0], F32), ("b2c", [P, D], F32)),
        routing, top2_ffn,
        release,
        relational_table,
        release,
        allocate(("wd_s", [P, NE * K1 * D], F32), ("v1_h", [P, KD, F1], F32R), ("v1_l", [P, KD, F1], F32R)),
        allocate(("agg", [P, NT, D], F32)),
        lambda: segment_sum("sum3", rel_rows, srcrel_i, True, late["agg"], True, load_expert_weights),
        choose_logits,
        release,
        dispatch, sorted_experts,
        release,
        combine,
    ]
    with ctx:
        for part in parts:
            part()


INS = ["x", "src", "dst", "edge_type_20", "edge_weight1", "L0_gnn_weight", "L0_gnn_bias", "L0_ffn_Wr", "L0_ffn_br",
       "L0_ffn_W1", "L0_ffn_b1", "L0_ffn_W2", "L0_ffn_b2", "L0_ffn_gamma", "L0_ffn_beta", "L1_gnn_weight",
       "L1_ffn_W1", "L1_ffn_b1", "L1_ffn_Wg", "L1_ffn_bg", "L1_ffn_Wd", "L1_ffn_bd"]


def kernel(**inputs):
    import numpy as np
    import concourse.bacc as bacc
    from concourse.bass_utils import run_bass_kernel_spmd

    nc = bacc.Bacc("TRN2", target_bir_lowering=False, num_devices=1)
    arrays, args = {}, []
    for name in INS:
        a = np.ascontiguousarray(inputs[name])
        arrays[f"in_{name}"] = a
        args.append(nc.dram_tensor(f"in_{name}", a.shape, mybir.dt.from_np(a.dtype), kind="ExternalInput").ap())
    out = nc.dram_tensor("out", (N, D), F32, kind="ExternalOutput").ap()
    build(nc, *args, out)
    r = run_bass_kernel_spmd(nc, [arrays], core_ids=[0])
    return r.results[0]["out"]
```
